# Optimizing a Trainium2 kernel written in Bass

```python
import numpy as np
import jax
import jax.numpy as jnp

def _softmax(x, axis=-1):
    return jax.nn.softmax(x, axis=axis)

def _gelu(x):
    return jax.nn.gelu(x, approximate=True)

def _silu(x):
    return jax.nn.silu(x)

def _sigmoid(x):
    return jax.nn.sigmoid(x)

def _layernorm(x, axis=-1, eps=1e-05):
    m = jnp.mean(x, axis=axis, keepdims=True)
    v = jnp.var(x, axis=axis, keepdims=True)
    return (x - m) / jnp.sqrt(v + eps)

def _scatter_add(tgt, idx, src, axis=0):
    return tgt.at[idx].add(src)

def _segment_sum(src, seg, n):
    return jax.ops.segment_sum(src, seg, n)
kernel_name = 'mk_prb_d2_jaxref_r8_696e69'

def setup_inputs(seed: int=0):
    np.random.seed(seed)
    _w = jnp.asarray

    def _L0_attn_setup():
        import jax, jax.numpy as jnp
        from jax import lax
        import numpy as np

        def _causal_dwconv(x, w, b):
            k = w.shape[-1]
            y = lax.conv_general_dilated(x, w, (1,), [(k - 1, 0)], feature_group_count=w.shape[0], dimension_numbers=('NCH', 'OIH', 'NCH'))
            return y + b[None, :, None]

        def _mamba_branch(xz, conv_w, conv_b, xproj_w, dtproj_w, dt_bias, A_log, Dp):
            x, z = jnp.split(xz, 2, axis=1)
            x = jax.nn.silu(_causal_dwconv(x, conv_w, conv_b))
            r = dtproj_w.shape[1]
            n = A_log.shape[1]
            x_dbl = jnp.einsum('bdl,ed->bel', x, xproj_w)
            dt, Bm, Cm = (x_dbl[:, :r], x_dbl[:, r:r + n], x_dbl[:, r + n:])
            delta = jax.nn.softplus(jnp.einsum('brl,dr->bdl', dt, dtproj_w) + dt_bias[None, :, None])
            A = -jnp.exp(A_log)
            dA = jnp.exp(jnp.einsum('bdl,dn->lbdn', delta, A))
            dBu = jnp.einsum('bdl,bnl,bdl->lbdn', delta, Bm, x)

            def step(h, ab):
                h = ab[0] * h + ab[1]
                return (h, h)
            _, hs = lax.scan(step, jnp.zeros_like(dA[0]), (dA, dBu))
            y = jnp.einsum('lbdn,bnl->bdl', hs, Cm) + Dp[None, :, None] * x
            return y * jax.nn.silu(z)
        key = jax.random.key(seed)
        ks = jax.random.split(key, 20)
        B, L, DM = (2, 128, 128)
        DI, DS, DR, K = (256, 16, 64, 4)
        f = lambda i, shape, s=1.0: jax.random.normal(ks[i], shape, jnp.float32) * s
        return {'hidden_states': f(0, (B, L, DM)), 'in_proj_w': f(1, (2 * DI, DM), 0.02), 'conv1d_w': f(2, (DI, 1, K), 0.2), 'conv1d_bias': f(3, (DI,), 0.1), 'x_proj_w': f(4, (DR + 2 * DS, DI), 0.02), 'dt_proj_w': f(5, (DI, DR), 0.05), 'dt_proj_b': f(6, (DI,), 0.1), 'A_log': f(7, (DI, DS), 0.5), 'D': f(8, (DI,), 1.0), 'conv1db_w': f(9, (DI, 1, K), 0.2), 'conv1db_bias': f(10, (DI,), 0.1), 'x_projb_w': f(11, (DR + 2 * DS, DI), 0.02), 'dt_projb_w': f(12, (DI, DR), 0.05), 'dt_projb_b': f(13, (DI,), 0.1), 'A_b_log': f(14, (DI, DS), 0.5), 'D_b': f(15, (DI,), 1.0), 'out_proj_w': f(16, (DM, DI), 0.02), 'fft_conv_w': f(17, (2 * DI, 2 * DI, 5), 0.01), 'fft_conv_b': f(18, (2 * DI,), 0.1)}
    _L0_attn_in = _L0_attn_setup()

    def _L0_ffn_setup():
        import math
        import jax, jax.numpy as jnp
        import numpy as np
        E = 8
        TOPK = 2
        CF = 1.25
        EPS = 1e-05
        NEG = -1e+30

        def _layer_norm(x, gamma, beta):
            mu = jnp.mean(x, axis=-1, keepdims=True)
            var = jnp.mean((x - mu) ** 2, axis=-1, keepdims=True)
            return (x - mu) * jax.lax.rsqrt(var + EPS) * gamma + beta
        key = jax.random.key(seed)
        ks = jax.random.split(key, 8)
        B, S, H, F = (4, 256, 128, 512)
        hidden_states = jax.random.normal(ks[0], (B, S, H), jnp.float32)
        token_mask = jnp.ones((B, S), jnp.int32)
        Wr = jax.random.normal(ks[1], (H, E), jnp.float32) * 0.001
        br = jnp.zeros((E,), jnp.float32)
        W1 = jax.random.normal(ks[2], (E, H, F), jnp.float32) * (1.0 / np.sqrt(H))
        b1 = jax.random.normal(ks[3], (E, F), jnp.float32) * 0.01
        W2 = jax.random.normal(ks[4], (E, F, H), jnp.float32) * (1.0 / np.sqrt(F))
        b2 = jax.random.normal(ks[5], (E, H), jnp.float32) * 0.01
        gamma = jnp.ones((H,), jnp.float32)
        beta = jnp.zeros((H,), jnp.float32)
        return {'hidden_states': hidden_states, 'Wr': Wr, 'br': br, 'W1': W1, 'b1': b1, 'W2': W2, 'b2': b2, 'gamma': gamma, 'beta': beta, 'token_mask': token_mask}
    _L0_ffn_in = _L0_ffn_setup()

    def _L1_attn_setup():
        import jax, jax.numpy as jnp
        import numpy as np
        from jax import lax
        B, T, D, H, CONV_K = (4, 256, 128, 4, 4)
        DH = D // H
        EPS = 1e-05

        def _depthwise_causal_conv(u, w):
            K = w.shape[0]
            u_pad = jnp.pad(u, ((0, 0), (K - 1, 0), (0, 0)))
            kern = w[:, None, :]
            return lax.conv_general_dilated(u_pad, kern, (1,), 'VALID', dimension_numbers=('NWC', 'WIO', 'NWC'), feature_group_count=u.shape[-1])

        def _l2norm(x):
            return x * lax.rsqrt(jnp.sum(x * x, axis=-1, keepdims=True) + 1e-06)

        def _delta_rule(q, k, v, beta):

            def step(S, inp):
                q_t, k_t, v_t, b_t = inp
                kS = jnp.einsum('bhk,bhkv->bhv', k_t, S)
                delta = (v_t - kS) * b_t[..., None]
                S = S + jnp.einsum('bhk,bhv->bhkv', k_t, delta)
                o_t = jnp.einsum('bhk,bhkv->bhv', q_t, S)
                return (S, o_t)
            S0 = jnp.zeros((q.shape[0], q.shape[2], q.shape[3], v.shape[3]), dtype=q.dtype)
            tm = lambda a: jnp.swapaxes(a, 0, 1)
            _, o = lax.scan(step, S0, (tm(q), tm(k), tm(v), jnp.swapaxes(beta, 0, 1)))
            return jnp.swapaxes(o, 0, 1)
        key = jax.random.key(seed)
        ks = jax.random.split(key, 10)
        s = 0.02
        return {'x': jax.random.normal(ks[0], (B, T, D), dtype=jnp.float32), 'Wq': jax.random.normal(ks[1], (D, D), dtype=jnp.float32) * s, 'Wk': jax.random.normal(ks[2], (D, D), dtype=jnp.float32) * s, 'Wv': jax.random.normal(ks[3], (D, D), dtype=jnp.float32) * s, 'Wb': jax.random.normal(ks[4], (D, H), dtype=jnp.float32) * s, 'conv_q': jax.random.normal(ks[5], (CONV_K, D), dtype=jnp.float32) * 0.1, 'conv_k': jax.random.normal(ks[6], (CONV_K, D), dtype=jnp.float32) * 0.1, 'conv_v': jax.random.normal(ks[7], (CONV_K, D), dtype=jnp.float32) * 0.1, 'g_rms': jnp.ones((DH,), dtype=jnp.float32), 'Wo': jax.random.normal(ks[8], (D, D), dtype=jnp.float32) * s, 'ln_g': jnp.ones((D,), dtype=jnp.float32), 'ln_b': jnp.zeros((D,), dtype=jnp.float32)}
    _L1_attn_in = _L1_attn_setup()

    def _L1_ffn_setup():
        import jax, jax.numpy as jnp
        import numpy as np
        BLOCK = 16
        _GRID = jnp.array([0.0, 0.5, 1.0, 1.5, 2.0, 3.0, 4.0, 6.0], dtype=jnp.float32)
        _MID = jnp.array([0.25, 0.75, 1.25, 1.75, 2.5, 3.5, 5.0], dtype=jnp.float32)

        def fp4_quant_dequant(x):
            shape = x.shape
            xb = x.reshape(shape[:-1] + (shape[-1] // BLOCK, BLOCK))
            scale = jnp.max(jnp.abs(xb), axis=-1, keepdims=True) / 6.0
            scale = jnp.maximum(scale, jnp.float32(1e-12))
            xn = xb / scale
            idx = jnp.searchsorted(_MID, jnp.abs(xn))
            q = _GRID[idx] * jnp.sign(xn) * scale
            return q.reshape(shape)

        def fp4_linear(x, w):
            xq = fp4_quant_dequant(x)
            wq = fp4_quant_dequant(w)
            return jnp.einsum('bsk,nk->bsn', xq, wq)
        key = jax.random.key(seed)
        k1, k2, k3, k4 = jax.random.split(key, 4)
        H, I = (128, 352)
        x = jax.random.normal(k1, (4, 512, H), dtype=jnp.float32)
        w_gate = jax.random.normal(k2, (I, H), dtype=jnp.float32) * 0.02
        w_up = jax.random.normal(k3, (I, H), dtype=jnp.float32) * 0.02
        w_down = jax.random.normal(k4, (H, I), dtype=jnp.float32) * 0.02
        return {'x': x, 'w_gate': w_gate, 'w_up': w_up, 'w_down': w_down}
    _L1_ffn_in = _L1_ffn_setup()
    _d = {'L0_attn_hidden_states': _L0_attn_in['hidden_states'], 'L0_attn_in_proj_w': _L0_attn_in['in_proj_w'], 'L0_attn_conv1d_w': _L0_attn_in['conv1d_w'], 'L0_attn_conv1d_bias': _L0_attn_in['conv1d_bias'], 'L0_attn_x_proj_w': _L0_attn_in['x_proj_w'], 'L0_attn_dt_proj_w': _L0_attn_in['dt_proj_w'], 'L0_attn_dt_proj_b': _L0_attn_in['dt_proj_b'], 'L0_attn_A_log': _L0_attn_in['A_log'], 'L0_attn_D': _L0_attn_in['D'], 'L0_attn_conv1db_w': _L0_attn_in['conv1db_w'], 'L0_attn_conv1db_bias': _L0_attn_in['conv1db_bias'], 'L0_attn_x_projb_w': _L0_attn_in['x_projb_w'], 'L0_attn_dt_projb_w': _L0_attn_in['dt_projb_w'], 'L0_attn_dt_projb_b': _L0_attn_in['dt_projb_b'], 'L0_attn_A_b_log': _L0_attn_in['A_b_log'], 'L0_attn_D_b': _L0_attn_in['D_b'], 'L0_attn_out_proj_w': _L0_attn_in['out_proj_w'], 'L0_attn_fft_conv_w': _L0_attn_in['fft_conv_w'], 'L0_attn_fft_conv_b': _L0_attn_in['fft_conv_b'], 'L0_ffn_Wr': _L0_ffn_in['Wr'], 'L0_ffn_br': _L0_ffn_in['br'], 'L0_ffn_W1': _L0_ffn_in['W1'], 'L0_ffn_b1': _L0_ffn_in['b1'], 'L0_ffn_W2': _L0_ffn_in['W2'], 'L0_ffn_b2': _L0_ffn_in['b2'], 'L0_ffn_gamma': _L0_ffn_in['gamma'], 'L0_ffn_beta': _L0_ffn_in['beta'], 'L0_ffn_token_mask': _L0_ffn_in['token_mask'], 'L1_attn_Wq': _L1_attn_in['Wq'], 'L1_attn_Wk': _L1_attn_in['Wk'], 'L1_attn_Wv': _L1_attn_in['Wv'], 'L1_attn_Wb': _L1_attn_in['Wb'], 'L1_attn_conv_q': _L1_attn_in['conv_q'], 'L1_attn_conv_k': _L1_attn_in['conv_k'], 'L1_attn_conv_v': _L1_attn_in['conv_v'], 'L1_attn_g_rms': _L1_attn_in['g_rms'], 'L1_attn_Wo': _L1_attn_in['Wo'], 'L1_attn_ln_g': _L1_attn_in['ln_g'], 'L1_attn_ln_b': _L1_attn_in['ln_b'], 'L1_ffn_w_gate': _L1_ffn_in['w_gate'], 'L1_ffn_w_up': _L1_ffn_in['w_up'], 'L1_ffn_w_down': _L1_ffn_in['w_down']}
    _x0 = _d['L0_attn_hidden_states']
    _d['L0_attn_hidden_states'] = jax.random.normal(jax.random.fold_in(jax.random.key(seed), 1), (16, 256, 128), dtype=_x0.dtype)
    del _x0
    return _d

def reference(L0_attn_hidden_states, L0_attn_in_proj_w, L0_attn_conv1d_w, L0_attn_conv1d_bias, L0_attn_x_proj_w, L0_attn_dt_proj_w, L0_attn_dt_proj_b, L0_attn_A_log, L0_attn_D, L0_attn_conv1db_w, L0_attn_conv1db_bias, L0_attn_x_projb_w, L0_attn_dt_projb_w, L0_attn_dt_projb_b, L0_attn_A_b_log, L0_attn_D_b, L0_attn_out_proj_w, L0_attn_fft_conv_w, L0_attn_fft_conv_b, L0_ffn_Wr, L0_ffn_br, L0_ffn_W1, L0_ffn_b1, L0_ffn_W2, L0_ffn_b2, L0_ffn_gamma, L0_ffn_beta, L0_ffn_token_mask, L1_attn_Wq, L1_attn_Wk, L1_attn_Wv, L1_attn_Wb, L1_attn_conv_q, L1_attn_conv_k, L1_attn_conv_v, L1_attn_g_rms, L1_attn_Wo, L1_attn_ln_g, L1_attn_ln_b, L1_ffn_w_gate, L1_ffn_w_up, L1_ffn_w_down):

    def _L0_attn_ref(hidden_states, in_proj_w, conv1d_w, conv1d_bias, x_proj_w, dt_proj_w, dt_proj_b, A_log, D, conv1db_w, conv1db_bias, x_projb_w, dt_projb_w, dt_projb_b, A_b_log, D_b, out_proj_w, fft_conv_w, fft_conv_b):
        import jax, jax.numpy as jnp
        from jax import lax
        import numpy as np

        def _causal_dwconv(x, w, b):
            k = w.shape[-1]
            y = lax.conv_general_dilated(x, w, (1,), [(k - 1, 0)], feature_group_count=w.shape[0], dimension_numbers=('NCH', 'OIH', 'NCH'))
            return y + b[None, :, None]

        def _mamba_branch(xz, conv_w, conv_b, xproj_w, dtproj_w, dt_bias, A_log, Dp):
            x, z = jnp.split(xz, 2, axis=1)
            x = jax.nn.silu(_causal_dwconv(x, conv_w, conv_b))
            r = dtproj_w.shape[1]
            n = A_log.shape[1]
            x_dbl = jnp.einsum('bdl,ed->bel', x, xproj_w)
            dt, Bm, Cm = (x_dbl[:, :r], x_dbl[:, r:r + n], x_dbl[:, r + n:])
            delta = jax.nn.softplus(jnp.einsum('brl,dr->bdl', dt, dtproj_w) + dt_bias[None, :, None])
            A = -jnp.exp(A_log)
            dA = jnp.exp(jnp.einsum('bdl,dn->lbdn', delta, A))
            dBu = jnp.einsum('bdl,bnl,bdl->lbdn', delta, Bm, x)

            def step(h, ab):
                h = ab[0] * h + ab[1]
                return (h, h)
            _, hs = lax.scan(step, jnp.zeros_like(dA[0]), (dA, dBu))
            y = jnp.einsum('lbdn,bnl->bdl', hs, Cm) + Dp[None, :, None] * x
            return y * jax.nn.silu(z)
        xz = jnp.einsum('bld,ed->bel', hidden_states, in_proj_w)
        out = _mamba_branch(xz, conv1d_w, conv1d_bias, x_proj_w, dt_proj_w, dt_proj_b, A_log, D)
        out_b = _mamba_branch(xz[:, :, ::-1], conv1db_w, conv1db_bias, x_projb_w, dt_projb_w, dt_projb_b, A_b_log, D_b)
        x, z = jnp.split(xz, 2, axis=1)
        xf = jnp.fft.fftn(x, axes=(-2, -1))
        xc = jnp.concatenate([xf.real, xf.imag], axis=1)
        xc = lax.conv_general_dilated(xc, fft_conv_w, (1,), [(2, 2)], dimension_numbers=('NCH', 'OIH', 'NCH'))
        xc = jax.nn.silu(xc + fft_conv_b[None, :, None])
        re, im = jnp.split(xc, 2, axis=1)
        x_out = jnp.fft.ifftn(lax.complex(re, im), axes=(-2, -1))
        z_out = jnp.max(jax.nn.silu(z), axis=-1, keepdims=True)
        v = jnp.abs(x_out * z_out)
        mu = jnp.mean(v, axis=-1, keepdims=True)
        var = jnp.var(v, axis=-1, keepdims=True)
        out_f = (v - mu) / jnp.sqrt(var + 1e-05)
        y = out + out_b[:, :, ::-1] + out_f
        return jnp.einsum('bdl,od->blo', y, out_proj_w)

    def _L0_ffn_ref(hidden_states, Wr, br, W1, b1, W2, b2, gamma, beta, token_mask):
        import math
        import jax, jax.numpy as jnp
        import numpy as np
        E = 8
        TOPK = 2
        CF = 1.25
        EPS = 1e-05
        NEG = -1e+30

        def _layer_norm(x, gamma, beta):
            mu = jnp.mean(x, axis=-1, keepdims=True)
            var = jnp.mean((x - mu) ** 2, axis=-1, keepdims=True)
            return (x - mu) * jax.lax.rsqrt(var + EPS) * gamma + beta
        B, S, H = hidden_states.shape
        x = hidden_states.reshape(-1, H)
        N = x.shape[0]
        logits = x @ Wr + br
        top_vals, top_idx = jax.lax.top_k(logits, TOPK)
        w = jax.nn.softmax(top_vals, axis=-1)
        flat_idx = top_idx.reshape(-1)
        flat_tok = jnp.repeat(jnp.arange(N), TOPK)
        w_flat = w.reshape(-1)
        cap = max(int(math.ceil(N / E * CF)), 1)
        key_mat = jnp.where(flat_idx[None, :] == jnp.arange(E)[:, None], w_flat[None, :], NEG)
        kv, ki = jax.lax.top_k(key_mat, cap)
        valid = kv > NEG / 2
        tok = flat_tok[ki]
        gate = jnp.where(valid, w_flat[ki], 0.0)
        xe = x[tok]
        h1 = jnp.einsum('ech,ehf->ecf', xe, W1) + b1[:, None, :]
        h1 = jax.nn.gelu(h1, approximate=False)
        y = jnp.einsum('ecf,efh->ech', h1, W2) + b2[:, None, :]
        out = jnp.zeros_like(x).at[tok.reshape(-1)].add((y * gate[..., None]).reshape(-1, H))
        out = out.reshape(B, S, H) + hidden_states
        return _layer_norm(out, gamma, beta)

    def _L1_attn_ref(x, Wq, Wk, Wv, Wb, conv_q, conv_k, conv_v, g_rms, Wo, ln_g, ln_b):
        import jax, jax.numpy as jnp
        import numpy as np
        from jax import lax
        B, T, D, H, CONV_K = (4, 256, 128, 4, 4)
        DH = D // H
        EPS = 1e-05

        def _depthwise_causal_conv(u, w):
            K = w.shape[0]
            u_pad = jnp.pad(u, ((0, 0), (K - 1, 0), (0, 0)))
            kern = w[:, None, :]
            return lax.conv_general_dilated(u_pad, kern, (1,), 'VALID', dimension_numbers=('NWC', 'WIO', 'NWC'), feature_group_count=u.shape[-1])

        def _l2norm(x):
            return x * lax.rsqrt(jnp.sum(x * x, axis=-1, keepdims=True) + 1e-06)

        def _delta_rule(q, k, v, beta):

            def step(S, inp):
                q_t, k_t, v_t, b_t = inp
                kS = jnp.einsum('bhk,bhkv->bhv', k_t, S)
                delta = (v_t - kS) * b_t[..., None]
                S = S + jnp.einsum('bhk,bhv->bhkv', k_t, delta)
                o_t = jnp.einsum('bhk,bhkv->bhv', q_t, S)
                return (S, o_t)
            S0 = jnp.zeros((q.shape[0], q.shape[2], q.shape[3], v.shape[3]), dtype=q.dtype)
            tm = lambda a: jnp.swapaxes(a, 0, 1)
            _, o = lax.scan(step, S0, (tm(q), tm(k), tm(v), jnp.swapaxes(beta, 0, 1)))
            return jnp.swapaxes(o, 0, 1)
        silu = jax.nn.silu
        q = silu(_depthwise_causal_conv(x @ Wq, conv_q))
        k = silu(_depthwise_causal_conv(x @ Wk, conv_k))
        v = silu(_depthwise_causal_conv(x @ Wv, conv_v))
        beta = jax.nn.sigmoid(x @ Wb)
        hs = lambda a: a.reshape(a.shape[0], a.shape[1], H, DH)
        q, k, v = (_l2norm(hs(q)), _l2norm(hs(k)), hs(v))
        o = _delta_rule(q, k, v, beta)
        o = o * lax.rsqrt(jnp.mean(o * o, axis=-1, keepdims=True) + EPS) * g_rms
        y = o.reshape(x.shape[0], x.shape[1], D) @ Wo
        y = y + x
        mu = jnp.mean(y, axis=-1, keepdims=True)
        var = jnp.mean((y - mu) ** 2, axis=-1, keepdims=True)
        y = (y - mu) * lax.rsqrt(var + EPS) * ln_g + ln_b
        return y

    def _L1_ffn_ref(x, w_gate, w_up, w_down):
        import jax, jax.numpy as jnp
        import numpy as np
        BLOCK = 16
        _GRID = jnp.array([0.0, 0.5, 1.0, 1.5, 2.0, 3.0, 4.0, 6.0], dtype=jnp.float32)
        _MID = jnp.array([0.25, 0.75, 1.25, 1.75, 2.5, 3.5, 5.0], dtype=jnp.float32)

        def fp4_quant_dequant(x):
            shape = x.shape
            xb = x.reshape(shape[:-1] + (shape[-1] // BLOCK, BLOCK))
            scale = jnp.max(jnp.abs(xb), axis=-1, keepdims=True) / 6.0
            scale = jnp.maximum(scale, jnp.float32(1e-12))
            xn = xb / scale
            idx = jnp.searchsorted(_MID, jnp.abs(xn))
            q = _GRID[idx] * jnp.sign(xn) * scale
            return q.reshape(shape)

        def fp4_linear(x, w):
            xq = fp4_quant_dequant(x)
            wq = fp4_quant_dequant(w)
            return jnp.einsum('bsk,nk->bsn', xq, wq)
        gate = fp4_linear(x, w_gate)
        y = fp4_linear(x, w_up)
        h = jax.nn.silu(gate) * y
        return fp4_linear(h, w_down)
    x = L0_attn_hidden_states
    xn = _layernorm(x, axis=-1)
    x = x + _L0_attn_ref(xn, L0_attn_in_proj_w, L0_attn_conv1d_w, L0_attn_conv1d_bias, L0_attn_x_proj_w, L0_attn_dt_proj_w, L0_attn_dt_proj_b, L0_attn_A_log, L0_attn_D, L0_attn_conv1db_w, L0_attn_conv1db_bias, L0_attn_x_projb_w, L0_attn_dt_projb_w, L0_attn_dt_projb_b, L0_attn_A_b_log, L0_attn_D_b, L0_attn_out_proj_w, L0_attn_fft_conv_w, L0_attn_fft_conv_b) + _L0_ffn_ref(xn, L0_ffn_Wr, L0_ffn_br, L0_ffn_W1, L0_ffn_b1, L0_ffn_W2, L0_ffn_b2, L0_ffn_gamma, L0_ffn_beta, L0_ffn_token_mask)
    xn = _layernorm(x, axis=-1)
    x = x + _L1_attn_ref(xn, L1_attn_Wq, L1_attn_Wk, L1_attn_Wv, L1_attn_Wb, L1_attn_conv_q, L1_attn_conv_k, L1_attn_conv_v, L1_attn_g_rms, L1_attn_Wo, L1_attn_ln_g, L1_attn_ln_b) + _L1_ffn_ref(xn, L1_ffn_w_gate, L1_ffn_w_up, L1_ffn_w_down)
    return x

_drawn_inputs = setup_inputs


def setup_inputs(seed=0):
    import zlib

    import numpy as np

    out = dict(_drawn_inputs(seed))
    spreads = {'L0_ffn_br': (0.0, 0.1),
     'L0_ffn_gamma': (1.0, 0.2),
     'L0_ffn_beta': (0.0, 0.1),
     'L1_attn_g_rms': (1.0, 0.6),
     'L1_attn_ln_g': (1.0, 0.6),
     'L1_attn_ln_b': (0.0, 0.8)}
    factors = {'L0_attn_conv1d_w': 8.0,
     'L0_attn_conv1d_bias': 8.0,
     'L0_attn_x_proj_w': 8.0,
     'L0_attn_dt_proj_w': 8.0,
     'L0_attn_dt_proj_b': 8.0,
     'L0_attn_A_log': 8.0,
     'L0_attn_D': 8.0,
     'L0_attn_conv1db_w': 8.0,
     'L0_attn_conv1db_bias': 8.0,
     'L0_attn_x_projb_w': 8.0,
     'L0_attn_dt_projb_w': 8.0,
     'L0_attn_dt_projb_b': 8.0,
     'L0_attn_A_b_log': 8.0,
     'L0_attn_D_b': 8.0,
     'L0_attn_fft_conv_b': 30.326,
     'L0_ffn_b1': 127.166,
     'L0_ffn_b2': 104.721,
     'L1_attn_Wb': 49.18,
     'L1_ffn_w_gate': 8.0,
     'L1_ffn_w_up': 8.0,
     'L1_ffn_w_down': 8.0,
     'L1_attn_Wq': 3.248,
     'L1_attn_Wk': 3.205,
     'L1_attn_Wv': 3.141,
     'L1_attn_conv_q': 3.314,
     'L1_attn_conv_k': 3.297,
     'L1_attn_conv_v': 3.268,
     'L1_attn_Wo': 3.232}
    for name, (base, spread) in spreads.items():
        noise = np.random.default_rng([zlib.crc32(name.encode()), seed]).standard_normal(out[name].shape)
        drawn = base * np.exp(spread * noise) if base else spread * noise
        out[name] = jnp.asarray(drawn.astype(out[name].dtype))
    for name, factor in factors.items():
        out[name] = (out[name] * factor).astype(out[name].dtype)
    return out
```

```python
from contextlib import ExitStack

import numpy as np

import concourse.bass as bass
from concourse import mybir

ALU = mybir.AluOpType
ACT = mybir.ActivationFunctionType
AX = mybir.AxisListType
F32 = mybir.dt.float32
BF16 = mybir.dt.bfloat16
I32 = mybir.dt.int32

P = 128
B, L, DM = 16, 256, 128
NTOK = B * L
NT = NTOK // P
DI, DS, DR = 256, 16, 64
EPS = 1e-5


def makers(nc, ctx, tag):
    def sb(name, shape, dt=F32):
        return ctx.enter_context(nc.sbuf_tensor(f"{tag}_{name}", shape, dt))

    def ps(name, shape, dt=F32):
        return ctx.enter_context(nc.psum_tensor(f"{tag}_{name}", shape, dt))

    def sem(name):
        return ctx.enter_context(nc.semaphore(f"{tag}_{name}"))

    return sb, ps, sem


def bcast(ap, n):
    return ap.unsqueeze(len(ap.shape)).broadcast_to([*ap.shape, n])


NE, CAP, FF = 8, 640, 512
NSLOT = NE * CAP
assert CAP == -(-NTOK * 5 // (4 * NE)) and CAP % P == 0


AH, AD = 4, 32
NLEV = 7


FI, QB = 352, 16
FCH = ((0, 128), (128, 128), (256, 96))


def norm_input(nc, x, xn_dram, xnT_dram, ident_in):
    with ExitStack() as ctx:
        sb, ps, sem = makers(nc, ctx, "n1")
        X = sb("X", [P, NT, DM])
        SQ = sb("SQ", [P, NT, DM])
        XT = sb("XT", [P, NT * P])
        ident = sb("ident", [P, P])
        stat = sb("stat", [P, 4, NT])
        psT = ps("psT", [P, 4, 512])
        x_loaded, ident_loaded = [sem("x_loaded0"), sem("x_loaded1")], sem("ident_loaded")
        var_ready, std_ready = sem("var_ready"), sem("std_ready")
        xn_ready, turned, evicted = sem("xn_ready"), sem("turned"), sem("evicted")
        stored, step_done = sem("stored"), sem("step_done")
        H = NT // 2
        with nc.Block() as block:
            @block.sync
            def _(sp):
                for h in range(2):
                    sp.dma_start(X[:, h * H:(h + 1) * H, :],
                                 x.rearrange("(n p) d -> p n d", p=P)[:, h * H:(h + 1) * H, :]).then_inc(x_loaded[h], 16)
                sp.dma_start(ident[:], ident_in).then_inc(ident_loaded, 16)
                for h in range(2):
                    sp.wait_ge(xn_ready, h + 1)
                    sp.dma_start(xn_dram.rearrange("(n p) d -> p n d", p=P)[:, h * H:(h + 1) * H, :],
                                 X[:, h * H:(h + 1) * H, :]).then_inc(stored, 16)
                sp.wait_ge(evicted, NT // 4)
                sp.dma_start(xnT_dram, XT[:]).then_inc(stored, 16)
                sp.wait_ge(stored, 48)

            @block.vector
            def _(dve):
                done = [0]

                def link(ins):
                    done[0] += 1
                    ins.then_inc(step_done, 1)
                    dve.wait_ge(step_done, done[0])

                for h in range(2):
                    xs, sq = X[:, h * H:(h + 1) * H, :], SQ[:, h * H:(h + 1) * H, :]
                    mean, var = stat[:, 0, h * H:(h + 1) * H], stat[:, 1, h * H:(h + 1) * H]
                    std, rstd = stat[:, 2, h * H:(h + 1) * H], stat[:, 3, h * H:(h + 1) * H]
                    dve.wait_ge(x_loaded[h], 16)
                    link(dve.tensor_reduce(mean, xs, AX.X, ALU.add))
                    link(dve.tensor_scalar(mean, mean, 1.0 / DM, None, ALU.mult))
                    link(dve.tensor_tensor(xs, xs, bcast(mean, DM), ALU.subtract))
                    link(dve.tensor_tensor(sq, xs, xs, ALU.mult))
                    link(dve.tensor_reduce(var, sq, AX.X, ALU.add))
                    dve.tensor_scalar(var, var, 1.0 / DM, EPS, ALU.mult, ALU.add).then_inc(var_ready, 1)
                    dve.wait_ge(std_ready, h + 1)
                    link(dve.reciprocal(rstd, std))
                    dve.tensor_tensor(xs, xs, bcast(rstd, DM), ALU.mult).then_inc(xn_ready, 1)

            @block.scalar
            def _(act):
                for h in range(2):
                    act.wait_ge(var_ready, h + 1)
                    act.activation(stat[:, 2, h * H:(h + 1) * H], stat[:, 1, h * H:(h + 1) * H],
                                   ACT.Sqrt).then_inc(std_ready, 1)
                for g in range(NT // 4):
                    act.wait_ge(turned, g + 1)
                    act.activation(XT[:, g * 512:(g + 1) * 512], psT[:, g % 4, :], ACT.Copy).then_inc(evicted, 1)

            @block.tensor
            def _(pe):
                pe.wait_ge(ident_loaded, 16)
                for g in range(NT // 4):
                    pe.wait_ge(xn_ready, 1 + g // (NT // 8))
                    if g >= 4:
                        pe.wait_ge(evicted, g - 3)
                    for k in range(4):
                        mm = pe.transpose(psT[:, g % 4, k * P:(k + 1) * P], X[:, 4 * g + k, :], ident[:])
                    mm.then_inc(turned, 1)


def mamba_fft(nc, x, xnT_dram, x1_dram, winT, dft, convw, xpT, dtT, woutT, small, sel_in, ident_in):
    NPAIR = B // 2
    ROW = 2 * L
    HN = DS // 2
    FFT_STEP = 5
    with ExitStack() as ctx:
        sb, ps, sem = makers(nc, ctx, "m")
        winT_s = sb("winT", [P, 4 * P])
        dft_s = sb("dft", [P, 3, 2, 512])
        convw_s = sb("convw", [P, 4, 5, 512])
        xp_s = sb("xp", [P, 2, 2, 160])
        dtT_s = sb("dtT", [DR, 2, DI])
        wout_s = sb("wout", [P, 2, DM])
        small_s = sb("small", [P, 96])
        negA = sb("negA", [P, 2, 32])
        self_s = sb("self", [96, 32])
        sel = sb("sel", [96, 32], BF16)
        one = sb("one", [P, 1])
        ident = sb("ident", [P, P])
        diag = sb("diag", [P, 2, 2, 4, P])
        xnT = sb("xnT", [P, ROW])
        xtok = sb("xtok", [P, 4, P])
        xl = sb("xl", [P, 2, 2, 256])
        XF = sb("XF", [P, 2, 2, 2, 256])
        U = XF[:].rearrange("p a b c d -> p (a b c d)").rearrange("p (k s n) -> p k s n", k=2, s=2)
        xc = sb("xc", [P, 4, 2, 260])
        Z = sb("Z", [P, 4, 2, 256])
        V = xl[:].rearrange("p a b c -> p (a b) c")
        stat = sb("stat", [P, 8, 4])
        xpad = sb("xpad", [P, 2, 2, 2, 3 + L])
        u = sb("u", [P, 2, 2, ROW])
        sz = sb("sz", [P, 2, ROW])
        dt = sb("dt", [DR, ROW])
        bc32 = sb("bc32", [96, ROW])
        bcr = sb("bcr", [96, ROW])
        bcq = sb("bcq", [64, ROW], BF16)
        bcs = sb("bcs", [96, 2, ROW], BF16)
        tmp = sb("tmp", [P, ROW])
        delta = sb("delta", [P, 2, 2, ROW])
        dx = sb("dx", [P, 2, 2, ROW])
        dA = sb("dA", [P, 2, 4, 2, L])
        h = sb("h", [P, 2, HN, ROW])
        y = sb("y", [P, 2, 2, ROW])
        ypart = sb("ypart", [P, ROW])
        psR = ps("psR", [P, 2, 1024])
        psG = ps("psG", [P, 4, 512])

        consts_loaded, rows_zeroed, negA_ready, sel_ready = (sem("consts_loaded"), sem("rows_zeroed"),
                                                           sem("negA_ready"), sem("sel_ready"))
        xnT_loaded, xtok_loaded, x1_stored = sem("xnT_loaded"), sem("xtok_loaded"), sem("x1_stored")
        job_ready, job_evicted = sem("job_ready"), sem("job_evicted")
        diag_ready = sem("diag_ready")
        bc_copied, bcs_ready = sem("bc_copied"), sem("bcs_ready")
        softplus_parts, dx_ready = sem("softplus_parts"), sem("dx_ready")
        spread, spread_used = sem("spread"), sem("spread_used")
        exp_ready, scan_done = sem("exp_ready"), sem("scan_done")
        gate_ready, y_ready, out_ready, res_ready = sem("gate_ready"), sem("y_ready"), sem("out_ready"), sem("res_ready")
        zz_ready, mod2_ready, mod_ready = sem("zz_ready"), sem("mod2_ready"), sem("mod_ready")
        var_ready, std_ready = sem("var_ready"), sem("std_ready")
        dve_step, act_step, pool_step = sem("dve_step"), sem("act_step"), sem("pool_step")

        def cw(r, c, k): return small_s[:, 46 * r + 4 * c + k:46 * r + 4 * c + k + 1]
        def cb(r, c): return small_s[:, 46 * r + 8 + c:46 * r + 9 + c]
        def dtb(r, c): return small_s[:, 46 * r + 10 + c:46 * r + 11 + c]
        def alog(r): return small_s[:, 46 * r + 12:46 * r + 44]
        def dskip(r, c): return small_s[:, 46 * r + 44 + c:46 * r + 45 + c]
        def fcb(o): return small_s[:, 92 + o:93 + o]

        XZ, XL, DW, DIR, S1 = 0, 4, 6, 10, 18
        S2, CV, S3, S4 = S1 + 4, S1 + 8, S1 + 12, S1 + 16
        JOBS = S4 + 4
        OUT = JOBS
        assert OUT % 4 == 2

        def wait_bank(pe, i, j):
            if j == OUT:
                pe.wait_ge(job_evicted, i * JOBS + (OUT - 4) + 1 + JOBS)
            elif j >= 4:
                pe.wait_ge(job_evicted, i * JOBS + j - 3 + JOBS)
            else:
                last = {0: JOBS - 2, 1: JOBS - 1, 2: JOBS - 4, 3: JOBS - 3}[j]
                pe.wait_ge(job_evicted, i * JOBS + last + 1)
                if j == 2:
                    pe.wait_ge(res_ready, i)

        ends = {}
        n = 0
        for j0, k in ((S1, 2), (S2, 4), (CV, 20), (S3, 4), (S4, 4)):
            for j in range(j0, j0 + 4):
                n += k
                ends[j] = (n - 1) // FFT_STEP
        slots = 32
        assert max(ends.values()) < slots

        with nc.Block() as block:
            @block.sync
            def _(sp):
                sp.dma_start(winT_s[:], winT).then_inc(consts_loaded, 16)
                sp.dma_start(small_s[:], small).then_inc(consts_loaded, 16)
                sp.dma_start(xp_s[:], xpT).then_inc(consts_loaded, 16)
                sp.dma_start(dtT_s[:], dtT).then_inc(consts_loaded, 16)
                sp.dma_start(wout_s[:], woutT).then_inc(consts_loaded, 16)
                sp.dma_start(self_s[:], sel_in).then_inc(consts_loaded, 16)
                sp.dma_start(ident[:], ident_in).then_inc(consts_loaded, 16)
                sp.dma_start(dft_s[:], dft).then_inc(consts_loaded, 16)
                sp.dma_start(convw_s[:], convw).then_inc(consts_loaded, 16)
                with sp.Fori(0, NPAIR) as i:
                    sp.wait_ge(job_evicted, i * JOBS + 6)
                    sp.dma_start(xnT[:], xnT_dram[:, bass.ds(i * ROW, ROW)]).then_inc(xnT_loaded, 16)
                    sp.wait_ge(x1_stored, i * 16)
                    sp.dma_start(xtok[:], x.rearrange("(i n p) d -> i p n d", p=P, n=4)[bass.ds(i, 1)].rearrange("i p n d -> p (i n) d")).then_inc(xtok_loaded, 16)
                    sp.wait_ge(res_ready, i + 1)
                    sp.dma_start(x1_dram.rearrange("(i n p) d -> i p n d", p=P, n=4)[bass.ds(i, 1)].rearrange("i p n d -> p (i n) d"), xtok[:]).then_inc(x1_stored, 16)
                sp.wait_ge(x1_stored, 16 * NPAIR)

            @block.gpsimd
            def _(pool):
                pool.memset(xpad[:, :, :, :, 0:3], 0.0)
                pool.memset(xc[:, :, :, 0:2], 0.0)
                pool.memset(xc[:, :, :, 258:260], 0.0)
                pool.memset(dA[:, :, :, :, 0:1], 0.0)
                pool.memset(one[:], 1.0).then_inc(rows_zeroed, 1)
                pool.wait_ge(consts_loaded, 16 * 9)
                with pool.Fori(0, NPAIR) as i:
                    steps = 0
                    for r in range(2):
                        for c in range(2):
                            pool.wait_ge(softplus_parts, i * 4 + r * 2 + c + 1)
                            steps += 1
                            pool.tensor_tensor(delta[:, r, c, :], delta[:, r, c, :], dx[:, r, c, :], ALU.add).then_inc(pool_step, 1)
                            pool.wait_ge(pool_step, steps)
                            pool.tensor_tensor(dx[:, r, c, :], delta[:, r, c, :], u[:, r, c, :], ALU.mult).then_inc(dx_ready, 1)
                    pool.sem_clear(pool_step)

            @block.scalar
            def _(act):
                act.sem_inc(job_evicted, JOBS)
                act.wait_ge(consts_loaded, 16 * 9)
                act.wait_ge(rows_zeroed, 1)
                for r in range(2):
                    act.activation(negA[:, r, :], alog(r), ACT.Exp).then_inc(negA_ready, 1)
                act.wait_ge(negA_ready, 4)
                with act.Fori(0, NPAIR) as i:
                    steps = [0]

                    def link(ins):
                        steps[0] += 1
                        ins.then_inc(act_step, 1)
                        act.wait_ge(act_step, steps[0])

                    def done(j):
                        act.wait_ge(job_ready, i * JOBS + j + 1)
                        return psG[:, j % 4, :]

                    for c in range(2):
                        pz = done(XZ + c).rearrange("p (s l) -> p s l", s=2)
                        act.activation(xpad[:, 0, c, :, 3:], pz, ACT.Copy)
                        act.activation(xpad[:, 1, c, :, 3:][:, :, ::-1], pz, ACT.Copy).then_inc(job_evicted, 1)
                    act.wait_ge(y_ready, i)
                    for c in range(2):
                        act.activation(sz[:, c, :], done(XZ + 2 + c), ACT.Silu).then_inc(job_evicted, 1)
                    for s in range(2):
                        act.activation(xl[:, s, :, :], done(XL + s).rearrange("p (k d) -> p k d", k=2), ACT.Copy).then_inc(job_evicted, 1)
                    for r in range(2):
                        for c in range(2):
                            act.activation(u[:, r, c, :], done(DW + 2 * r + c), ACT.Silu, bias=cb(r, c)).then_inc(job_evicted, 1)
                    for r in range(2):
                        j = DIR + 4 * r
                        act.activation(dt[:], done(j)[0:DR, :], ACT.Copy).then_inc(job_evicted, 1)
                        pb = done(j + 1)[0:96, :]
                        act.wait_ge(bcs_ready, i * 2 + r)
                        act.activation(bcs[:, r, :], pb, ACT.Copy).then_inc(bc_copied, 1)
                        act.activation(bc32[:], pb, ACT.Copy).then_inc(job_evicted, 1)
                        for c in range(2):
                            pd = done(j + 2 + c)
                            act.wait_ge(softplus_parts, i * 4 + 2 * r + c)
                            link(act.activation(tmp[:], pd, ACT.Abs, bias=dtb(r, c)))
                            act.activation(dx[:, r, c, :], pd, ACT.Relu, bias=dtb(r, c)).then_inc(job_evicted, 1)
                            link(act.activation(tmp[:], tmp[:], ACT.Exp, scale=-1.0))
                            act.activation(delta[:, r, c, :], tmp[:], ACT.Ln, bias=one[:]).then_inc(softplus_parts, 1)

                    def decays(e):
                        r, c = e // 8, e % 2
                        n0 = (e // 4 % 2) * HN + (e // 2 % 2) * 4
                        act.wait_ge(scan_done, i * 16 + e + 1)
                        act.wait_ge(dx_ready, i * 4 + r * 2 + c + 1)
                        dr = delta[:, r, c, :].rearrange("p (s l) -> p s l", s=2)[:, :, 1:]
                        for n in range(4):
                            k = 16 * c + n0 + n
                            ins = act.activation(dA[:, e % 2, n, :, 1:], dr, ACT.Exp, scale=negA[:, r, k:k + 1])
                        ins.then_inc(exp_ready, 1)

                    def evict(j):
                        pj = done(j)
                        k = (j - S1) % 4
                        if j < S2:
                            out = XF[:, :, k % 2, k // 2, :]
                            ins = act.activation(out, pj.rearrange("p (a k) -> p a k", a=2), ACT.Copy)
                        elif j < CV:
                            ins = act.activation(xc[:, k, :, 2:258], pj.rearrange("p (s k) -> p s k", s=2), ACT.Copy)
                        elif j < S3:
                            ins = act.activation(Z[:, k, :, :], pj.rearrange("p (s k) -> p s k", s=2), ACT.Silu, bias=fcb(k))
                        elif j < S4:
                            ins = act.activation(U[:, k % 2, k // 2, :], pj, ACT.Copy)
                        else:
                            ins = act.activation(Z[:, k, :, :], pj.rearrange("p (a l) -> p a l", a=2), ACT.Square)
                        ins.then_inc(job_evicted, 1)

                    decays(0)
                    decays(1)
                    for s in range(slots):
                        if s % 8 in (2, 4) and s < slots - 4:
                            e = s // 8 * 4 + (2 if s % 8 == 2 else 4)
                            decays(e)
                            decays(e + 1)
                        for j in sorted(ends):
                            if ends[j] == s:
                                evict(j)
                    act.wait_ge(mod2_ready, i + 1)
                    for k in range(4):
                        ins = act.activation(V[:, k, :], V[:, k, :], ACT.Sqrt, scale=stat[:, 1, k:k + 1])
                    ins.then_inc(mod_ready, 1)
                    act.wait_ge(var_ready, i + 1)
                    act.activation(stat[:, 5, :], stat[:, 4, :], ACT.Sqrt).then_inc(std_ready, 1)
                    act.sem_clear(act_step)

            @block.tensor
            def _(pe):
                pe.wait_ge(consts_loaded, 16 * 9)
                pe.wait_ge(rows_zeroed, 1)
                pe.wait_ge(sel_ready, 1)
                pe.wait_ge(diag_ready, 1)
                with pe.Fori(0, NPAIR) as i:
                    def job(j, mms, start=None):
                        for n, (out, lhsT, rhs, st, sp_) in enumerate(mms):
                            yield
                            if n == 0:
                                if start:
                                    start()
                                wait_bank(pe, i, j)
                            mm = pe.matmul(out, lhsT=lhsT, rhs=rhs, start=st, stop=sp_)
                        mm.then_inc(job_ready if j != OUT else out_ready, 1)

                    def run(steps):
                        for _ in steps:
                            pass

                    pe.wait_ge(xnT_loaded, 16 * i + 16)
                    for c in range(4):
                        run(job(XZ + c, [(psG[:, (XZ + c) % 4, :], winT_s[:, c * P:(c + 1) * P], xnT[:], True, True)]))
                    for s in range(2):
                        g = (XL + s) % 4
                        run(job(XL + s, [(psG[:, g, k * 256:(k + 1) * 256],
                                          xnT[:, s * L + k * P:s * L + (k + 1) * P], winT_s[:, 0:256], True, True)
                                         for k in range(2)]))
                    for r in range(2):
                        for c in range(2):
                            j = DW + 2 * r + c
                            if r == 0:
                                pe.wait_ge(job_evicted, i * JOBS + XZ + c + 1 + JOBS)
                            run(job(j, [(psG[:, j % 4, :], diag[:, r, c, k, :], xpad[:, r, c, :, k:k + L], k == 0, k == 3) for k in range(4)]))
                    for r in range(2):
                        j = DIR + 4 * r
                        pe.wait_ge(job_evicted, i * JOBS + DW + 2 * r + 2 + JOBS)
                        run(job(j, [(psG[0:DR, j % 4, :], xp_s[:, r, c, 0:DR], u[:, r, c, :], c == 0, c == 1) for c in range(2)]))
                        run(job(j + 1, [(psG[0:96, (j + 1) % 4, :], xp_s[:, r, c, DR:DR + 96], u[:, r, c, :], c == 0, c == 1) for c in range(2)]))
                        for c in range(2):
                            if c == 0:
                                pe.wait_ge(job_evicted, i * JOBS + j + 1 + JOBS)
                            run(job(j + 2 + c, [(psG[:, (j + 2 + c) % 4, :], dtT_s[:, r, c * P:(c + 1) * P], dt[:], True, True)]))

                    def evicted(upto):
                        return lambda: pe.wait_ge(job_evicted, i * JOBS + upto + JOBS)

                    def fft():
                        C, S, NS = (dft_s[:, 1, :, 0:256], dft_s[:, 1, :, 256:512], dft_s[:, 0, :, 256:512])
                        for k in range(4):
                            s, dc = k // 2, k % 2
                            yield from job(S1 + k, [(psG[:, (S1 + k) % 4, :], xl[:, s, lc, dc * P:(dc + 1) * P],
                                                     dft_s[:, 0, lc, :], lc == 0, lc == 1) for lc in range(2)],
                                           evicted(XL + 2) if k == 0 else None)
                        for k in range(4):
                            im, mc = k // 2, k % 2
                            pairs = ((C, 0), (S, 1)) if not im else ((C, 1), (NS, 0))
                            yield from job(S2 + k, [(psG[:, (S2 + k) % 4, :], t[:, dc, mc * P:(mc + 1) * P],
                                                     XF[:, a, dc, :, :], (n, dc) == (0, 0), (n, dc) == (1, 1))
                                                    for n, (t, a) in enumerate(pairs) for dc in range(2)],
                                           evicted(S2) if k == 0 else None)
                        for o in range(4):
                            yield from job(CV + o, [(psG[:, (CV + o) % 4, :], convw_s[:, c, t, o * P:(o + 1) * P],
                                                     xc[:, c, :, t:t + 256], (c, t) == (0, 0), (c, t) == (3, 4))
                                                    for c in range(4) for t in range(5)],
                                           evicted(CV) if o == 0 else None)
                        for k in range(4):
                            s, kc = k // 2, k % 2
                            yield from job(S3 + k, [(psG[:, (S3 + k) % 4, :], Z[:, m, s, kc * P:(kc + 1) * P],
                                                     dft_s[:, 1 + m // 2, m % 2, :], m == 0, m == 3) for m in range(4)],
                                           evicted(S3) if k == 0 else None)
                        for k in range(4):
                            s, dc = k // 2, k % 2
                            yield from job(S4 + k, [(psG[:, (S4 + k) % 4, :], U[:, kc, s, a * 256 + dc * P:a * 256 + (dc + 1) * P],
                                                     dft_s[:, 1 + a, kc, :], (a, kc) == (0, 0), (a, kc) == (1, 1))
                                                    for a in range(2) for kc in range(2)],
                                           evicted(S4) if k == 0 else None)

                    steps = fft()
                    next(steps)
                    for s in range(slots):
                        r, hf, k = s // 16, s // 8 % 2, s % 8
                        if s % 16 == 0:
                            pe.wait_ge(bcs_ready, i * 2 + r + 1)
                        pe.wait_ge(spread_used, i * slots + s + 1)
                        for m in range(2):
                            row = DS * (k // 4) + HN * hf + 2 * (k % 4) + m
                            mm = pe.matmul(psR[:, s % 2, m * 512:(m + 1) * 512],
                                           lhsT=sel[:, row:row + 1].broadcast_to([96, P]), rhs=bcs[:, r, :], start=True, stop=True)
                        mm.then_inc(spread, 1)
                        for _ in range(FFT_STEP):
                            next(steps, None)
                    run(steps)
                    pe.wait_ge(y_ready, i + 1)
                    run(job(OUT, [(psG[:, OUT % 4, n * P:(n + 1) * P], y[:, 0, c, n * P:(n + 1) * P], wout_s[:, c, :], c == 0, c == 1)
                                  for n in range(4) for c in range(2)]))

            @block.vector
            def _(dve):
                dve.sem_inc(spread_used, 2)
                dve.sem_inc(scan_done, 2)
                dve.wait_ge(consts_loaded, 16 * 9)
                dve.tensor_copy(sel[:], self_s[:]).then_inc(sel_ready, 1)
                for r in range(2):
                    for c in range(2):
                        for k in range(4):
                            ins = dve.tensor_scalar(diag[:, r, c, k, :], ident[:], cw(r, c, k), None, ALU.mult)
                ins.then_inc(diag_ready, 1)
                dve.wait_ge(negA_ready, 2)
                for r in range(2):
                    dve.tensor_scalar(negA[:, r, :], negA[:, r, :], -1.0, None, ALU.mult).then_inc(negA_ready, 1)
                dve.wait_ge(sel_ready, 1)
                with dve.Fori(0, NPAIR) as i:
                    done = [0]

                    def link(ins):
                        done[0] += 1
                        ins.then_inc(dve_step, 1)
                        dve.wait_ge(dve_step, done[0])

                    dve.wait_ge(job_evicted, i * JOBS + XL + JOBS)
                    link(dve.tensor_reduce(stat[:, 0, :].rearrange("p (s c) -> p c s", s=2),
                                           sz[:].rearrange("p c (s l) -> p c s l", s=2), AX.X, ALU.max))
                    link(dve.tensor_tensor(stat[:, 1, :], stat[:, 0, :], stat[:, 0, :], ALU.mult))
                    link(dve.tensor_scalar(stat[:, 1, :], stat[:, 1, :], 1.0 / (DI * L) ** 2, None, ALU.mult))
                    for r in range(2):
                        dve.wait_ge(bc_copied, i * 2 + r + 1)
                        dve.wait_ge(job_evicted, i * JOBS + DIR + 4 * r + 2 + JOBS)
                        link(dve.tensor_tensor(bcr[:], bc32[:], bcs[:, r, :], ALU.subtract))
                        link(dve.tensor_copy(bcs[64:96, r, :], bcr[64:96, :]))
                        link(dve.tensor_copy(bcq[32:64, :], bcr[32:64, :]))
                        dve.tensor_tensor(bcs[32:64, r, :], bcr[32:64, :], bcq[32:64, :], ALU.subtract).then_inc(bcs_ready, 1)
                    for r in range(2):
                        dve.wait_ge(dx_ready, i * 4 + 2 * r + 2)
                        for hf in range(2):
                            s0 = r * 16 + hf * 8
                            for j in range(4):
                                dve.wait_ge(spread, i * slots + s0 + j + 1)
                                for c in range(2):
                                    ins = dve.tensor_tensor(h[:, c, 2 * j:2 * j + 2, :], psR[:, j % 2, :].rearrange("p (n l) -> p n l", n=2),
                                                            dx[:, r, c, :].unsqueeze(1).broadcast_to([P, 2, ROW]), ALU.mult)
                                    if c == 0:
                                        link(ins)
                                ins.then_inc(spread_used, 1)
                                if j % 2 == 1:
                                    dve.wait_ge(spread_used, i * slots + s0 + j + 1 + 2)
                                    for c in range(2):
                                        e = r * 8 + hf * 4 + (j // 2) * 2 + c
                                        dve.wait_ge(exp_ready, i * 16 + e + 1)
                                        hq = h[:, c, 2 * j - 2:2 * j + 2, :].rearrange("p n l -> p (n l)")
                                        dve.tensor_tensor_scan(hq, dA[:, e % 2].rearrange("p n s l -> p (n s l)"), hq, 0.0,
                                                               ALU.mult, ALU.add).then_inc(scan_done, 1)
                            dve.wait_ge(scan_done, i * 16 + r * 8 + hf * 4 + 4 + 2)
                            for j in range(4):
                                dve.wait_ge(spread, i * slots + s0 + 4 + j + 1)
                                for c in range(2):
                                    hj = h[:, c, 2 * j:2 * j + 2, :]
                                    ins = dve.tensor_tensor(hj, psR[:, j % 2, :].rearrange("p (n l) -> p n l", n=2), hj, ALU.mult)
                                    if c == 0:
                                        link(ins)
                                ins.then_inc(spread_used, 1)
                            dve.wait_ge(spread_used, i * slots + s0 + 8 + 2)
                            for c in range(2):
                                hs = h[:, c].rearrange("p n l -> p l n")
                                if hf == 0:
                                    if r == 0 and c == 0:
                                        dve.wait_ge(out_ready, i)
                                    link(dve.tensor_reduce(y[:, r, c, :], hs, AX.X, ALU.add))
                                else:
                                    link(dve.tensor_reduce(ypart[:], hs, AX.X, ALU.add))
                                    link(dve.tensor_tensor(y[:, r, c, :], y[:, r, c, :], ypart[:], ALU.add))
                                    link(dve.scalar_tensor_tensor(y[:, r, c, :], u[:, r, c, :], dskip(r, c), y[:, r, c, :], ALU.mult, ALU.add))
                    dve.wait_ge(job_evicted, i * JOBS + JOBS + JOBS)
                    dve.tensor_tensor(V, Z[:, :, 0, :], Z[:, :, 1, :], ALU.add).then_inc(mod2_ready, 1)
                    dve.wait_ge(mod_ready, i + 1)
                    link(dve.tensor_reduce(stat[:, 2, :], V, AX.X, ALU.add))
                    link(dve.tensor_scalar(stat[:, 2, :], stat[:, 2, :], 1.0 / L, None, ALU.mult))
                    link(dve.tensor_tensor(V, V, bcast(stat[:, 2, :], L), ALU.subtract))
                    sq = h[:, 0, 0:2, :].rearrange("p n (s l) -> p (n s) l", s=2)
                    link(dve.tensor_tensor(sq, V, V, ALU.mult))
                    link(dve.tensor_reduce(stat[:, 3, :], sq, AX.X, ALU.add))
                    dve.tensor_scalar(stat[:, 4, :], stat[:, 3, :], 1.0 / L, EPS, ALU.mult, ALU.add).then_inc(var_ready, 1)
                    for c in range(2):
                        y0 = y[:, 0, c, :].rearrange("p (s l) -> p s l", s=2)
                        y1 = y[:, 1, c, :].rearrange("p (s l) -> p s l", s=2)
                        link(dve.tensor_tensor(y0, y0, y1[:, :, ::-1], ALU.add))
                    link(dve.tensor_tensor(y[:, 0], y[:, 0], sz[:], ALU.mult))
                    dve.wait_ge(std_ready, i + 1)
                    link(dve.reciprocal(stat[:, 6, :], stat[:, 5, :]))
                    link(dve.tensor_tensor(V, V, bcast(stat[:, 6, :], L), ALU.mult))
                    dve.tensor_tensor(y[:, 0].rearrange("p c (s l) -> p s c l", s=2), y[:, 0].rearrange("p c (s l) -> p s c l", s=2),
                                      V.rearrange("p (s c) l -> p s c l", s=2), ALU.add).then_inc(y_ready, 1)
                    dve.wait_ge(out_ready, i + 1)
                    dve.wait_ge(xtok_loaded, 16 * i + 16)
                    dve.tensor_tensor(xtok[:].rearrange("p n d -> p (n d)"), xtok[:].rearrange("p n d -> p (n d)"),
                                      psG[:, OUT % 4, :], ALU.add).then_inc(res_ready, 1)
                    dve.sem_clear(dve_step)
def moe_route(nc, xn_dram, xnT_dram, slots_dram, wr, br, iota8, lower_in, pos, gate):
    G = 4
    with ExitStack() as ctx:
        sb, ps, sem = makers(nc, ctx, "r")
        xT = sb("xT", [P, NTOK])
        wr_s, br_s, iota = sb("wr", [P, NE]), sb("br", [P, NE]), sb("iota", [P, NE])
        lower, ones = sb("lower", [P, P]), sb("ones", [P, P])
        lg, oh, key = sb("lg", [P, NT, NE]), sb("oh", [P, 2, NT, NE]), sb("key", [P, NT, NE])
        t, t2, gt, base = sb("t", [P, NT, NE]), sb("t2", [P, NT, NE]), sb("gt", [P, NT, NE]), sb("base", [P, NT, NE])
        m, w = sb("m", [P, 3, NT]), sb("w", [P, 3, NT])
        kept, dest = sb("kept", [P, 2, NT]), sb("dest", [P, 2, NT])
        bit, thr, cand, acc = sb("bit", [P, NE], I32), sb("thr", [P, NE], I32), sb("cand", [P, NE], I32), sb("acc", [P, NE], I32)
        cnt, need, first = sb("cnt", [P, NE]), sb("need", [P, NE]), sb("first", [P, NE])
        zeros = sb("zeros", [P, NSLOT // P * DM])
        xbuf, ibuf = sb("xbuf", [P, 2, G, DM]), sb("ibuf", [P, 2, 2, G], I32)
        psL, psC, psA = ps("psL", [P, NT, NE]), ps("psC", [P, NE]), ps("psA", [P, 2, 256])
        loaded, const_ready = sem("loaded"), sem("const_ready")
        logits_ready, diff_ready, exp_ready = sem("logits_ready"), sem("diff_ready"), sem("exp_ready")
        count_ready, count_summed = sem("count_ready"), sem("count_summed")
        mask_ready, mask_summed = sem("mask_ready"), sem("mask_summed")
        slots_zeroed, index_ready, row_loaded, scattered = sem("slots_zeroed"), sem("index_ready"), [sem("row_loaded0"), sem("row_loaded1")], [sem("scattered0"), sem("scattered1")]
        step_done, scatter_begun = sem("step_done"), sem("scatter_begun")
        flat = lambda a: a.rearrange("p n e -> p (n e)")
        over_n = lambda a: a.unsqueeze(1).broadcast_to([P, NT, NE])
        by_e = lambda a: a.rearrange("p n e -> p e n")
        with nc.Block() as block:
            @block.sync
            def _(sp):
                for dst, src in ((wr_s[:], wr), (br_s[:], br.rearrange("(o e) -> o e", o=1).broadcast_to([P, NE])),
                                 (iota[:], iota8.rearrange("(o e) -> o e", o=1).broadcast_to([P, NE])), (lower[:], lower_in), (xT[:], xnT_dram)):
                    sp.dma_start(dst, src).then_inc(loaded, 16)
                sp.wait_ge(const_ready, 3)
                sp.dma_start(slots_dram.rearrange("(p n) d -> p (n d)", p=P), zeros[:]).then_inc(slots_zeroed, 16)
                with sp.Fori(0, NT // (2 * G)) as i:
                    for b in range(2):
                        sp.wait_ge(scattered[b], i * (2 * G * 16))
                        sp.dma_start(xbuf[:, b], xn_dram.rearrange("(i b n p) d -> i b p n d", p=P, n=G, b=2)[bass.ds(i, 1)].rearrange("i b p n d -> b p (i n) d")[b]).then_inc(row_loaded[b], 16)

            @block.tensor
            def _(pe):
                pe.wait_ge(loaded, 5 * 16)
                for n in range(NT):
                    mm = pe.matmul(psL[:, n, :], lhsT=xT[:, n * P:(n + 1) * P], rhs=wr_s[:], start=True, stop=True)
                mm.then_inc(logits_ready, 1)
                pe.wait_ge(const_ready, 3)
                with pe.Fori(0, 31) as i:
                    pe.wait_ge(count_ready, i + 1)
                    pe.matmul(psC[:], lhsT=ones[:], rhs=cnt[:], start=True, stop=True).then_inc(count_summed, 1)
                for k, mask in enumerate((t, t)):
                    pe.wait_ge(mask_ready, k + 1)
                    pe.matmul(psA[:, 0, :], lhsT=lower[:], rhs=flat(mask[:]), start=True, stop=True)
                    pe.matmul(psA[:, 1, :], lhsT=ones[:], rhs=flat(mask[:]), start=True, stop=True).then_inc(mask_summed, 1)

            @block.scalar
            def _(act):
                act.wait_ge(diff_ready, 1)
                act.activation(w[:, 1, :], m[:, 2, :], ACT.Exp).then_inc(exp_ready, 1)

            @block.gpsimd
            def _(pool):
                pool.memset(zeros[:], 0.0).then_inc(const_ready, 1)
                pool.memset(ones[:], 1.0).then_inc(const_ready, 1)
                pool.memset(bit[:], 1 << 29).then_inc(const_ready, 1)
                pool.wait_ge(slots_zeroed, 16)
                with pool.Fori(0, NT // (2 * G)) as i:
                    for b in range(2):
                        pool.wait_ge(index_ready, i * 2 + b + 1)
                        pool.wait_ge(row_loaded[b], i * 16 + 16)
                        pool.sem_inc(scatter_begun, 1)
                        for n in range(G):
                            for k in range(2):
                                pool.indirect_dma_start(slots_dram, bass.IndirectOffsetOnAxis(ap=ibuf[:, b, k, n:n + 1], axis=0),
                                                        xbuf[:, b, n, :], None, bounds_check=NSLOT - 1, oob_is_err=False).then_inc(scattered[b], 16)
                for b in range(2):
                    pool.wait_ge(scattered[b], NT * 16)

            @block.vector
            def _(dve):
                done = [0]

                def link(ins):
                    done[0] += 1
                    ins.then_inc(step_done, 1)
                    dve.wait_ge(step_done, done[0])

                dve.wait_ge(loaded, 5 * 16)
                dve.wait_ge(logits_ready, 1)
                link(dve.memset(thr[:], 0))
                link(dve.tensor_tensor(lg[:], psL[:], over_n(br_s[:]), ALU.add))
                for k in range(2):
                    link(dve.tensor_reduce(m[:, k, :], lg[:], AX.X, ALU.max))
                    link(dve.tensor_tensor(t[:], lg[:], bcast(m[:, k, :], NE), ALU.not_equal))
                    link(dve.scalar_tensor_tensor(t[:], t[:], float(NE), over_n(iota[:]), ALU.mult, ALU.add))
                    link(dve.tensor_reduce(m[:, 2, :], t[:], AX.X, ALU.min))
                    link(dve.tensor_tensor(oh[:, k], over_n(iota[:]), bcast(m[:, 2, :], NE), ALU.is_equal))
                    if k == 0:
                        link(dve.scalar_tensor_tensor(lg[:], oh[:, 0], -3e38, lg[:], ALU.mult, ALU.add))
                dve.tensor_tensor(m[:, 2, :], m[:, 1, :], m[:, 0, :], ALU.subtract).then_inc(diff_ready, 1)
                dve.wait_ge(exp_ready, 1)
                link(dve.tensor_scalar(w[:, 2, :], w[:, 1, :], 1.0, None, ALU.add))
                link(dve.reciprocal(w[:, 0, :], w[:, 2, :]))
                link(dve.tensor_tensor(w[:, 1, :], w[:, 1, :], w[:, 0, :], ALU.mult))
                link(dve.tensor_tensor(key[:], oh[:, 0], bcast(w[:, 0, :], NE), ALU.mult))
                link(dve.tensor_tensor(t[:], oh[:, 1], bcast(w[:, 1, :], NE), ALU.mult))
                link(dve.tensor_tensor(key[:], key[:], t[:], ALU.add))
                link(dve.tensor_tensor(t[:], oh[:, 0], oh[:, 1], ALU.add))
                link(dve.scalar_tensor_tensor(key[:], t[:], -1.0, key[:], ALU.add, ALU.add))
                dve.wait_ge(const_ready, 3)
                dve.sem_clear(step_done)
                with dve.Fori(0, 30) as i:
                    done[0] = 0
                    link(dve.tensor_tensor(cand[:], thr[:], bit[:], ALU.bitwise_or))
                    link(dve.tensor_tensor(t[:], key[:], over_n(cand[:].bitcast(F32)), ALU.is_ge))
                    dve.tensor_reduce(cnt[:], by_e(t[:]), AX.X, ALU.add).then_inc(count_ready, 1)
                    dve.wait_ge(count_summed, i + 1)
                    link(dve.tensor_scalar(acc[:], psC[:], float(CAP), -1.0, ALU.is_ge, ALU.mult))
                    link(dve.tensor_tensor(acc[:], acc[:], bit[:], ALU.bitwise_and))
                    link(dve.tensor_tensor(thr[:], thr[:], acc[:], ALU.bitwise_or))
                    link(dve.tensor_scalar(bit[:], bit[:], 1, None, ALU.logical_shift_right))
                    dve.sem_clear(step_done)
                done[0] = 0
                thrf = over_n(thr[:].bitcast(F32))
                link(dve.tensor_tensor(gt[:], key[:], thrf, ALU.is_gt))
                dve.tensor_reduce(cnt[:], by_e(gt[:]), AX.X, ALU.add).then_inc(count_ready, 1)
                dve.wait_ge(count_summed, 31)
                link(dve.tensor_scalar(need[:], psC[:], -1.0, float(CAP), ALU.mult, ALU.add))
                dve.tensor_tensor(t[:], key[:], thrf, ALU.is_equal).then_inc(mask_ready, 1)

                def rank(k):
                    dve.wait_ge(mask_summed, k + 1)
                    link(dve.tensor_copy(flat(t2[:]), psA[:, 1, :]))
                    for e in range(NE):
                        link(dve.tensor_tensor_scan(base[:, :, e], ones[:, 0:NT], t2[:, :, e], 0.0, ALU.mult, ALU.add))
                    link(dve.tensor_tensor(base[:], base[:], t2[:], ALU.subtract))
                    link(dve.tensor_tensor(flat(base[:]), flat(base[:]), psA[:, 0, :], ALU.add))

                rank(0)
                link(dve.tensor_tensor(base[:], base[:], over_n(need[:]), ALU.is_lt))
                link(dve.tensor_tensor(t[:], t[:], base[:], ALU.mult))
                dve.tensor_tensor(t[:], t[:], gt[:], ALU.add).then_inc(mask_ready, 1)
                link(dve.tensor_scalar(first[:], iota[:], float(CAP), None, ALU.mult))
                rank(1)
                link(dve.tensor_tensor(base[:], base[:], over_n(first[:]), ALU.add))
                for k in range(2):
                    link(dve.tensor_tensor(t2[:], oh[:, k], t[:], ALU.mult))
                    link(dve.tensor_reduce(kept[:, k, :], t2[:], AX.X, ALU.add))
                    link(dve.tensor_tensor(t2[:], t2[:], base[:], ALU.mult))
                    link(dve.tensor_reduce(dest[:, k, :], t2[:], AX.X, ALU.add))
                    link(dve.tensor_tensor(gate[:, k, :], w[:, k, :], kept[:, k, :], ALU.mult))
                link(dve.tensor_scalar(kept[:], kept[:], -float(NSLOT), float(NSLOT), ALU.mult, ALU.add))
                link(dve.tensor_tensor(pos[:], dest[:], kept[:], ALU.add))
                dve.sem_clear(step_done)
                with dve.Fori(0, NT // (2 * G)) as i:
                    for b in range(2):
                        dve.wait_ge(scattered[b], i * (2 * G * 16))
                        dve.tensor_copy(ibuf[:, b], pos[:, :, bass.ds(i * (2 * G) + b * G, G)]).then_inc(index_ready, 1)


def moe_experts(nc, slots_dram, y_dram, w1, b1, w2, b2, ident_in):
    NS, HC = CAP // P, CAP // 2
    with ExitStack() as ctx:
        sb, ps, sem = makers(nc, ctx, "e")
        ident = sb("ident", [P, P])
        xs, xT = sb("xs", [P, 2, NS, DM]), sb("xT", [P, CAP])
        w1s, w2s = sb("w1", [P, 2, FF]), sb("w2", [P, 2, FF // P, DM])
        b1s, b2s = sb("b1", [P, 2, FF // P]), sb("b2", [P, 2, DM])
        hT, ys = sb("hT", [P, FF // P, CAP]), sb("ys", [P, 2, NS, DM])
        psT, psH, psY = ps("psT", [P, 2, 512]), ps("psH", [P, 4, 512]), ps("psY", [P, 2, 512])
        ident_loaded, loaded = sem("ident_loaded"), [sem("loaded0"), sem("loaded1")]
        turned, turned_out = sem("turned"), sem("turned_out")
        h_ready, gelu_ready, y_summed, y_ready = sem("h_ready"), sem("gelu_ready"), sem("y_summed"), sem("y_ready")
        stored = [sem("stored0"), sem("stored1")]
        at = lambda n: (n // 4 if n < 4 else 1, (n % 4) * P)
        with nc.Block() as block:
            @block.sync
            def _(sp):
                sp.dma_start(ident[:], ident_in).then_inc(ident_loaded, 16)
                with sp.Fori(0, NE // 2) as i:
                    for b in range(2):
                        sp.wait_ge(y_summed, i * 2 + b)
                        one = lambda a: a.rearrange("(i b) ... -> i b ...", b=2)[bass.ds(i, 1)]
                        sp.dma_start(xs[:, b], slots_dram.rearrange("(i b n p) d -> i b p n d", b=2, n=NS, p=P)[bass.ds(i, 1)].rearrange("i b p n d -> b p (i n) d")[b]).then_inc(loaded[b], 16)
                        sp.dma_start(w1s[:, b], w1.rearrange("(i b) p f -> i b p f", b=2)[bass.ds(i, 1)].rearrange("i b p f -> b p (i f)")[b]).then_inc(loaded[b], 16)
                        sp.dma_start(w2s[:, b], w2.rearrange("(i b) (c p) f -> i b p c f", b=2, p=P)[bass.ds(i, 1)].rearrange("i b p c f -> b p (i c) f")[b]).then_inc(loaded[b], 16)
                        sp.dma_start(b1s[:, b], b1.rearrange("(i b) p c -> i b p c", b=2)[bass.ds(i, 1)].rearrange("i b p c -> b p (i c)")[b]).then_inc(loaded[b], 16)
                        sp.dma_start(b2s[:, b], b2.rearrange("(i b) f -> i b f", b=2)[bass.ds(i, 1)].rearrange("i b f -> b i f")[b].broadcast_to([P, DM])).then_inc(loaded[b], 16)

            @block.tensor
            def _(pe):
                pe.wait_ge(ident_loaded, 16)
                with pe.Fori(0, NE // 2) as i:
                    for b in range(2):
                        pe.wait_ge(loaded[b], i * 80 + 80)
                        pe.wait_ge(turned_out, (i * 2 + b) * 2)
                        for n in range(NS):
                            g, c = n // 4, n % 4 * P
                            mm = pe.transpose(psT[:, g, c:c + P], xs[:, b, n, :], ident[:])
                        mm.then_inc(turned, 1)
                        pe.wait_ge(turned_out, (i * 2 + b) * 2 + 2)
                        for f in range(FF // P):
                            for q in range(2):
                                k = 2 * f + q
                                pe.wait_ge(gelu_ready, (i * 2 + b) * 8 + k + 1)
                                pe.matmul(psH[:, k % 4, 0:HC], lhsT=w1s[:, b, f * P:(f + 1) * P], rhs=xT[:, q * HC:(q + 1) * HC],
                                          start=True, stop=True).then_inc(h_ready, 1)
                        pe.wait_ge(gelu_ready, (i * 2 + b) * 8 + 8 + 4)
                        pe.wait_ge(y_ready, (i * 2 + b) * 2)
                        for n in range(NS):
                            g, c = n // 4, n % 4 * P
                            for f in range(FF // P):
                                mm = pe.matmul(psY[:, g, c:c + P], lhsT=hT[:, f, n * P:(n + 1) * P], rhs=w2s[:, b, f, :],
                                               start=f == 0, stop=f == FF // P - 1)
                        mm.then_inc(y_summed, 1)

            @block.scalar
            def _(act):
                act.sem_inc(gelu_ready, 4)
                with act.Fori(0, NE // 2) as i:
                    for b in range(2):
                        act.wait_ge(turned, i * 2 + b + 1)
                        act.activation(xT[:, 0:512], psT[:, 0, :], ACT.Copy).then_inc(turned_out, 1)
                        act.activation(xT[:, 512:CAP], psT[:, 1, 0:CAP - 512], ACT.Copy).then_inc(turned_out, 1)
                        act.wait_ge(y_summed, i * 2 + b)
                        for f in range(FF // P):
                            for q in range(2):
                                k = 2 * f + q
                                act.wait_ge(h_ready, (i * 2 + b) * 8 + k + 1)
                                act.activation(hT[:, f, q * HC:(q + 1) * HC], psH[:, k % 4, 0:HC], ACT.Gelu,
                                               bias=b1s[:, b, f:f + 1]).then_inc(gelu_ready, 1)

            @block.vector
            def _(dve):
                with dve.Fori(0, NE // 2) as i:
                    for b in range(2):
                        dve.wait_ge(y_summed, i * 2 + b + 1)
                        dve.wait_ge(stored[b], i * 16)
                        dve.tensor_tensor(ys[:, b, 0:4, :], psY[:, 0, :].rearrange("p (n d) -> p n d", n=4),
                                          b2s[:, b, :].unsqueeze(1).broadcast_to([P, 4, DM]), ALU.add).then_inc(y_ready, 1)
                        dve.tensor_tensor(ys[:, b, 4, :], psY[:, 1, 0:P], b2s[:, b, :], ALU.add).then_inc(y_ready, 1)

            @block.gpsimd
            def _(pool):
                with pool.Fori(0, NE // 2) as i:
                    for b in range(2):
                        pool.wait_ge(y_ready, (i * 2 + b) * 2 + 2)
                        pool.dma_start(y_dram.rearrange("(i b n p) d -> i b p n d", b=2, n=NS, p=P)[bass.ds(i, 1)].rearrange("i b p n d -> b p (i n) d")[b], ys[:, b]).then_inc(stored[b], 16)
                for b in range(2):
                    pool.wait_ge(stored[b], 16 * (NE // 2))


def moe_combine(nc, xn_dram, y_dram, x1_dram, x1_out, xn2_dram, xn2T_dram, gamma, beta, ident_in, pos, gate):
    G = 4
    with ExitStack() as ctx:
        sb, ps, sem = makers(nc, ctx, "c")
        F_, X1, SQ = sb("F", [P, NT, DM]), sb("X1", [P, NT, DM]), sb("SQ", [P, NT, DM])
        XT = sb("XT", [P, NTOK])
        gam, bet, ident = sb("gam", [P, DM]), sb("bet", [P, DM]), sb("ident", [P, P])
        yb, ib = sb("yb", [P, 2, 2, G, DM]), sb("ib", [P, 2, 2, G], I32)
        posg = sb("posg", [P, 2, NT], I32)
        gz = sb("gz", [P, 2, NT])
        stat = sb("stat", [P, 4, NT])
        psT = ps("psT", [P, 4, 512])
        loaded, index_ready, gathered, used = sem("loaded"), sem("index_ready"), [sem("gathered0"), sem("gathered1")], sem("used")
        var_ready, std_ready, xn_ready, x1_ready = sem("var_ready"), sem("std_ready"), sem("xn_ready"), sem("x1_ready")
        turned, evicted, stored, step_done = sem("turned"), sem("evicted"), sem("stored"), sem("step_done")
        gather_begun = sem("gather_begun")
        tok = lambda a: a.rearrange("(n p) d -> p n d", p=P)
        row = lambda a: a.rearrange("(o d) -> o d", o=1).broadcast_to([P, DM])
        with nc.Block() as block:
            @block.sync
            def _(sp):
                for dst, src in ((F_[:], tok(xn_dram)), (X1[:], tok(x1_dram)), (gam[:], row(gamma)), (bet[:], row(beta)), (ident[:], ident_in)):
                    sp.dma_start(dst, src).then_inc(loaded, 16)
                sp.wait_ge(x1_ready, 1)
                sp.dma_start(tok(x1_out), X1[:]).then_inc(stored, 16)
                sp.wait_ge(xn_ready, 1)
                sp.dma_start(tok(xn2_dram), F_[:]).then_inc(stored, 16)
                sp.wait_ge(evicted, NT // 4)
                sp.dma_start(xn2T_dram, XT[:]).then_inc(stored, 16)
                sp.wait_ge(stored, 48)

            @block.gpsimd
            def _(pool):
                with pool.Fori(0, NT // (2 * G)) as i:
                    for b in range(2):
                        pool.wait_ge(index_ready, i * 2 + b + 1)
                        pool.sem_inc(gather_begun, 1)
                        for n in range(G):
                            for k in range(2):
                                pool.indirect_dma_start(yb[:, b, k, n, :], None, y_dram, bass.IndirectOffsetOnAxis(ap=ib[:, b, k, n:n + 1], axis=0)).then_inc(gathered[b], 16)

            @block.vector
            def _(dve):
                done = [0]

                def link(ins):
                    done[0] += 1
                    ins.then_inc(step_done, 1)
                    dve.wait_ge(step_done, done[0])

                link(dve.tensor_scalar(gz[:], pos[:], float(NSLOT), None, ALU.is_lt))
                link(dve.tensor_tensor(posg[:], pos[:], gz[:], ALU.mult))
                dve.wait_ge(loaded, 16 * 5)
                dve.sem_clear(step_done)
                for b in range(2):
                    dve.tensor_copy(ib[:, b], posg[:, :, b * G:(b + 1) * G]).then_inc(index_ready, 1)
                with dve.Fori(0, NT // (2 * G)) as i:
                    done[0] = 0
                    for b in range(2):
                        dve.wait_ge(gathered[b], i * (2 * G * 16) + 2 * G * 16)
                        fs = F_[:, bass.ds(i * (2 * G) + b * G, G), :]
                        for k in range(2):
                            g = gate[:, k, bass.ds(i * (2 * G) + b * G, G)].unsqueeze(2).broadcast_to([P, G, DM])
                            link(dve.tensor_tensor(yb[:, b, k], yb[:, b, k], g, ALU.mult))
                            link(dve.tensor_tensor(fs, fs, yb[:, b, k], ALU.add))
                        dve.tensor_copy(ib[:, b], posg[:, :, bass.ds((i * (2 * G) + b * G + 2 * G) % NT, G)]).then_inc(index_ready, 1)
                    dve.sem_clear(step_done)
                done[0] = 0

                def norm(v, k):
                    link(dve.tensor_reduce(stat[:, 0, :], v, AX.X, ALU.add))
                    link(dve.tensor_scalar(stat[:, 0, :], stat[:, 0, :], 1.0 / DM, None, ALU.mult))
                    link(dve.tensor_tensor(v, v, bcast(stat[:, 0, :], DM), ALU.subtract))
                    link(dve.tensor_tensor(SQ[:], v, v, ALU.mult))
                    link(dve.tensor_reduce(stat[:, 1, :], SQ[:], AX.X, ALU.add))
                    dve.tensor_scalar(stat[:, 1, :], stat[:, 1, :], 1.0 / DM, EPS, ALU.mult, ALU.add).then_inc(var_ready, 1)
                    dve.wait_ge(std_ready, k)
                    link(dve.reciprocal(stat[:, 3, :], stat[:, 2, :]))
                    return dve.tensor_tensor(v, v, bcast(stat[:, 3, :], DM), ALU.mult)

                link(norm(F_[:], 1))
                link(dve.tensor_tensor(F_[:], F_[:], gam[:].unsqueeze(1).broadcast_to([P, NT, DM]), ALU.mult))
                link(dve.tensor_tensor(F_[:], F_[:], bet[:].unsqueeze(1).broadcast_to([P, NT, DM]), ALU.add))
                dve.tensor_tensor(X1[:], X1[:], F_[:], ALU.add).then_inc(x1_ready, 1)
                dve.wait_ge(x1_ready, 1)
                link(dve.tensor_copy(F_[:], X1[:]))
                norm(F_[:], 2).then_inc(xn_ready, 1)

            @block.scalar
            def _(act):
                for k in range(2):
                    act.wait_ge(var_ready, k + 1)
                    act.activation(stat[:, 2, :], stat[:, 1, :], ACT.Sqrt).then_inc(std_ready, 1)
                for g in range(NT // 4):
                    act.wait_ge(turned, g + 1)
                    act.activation(XT[:, g * 512:(g + 1) * 512], psT[:, g % 4, :], ACT.Copy).then_inc(evicted, 1)

            @block.tensor
            def _(pe):
                pe.wait_ge(loaded, 16 * 5)
                pe.wait_ge(xn_ready, 1)
                for g in range(NT // 4):
                    if g >= 4:
                        pe.wait_ge(evicted, g - 3)
                    for k in range(4):
                        mm = pe.transpose(psT[:, g % 4, k * P:(k + 1) * P], F_[:, 4 * g + k, :], ident[:])
                    mm.then_inc(turned, 1)
def delta_attention(nc, xn2_dram, xn2T_dram, x1_dram, x2_dram, wqkv, wb, cw_in, wo, grms, lng, lnb, ident_in, levels_in, masks_in):
    NPAIR = B // 2
    ROW = 2 * L
    with ExitStack() as ctx:
        sb, ps, sem = makers(nc, ctx, "a")
        wqkv_s, wb_s, cw, wo_s = sb("wqkv", [P, 3, P]), sb("wb", [P, AH]), sb("cw", [P, 3, 4]), sb("wo", [P, P])
        grms_s, lng_s, lnb_s, ident = sb("grms", [P, AD]), sb("lng", [P, DM]), sb("lnb", [P, DM]), sb("ident", [P, P])
        lev = sb("lev", [P, 2, NLEV, P])
        masks = sb("masks", [P, 2, P])
        xT, xtok, x1 = sb("xT", [P, ROW]), sb("xtok", [P, 4, DM]), sb("x1", [P, 4, DM])
        pad, qkv = sb("pad", [P, 3, 2, 3 + L]), sb("qkv", [P, 3, ROW])
        diag = sb("diag", [P, 3, 4, P])
        beta = sb("beta", [P, 4, AH])
        tok = sb("tok", [P, 4, 4, P])
        sq, ss = sb("sq", [P, 4, 2, P]), sb("ss", [P, 4, 2, AH])
        fm = sb("fm", [P, 4, 3, P])
        bd = sb("bd", [P, 4, 3, AH, P])
        M, X, XT, QT = (sb(n, [P, 2, AH, P]) for n in ("M", "X", "XT", "QT"))
        T1, PT = sb("T1", [P, 2, 2, AH, P]), sb("PT", [P, 2, AH, P])
        R, D, S = sb("R", [P, 2, P]), sb("D", [P, 2, P]), sb("S", [P, 2, P])
        o, oT, osq = sb("o", [P, 4, P]), sb("oT", [P, 4, P]), sb("osq", [P, 4, P])
        rs, st = sb("rs", [P, 2, 16]), sb("st", [P, 4, 4])
        bank = ps("bank", [P, 8, 512])
        consts_loaded, pads_zeroed, xT_loaded, xtok_loaded, x1_loaded, stored = (sem(n) for n in (
            "consts_loaded", "pads_zeroed", "xT_loaded", "xtok_loaded", "x1_loaded", "stored"))
        proj_ready, proj_out, beta_ready, beta_out = sem("proj_ready"), sem("proj_out"), sem("beta_ready"), sem("beta_out")
        diag_ready, dw_ready, silu_ready, tok_ready, tok_out = sem("diag_ready"), sem("dw_ready"), sem("silu_ready"), sem("tok_ready"), sem("tok_out")
        norm_sq, norm_root, keys_ready, fm_ready, fm_out, bd_out = (sem(n) for n in (
            "norm_sq", "norm_root", "keys_ready", "fm_ready", "fm_out", "bd_out"))
        gram_ready, m_out, x_ready, q_ready, q_out, xx_ready = (sem(n) for n in (
            "gram_ready", "m_out", "x_ready", "q_ready", "q_out", "xx_ready"))
        ks_ready, r_ready, d_ready, d_out, o_ready, o_out, s_ready, s_out = (sem(n) for n in (
            "ks_ready", "r_ready", "d_ready", "d_out", "o_ready", "o_out", "s_ready", "s_out"))
        rms_sq, rms_root, on_ready, oT_ready, oT_out, y_ready, y_out = (sem(n) for n in (
            "rms_sq", "rms_root", "on_ready", "oT_ready", "oT_out", "y_ready", "y_out"))
        var_ready, std_ready, x2_ready, step_done = sem("var_ready"), sem("std_ready"), sem("x2_ready"), sem("step_done")
        NL = NLEV - 1
        row = lambda a: a.rearrange("(o d) -> o d", o=1)
        pair = lambda a, i: a.rearrange("(i n p) d -> i p n d", p=P, n=4)[bass.ds(i, 1)].rearrange("i p n d -> p (i n) d")
        A, Bk, Cb = (0, 4), (1, 5), (2, 6)
        with nc.Block() as block:
            @block.sync
            def _(sp):
                for dst, src in ((wqkv_s[:], wqkv), (wb_s[:], wb), (cw[:], cw_in), (wo_s[:], wo), (ident[:], ident_in),
                                 (grms_s[:], row(grms).broadcast_to([P, AD])), (lng_s[:], row(lng).broadcast_to([P, DM])),
                                 (lnb_s[:], row(lnb).broadcast_to([P, DM])), (lev[:], levels_in), (masks[:], masks_in)):
                    sp.dma_start(dst, src).then_inc(consts_loaded, 16)
                with sp.Fori(0, NPAIR) as i:
                    sp.wait_ge(beta_ready, i)
                    sp.dma_start(xT[:], xn2T_dram[:, bass.ds(i * ROW, ROW)]).then_inc(xT_loaded, 16)
                    sp.wait_ge(x2_ready, i)
                    sp.dma_start(xtok[:], pair(xn2_dram, i)).then_inc(xtok_loaded, 16)
                    sp.wait_ge(stored, 16 * i)
                    sp.dma_start(x1[:], pair(x1_dram, i)).then_inc(x1_loaded, 16)
                    sp.wait_ge(x2_ready, i + 1)
                    sp.dma_start(pair(x2_dram, i), x1[:]).then_inc(stored, 16)
                sp.wait_ge(stored, 16 * NPAIR)

            @block.tensor
            def _(pe):
                pe.wait_ge(consts_loaded, 160)
                pe.wait_ge(diag_ready, 1)
                pe.wait_ge(pads_zeroed, 1)
                with pe.Fori(0, NPAIR) as i:
                    pe.wait_ge(xT_loaded, 16 * i + 16)
                    pe.wait_ge(o_out, 4 * i)
                    pe.wait_ge(s_out, 2 * i)
                    for j in range(3):
                        pe.matmul(bank[:, j, :], lhsT=wqkv_s[:, j, :], rhs=xT[:], start=True, stop=True).then_inc(proj_ready, 1)
                    pe.wait_ge(oT_out, i)
                    for n in range(4):
                        mm = pe.matmul(bank[:, 3, n * AH:(n + 1) * AH], lhsT=xT[:, n * P:(n + 1) * P], rhs=wb_s[:], start=True, stop=True)
                    mm.then_inc(beta_ready, 1)
                    pe.wait_ge(y_out, i)
                    for j in range(3):
                        pe.wait_ge(proj_out, 3 * i + j + 1)
                        for k in range(4):
                            mm = pe.matmul(bank[:, 4 + j, :], lhsT=diag[:, j, k, :], rhs=pad[:, j, :, k:k + L], start=k == 0, stop=k == 3)
                        mm.then_inc(dw_ready, 1)
                    pe.wait_ge(silu_ready, 3 * i + 3)
                    for n in range(4):
                        for j in range(3):
                            mm = pe.transpose(bank[:, 4 + n, j * P:(j + 1) * P], qkv[:, j, n * P:(n + 1) * P], ident[:])
                        mm.then_inc(tok_ready, 1)
                    pe.wait_ge(keys_ready, i + 1)
                    pe.wait_ge(beta_out, i + 1)
                    for n in range(4):
                        for j, src in enumerate((0, 1, 3)):
                            mm = pe.transpose(bank[:, n, j * P:(j + 1) * P], tok[:, n, src, :], ident[:])
                        mm.then_inc(fm_ready, 1)
                    pe.wait_ge(fm_out, 4 * i + 4)
                    pe.wait_ge(bd_out, 4 * i + 4)
                    for ck in range(2):
                        for s in range(2):
                            n = 2 * s + ck
                            if ck == 1:
                                pe.wait_ge(o_out, 4 * i + s + 1)
                                pe.wait_ge(s_out, 2 * i + s + 1)
                            flat = lambda a: a.rearrange("p h t -> p (h t)")
                            pe.matmul(bank[:, A[s], :], lhsT=fm[:, n, 2, :], rhs=flat(bd[:, n, 1]), start=True, stop=True)
                            pe.matmul(bank[:, Bk[s], :], lhsT=fm[:, n, 1, :], rhs=flat(bd[:, n, 2]), start=True, stop=True)
                            pe.matmul(bank[:, Cb[s], :], lhsT=fm[:, n, 1, :], rhs=flat(bd[:, n, 0]), start=True, stop=True).then_inc(gram_ready, 1)
                        for l in range(NL):
                            for s in range(2):
                                pe.wait_ge(x_ready, (i * 2 + ck) * 2 * (NL + 1) + 2 * l + s + 1)
                                if l == 0:
                                    pe.wait_ge(m_out, (i * 2 + ck) * 2 + s + 1)
                                for h in range(AH):
                                    mm = pe.matmul(bank[:, A[s], h * P:(h + 1) * P], lhsT=M[:, s, h, :], rhs=XT[:, s, h, :], start=True, stop=True)
                                mm.then_inc(q_ready, 1)
                            for s in range(2):
                                pe.wait_ge(q_out, (i * 2 + ck) * 2 * NL + 2 * l + s + 1)
                                if l < NL - 1:
                                    for h in range(AH):
                                        pe.matmul(bank[:, Bk[s], h * P:(h + 1) * P], lhsT=QT[:, s, h, :], rhs=X[:, s, h, :], start=True, stop=True)
                                for h in range(AH):
                                    mm = pe.matmul(bank[:, Cb[s], h * P:(h + 1) * P], lhsT=X[:, s, h, :], rhs=QT[:, s, h, :], start=True, stop=True)
                                mm.then_inc(xx_ready, 1)
                        for s in range(2):
                            n = 2 * s + ck
                            if ck == 1:
                                pe.matmul(bank[:, A[s], 0:P], lhsT=fm[:, n, 2, :], rhs=S[:, s, :], start=True, stop=True).then_inc(ks_ready, 1)
                        for s in range(2):
                            pe.wait_ge(r_ready, (i * 2 + ck) * 2 + s + 1)
                            pe.wait_ge(x_ready, (i * 2 + ck) * 2 * (NL + 1) + 2 * NL + s + 1)
                            for h in range(AH):
                                mm = pe.matmul(bank[:, Bk[s], h * AD:(h + 1) * AD], lhsT=XT[:, s, h, :], rhs=R[:, s, h * AD:(h + 1) * AD], start=True, stop=True)
                            mm.then_inc(d_ready, 1)
                        for s in range(2):
                            n = 2 * s + ck
                            pe.wait_ge(d_out, (i * 2 + ck) * 2 + s + 1)
                            if ck == 1:
                                pe.matmul(bank[:, Cb[s], 0:P], lhsT=fm[:, n, 0, :], rhs=S[:, s, :], start=True, stop=False, skip_group_check=True)
                            for h in range(AH):
                                mm = pe.matmul(bank[:, Cb[s], h * AD:(h + 1) * AD], lhsT=PT[:, s, h, :], rhs=D[:, s, h * AD:(h + 1) * AD],
                                               start=ck == 0, stop=True, skip_group_check=ck == 1)
                            mm.then_inc(o_ready, 1)
                            if ck == 0:
                                pe.matmul(bank[:, A[s], P:2 * P], lhsT=tok[:, n, 1, :], rhs=D[:, s, :], start=True, stop=True).then_inc(s_ready, 1)
                    pe.wait_ge(on_ready, i + 1)
                    for n in range(4):
                        mm = pe.transpose(bank[:, 3, n * P:(n + 1) * P], o[:, n, :], ident[:])
                    mm.then_inc(oT_ready, 1)
                    pe.wait_ge(oT_out, i + 1)
                    for n in range(4):
                        mm = pe.matmul(bank[:, 7, n * P:(n + 1) * P], lhsT=oT[:, n, :], rhs=wo_s[:], start=True, stop=True)
                    mm.then_inc(y_ready, 1)

            @block.scalar
            def _(act):
                act.wait_ge(pads_zeroed, 1)
                act.wait_ge(consts_loaded, 160)
                with act.Fori(0, NPAIR) as i:
                    for j in range(3):
                        act.wait_ge(proj_ready, 3 * i + j + 1)
                        act.activation(pad[:, j, :, 3:], bank[:, j, :].rearrange("p (s l) -> p s l", s=2), ACT.Copy).then_inc(proj_out, 1)
                    act.wait_ge(beta_ready, i + 1)
                    act.activation(beta[:].rearrange("p n h -> p (n h)"), bank[:, 3, 0:4 * AH], ACT.Sigmoid).then_inc(beta_out, 1)
                    for j in range(3):
                        act.wait_ge(dw_ready, 3 * i + j + 1)
                        act.activation(qkv[:, j, :], bank[:, 4 + j, :], ACT.Silu).then_inc(silu_ready, 1)
                    for n in range(4):
                        act.wait_ge(tok_ready, 4 * i + n + 1)
                        act.activation(tok[:, n, 0:3, :], bank[:, 4 + n, 0:3 * P].rearrange("p (j t) -> p j t", j=3), ACT.Copy).then_inc(tok_out, 1)
                    act.wait_ge(norm_sq, i + 1)
                    act.activation(ss[:], ss[:], ACT.Sqrt).then_inc(norm_root, 1)
                    for n in range(4):
                        act.wait_ge(fm_ready, 4 * i + n + 1)
                        act.activation(fm[:, n, :, :], bank[:, n, 0:3 * P].rearrange("p (j t) -> p j t", j=3), ACT.Copy).then_inc(fm_out, 1)
                    for ck in range(2):
                        for s in range(2):
                            act.wait_ge(gram_ready, (i * 2 + ck) * 2 + s + 1)
                            act.activation(M[:, s], bank[:, A[s], :].rearrange("p (h t) -> p h t", h=AH), ACT.Copy).then_inc(m_out, 1)
                        for l in range(NL):
                            for s in range(2):
                                act.wait_ge(q_ready, (i * 2 + ck) * 2 * NL + 2 * l + s + 1)
                                act.activation(QT[:, s], bank[:, A[s], :].rearrange("p (h t) -> p h t", h=AH), ACT.Copy).then_inc(q_out, 1)
                        for s in range(2):
                            act.wait_ge(d_ready, (i * 2 + ck) * 2 + s + 1)
                            act.activation(D[:, s, :], bank[:, Bk[s], 0:P], ACT.Copy).then_inc(d_out, 1)
                        for s in range(2):
                            act.wait_ge(o_ready, (i * 2 + ck) * 2 + s + 1)
                            act.activation(o[:, 2 * s + ck, :], bank[:, Cb[s], 0:P], ACT.Copy).then_inc(o_out, 1)
                    act.wait_ge(rms_sq, i + 1)
                    act.activation(rs[:, 1, :], rs[:, 0, :], ACT.Sqrt).then_inc(rms_root, 1)
                    act.wait_ge(oT_ready, i + 1)
                    act.activation(oT[:], bank[:, 3, :].rearrange("p (n t) -> p n t", n=4), ACT.Copy).then_inc(oT_out, 1)
                    act.wait_ge(var_ready, i + 1)
                    act.activation(st[:, 2, :], st[:, 1, :], ACT.Sqrt).then_inc(std_ready, 1)

            @block.gpsimd
            def _(pool):
                pool.memset(pad[:, :, :, 0:3], 0.0).then_inc(pads_zeroed, 1)

            @block.vector
            def _(dve):
                dve.wait_ge(consts_loaded, 160)
                for j in range(3):
                    for k in range(4):
                        ins = dve.tensor_scalar(diag[:, j, k, :], ident[:], cw[:, j, k:k + 1], None, ALU.mult)
                ins.then_inc(diag_ready, 1)
                with dve.Fori(0, NPAIR) as i:
                    done = [0]

                    def link(ins):
                        done[0] += 1
                        ins.then_inc(step_done, 1)
                        dve.wait_ge(step_done, done[0])

                    dve.wait_ge(tok_out, 4 * i + 4)
                    dve.wait_ge(beta_out, i + 1)
                    qk = tok[:, :, 0:2, :]
                    link(dve.tensor_tensor(sq[:], qk, qk, ALU.mult))
                    link(dve.tensor_reduce(ss[:].rearrange("p n j h -> p (n j h)"), sq[:].rearrange("p n j (h d) -> p (n j h) d", d=AD), AX.X, ALU.add))
                    dve.tensor_scalar(ss[:], ss[:], 1e-6, None, ALU.add).then_inc(norm_sq, 1)
                    dve.wait_ge(norm_root, i + 1)
                    link(dve.reciprocal(ss[:], ss[:]))
                    for n in range(4):
                        qh = tok[:, n, 0:2, :].rearrange("p j (h d) -> p (j h) d", d=AD)
                        link(dve.tensor_tensor(qh, qh, bcast(ss[:, n].rearrange("p j h -> p (j h)"), AD), ALU.mult))
                        hd = lambda k: tok[:, n, k, :].rearrange("p (h d) -> p h d", d=AD)
                        bt = bcast(beta[:, n, :], AD)
                        link(dve.tensor_tensor(hd(3), hd(1), bt, ALU.mult))
                        ins = dve.tensor_tensor(hd(2), hd(2), bt, ALU.mult)
                        if n < 3:
                            link(ins)
                    ins.then_inc(keys_ready, 1)
                    for n in range(4):
                        dve.wait_ge(fm_out, 4 * i + n + 1)
                        head = masks[:, 1, ::AD].unsqueeze(2).broadcast_to([P, AH, P])
                        for j in range(3):
                            ins = dve.tensor_tensor(bd[:, n, j], fm[:, n, j, :].unsqueeze(1).broadcast_to([P, AH, P]), head, ALU.mult)
                        ins.then_inc(bd_out, 1)
                    over_h = lambda a: a.unsqueeze(1).broadcast_to([P, AH, P])
                    h4 = lambda k: bank[:, k, :].rearrange("p (h t) -> p h t", h=AH)
                    for ck in range(2):
                        for s in range(2):
                            dve.wait_ge(gram_ready, (i * 2 + ck) * 2 + s + 1)
                            dve.wait_ge(o_ready, (i * 2 + ck) * 2)
                            dve.wait_ge(m_out, (i * 2 + ck) * 2 + s + 1)
                            for t, src, dst in ((0, M[:, s], X), (1, h4(Bk[s]), XT)):
                                link(dve.tensor_tensor(T1[:, s, t], src, over_h(lev[:, t, 0, :]), ALU.mult))
                                link(dve.tensor_tensor(dst[:, s], T1[:, s, t], over_h(ident[:]), ALU.add))
                            dve.tensor_tensor(PT[:, s], h4(Cb[s]), over_h(masks[:, 0, :]), ALU.mult).then_inc(x_ready, 1)
                        for l in range(NL):
                            for s in range(2):
                                dve.wait_ge(xx_ready, (i * 2 + ck) * 2 * NL + 2 * l + s + 1)
                                if l < NL - 1:
                                    link(dve.tensor_tensor(T1[:, s, 0], h4(Bk[s]), over_h(lev[:, 0, l + 1, :]), ALU.mult))
                                    link(dve.tensor_tensor(X[:, s], X[:, s], T1[:, s, 0], ALU.add))
                                link(dve.tensor_tensor(T1[:, s, 1], h4(Cb[s]), over_h(lev[:, 1, l + 1, :]), ALU.mult))
                                dve.tensor_tensor(XT[:, s], XT[:, s], T1[:, s, 1], ALU.add).then_inc(x_ready, 1)
                        for s in range(2):
                            n = 2 * s + ck
                            dve.wait_ge(d_ready, (i * 2 + ck) * 2)
                            if ck == 0:
                                dve.tensor_copy(R[:, s, :], tok[:, n, 2, :]).then_inc(r_ready, 1)
                            else:
                                dve.wait_ge(ks_ready, i * 2 + s + 1)
                                dve.tensor_tensor(R[:, s, :], tok[:, n, 2, :], bank[:, A[s], 0:P], ALU.subtract).then_inc(r_ready, 1)
                        if ck == 0:
                            for s in range(2):
                                dve.wait_ge(s_ready, i * 2 + s + 1)
                                dve.tensor_tensor(S[:, s, :], bank[:, A[s], P:2 * P], masks[:, 1, :], ALU.mult).then_inc(s_out, 1)
                    dve.wait_ge(o_out, 4 * i + 4)
                    link(dve.tensor_tensor(osq[:], o[:], o[:], ALU.mult))
                    link(dve.tensor_reduce(rs[:, 0, :], osq[:].rearrange("p n (h d) -> p (n h) d", d=AD), AX.X, ALU.add))
                    dve.tensor_scalar(rs[:, 0, :], rs[:, 0, :], 1.0 / AD, EPS, ALU.mult, ALU.add).then_inc(rms_sq, 1)
                    dve.wait_ge(rms_root, i + 1)
                    link(dve.reciprocal(rs[:, 0, :], rs[:, 1, :]))
                    oh = o[:].rearrange("p n (h d) -> p (n h) d", d=AD)
                    link(dve.tensor_tensor(oh, oh, bcast(rs[:, 0, :], AD), ALU.mult))
                    dve.tensor_tensor(oh, oh, grms_s[:].unsqueeze(1).broadcast_to([P, 16, AD]), ALU.mult).then_inc(on_ready, 1)
                    dve.wait_ge(y_ready, i + 1)
                    dve.wait_ge(xtok_loaded, 16 * i + 16)
                    v = xtok[:]
                    dve.tensor_tensor(v, v, bank[:, 7, :].rearrange("p (n t) -> p n t", n=4), ALU.add).then_inc(y_out, 1)
                    dve.wait_ge(y_out, i + 1)
                    link(dve.tensor_reduce(st[:, 0, :], v, AX.X, ALU.add))
                    link(dve.tensor_scalar(st[:, 0, :], st[:, 0, :], 1.0 / DM, None, ALU.mult))
                    link(dve.tensor_tensor(v, v, bcast(st[:, 0, :], DM), ALU.subtract))
                    link(dve.tensor_tensor(osq[:], v, v, ALU.mult))
                    link(dve.tensor_reduce(st[:, 1, :], osq[:], AX.X, ALU.add))
                    dve.tensor_scalar(st[:, 1, :], st[:, 1, :], 1.0 / DM, EPS, ALU.mult, ALU.add).then_inc(var_ready, 1)
                    dve.wait_ge(std_ready, i + 1)
                    link(dve.reciprocal(st[:, 3, :], st[:, 2, :]))
                    link(dve.tensor_tensor(v, v, bcast(st[:, 3, :], DM), ALU.mult))
                    over_n = lambda a: a.unsqueeze(1).broadcast_to([P, 4, DM])
                    link(dve.tensor_tensor(v, v, over_n(lng_s[:]), ALU.mult))
                    link(dve.tensor_tensor(v, v, over_n(lnb_s[:]), ALU.add))
                    dve.wait_ge(x1_loaded, 16 * i + 16)
                    dve.tensor_tensor(x1[:], x1[:], v, ALU.add).then_inc(x2_ready, 1)
                    dve.sem_clear(step_done)
def fp4_ffn(nc, xn2_dram, x2_dram, out_dram, wgu, wd, ident_in):
    G = 4
    with ExitStack() as ctx:
        sb, ps, sem = makers(nc, ctx, "f")
        ident = sb("ident", [P, P])
        wgu_s, wd_s = sb("wgu", [P, 6, DM]), sb("wd", [P, FI])
        wguq, wdq = sb("wguq", [P, 6, DM]), sb("wdq", [P, FI])
        wguT, wdT = sb("wguT", [P, 2, FI]), sb("wdT", [P, 3, DM])
        x, xq, xqT = sb("x", [P, G, DM]), sb("xq", [P, G, DM]), sb("xqT", [P, G * P])
        x2 = sb("x2", [P, G, DM])
        g, h, hq, hqT = sb("g", [P, G, FI]), sb("h", [P, G, FI]), sb("hq", [P, G, FI]), sb("hqT", [P, G, 3, P])
        NMAX = G * FI
        a, lo, hi = sb("a", [P, NMAX]), sb("lo", [P, NMAX]), sb("hi", [P, NMAX])
        scale, rscale = sb("scale", [P, NMAX // QB]), sb("rscale", [P, NMAX // QB])
        bank = ps("bank", [P, 8, 512])
        consts_loaded, x_loaded, x2_loaded, stored = sem("consts_loaded"), sem("x_loaded"), sem("x2_loaded"), sem("stored")
        rest_zeroed = sem("rest_zeroed")
        wq_ready, wT_ready, wT_out = sem("wq_ready"), sem("wT_ready"), sem("wT_out")
        xq_ready, xT_ready, xT_out, g_ready, g_out, h_out = (sem(n) for n in ("xq_ready", "xT_ready", "xT_out", "g_ready", "g_out", "h_out"))
        hq_ready, hT_ready, hT_out, y_ready, out_ready, step_done = (sem(n) for n in ("hq_ready", "hT_ready", "hT_out", "y_ready", "out_ready", "step_done"))
        group = lambda t, i: t.rearrange("(i n p) d -> i p n d", p=P, n=G)[bass.ds(i, 1)].rearrange("i p n d -> p (i n) d")
        with nc.Block() as block:
            @block.sync
            def _(sp):
                sp.wait_ge(rest_zeroed, 1)
                for dst, src in ((ident[:], ident_in), (wd_s[:], wd)):
                    sp.dma_start(dst, src).then_inc(consts_loaded, 16)
                for k in range(2):
                    for c, (c0, n) in enumerate(FCH):
                        sp.dma_start(wgu_s[0:n, 3 * k + c, :], wgu[k, c0:c0 + n, :]).then_inc(consts_loaded, 16)
                with sp.Fori(0, NT // G) as i:
                    sp.wait_ge(xT_ready, i + 1)
                    sp.dma_start(x[:], group(xn2_dram, i)).then_inc(x_loaded, 16)
                    sp.wait_ge(stored, 16 * i)
                    sp.dma_start(x2[:], group(x2_dram, i)).then_inc(x2_loaded, 16)
                    sp.wait_ge(out_ready, i + 1)
                    sp.dma_start(group(out_dram, i), x2[:]).then_inc(stored, 16)
                sp.wait_ge(stored, 16 * (NT // G))

            @block.gpsimd
            def _(pool):
                pool.memset(wgu_s[:], 0.0).then_inc(rest_zeroed, 1)

            @block.tensor
            def _(pe):
                pe.sem_inc(xT_ready, 1)
                pe.wait_ge(wq_ready, 2)
                for k in range(2):
                    for c, (c0, n) in enumerate(FCH):
                        pe.transpose(bank[:, k, c0:c0 + n], wguq[0:n, 3 * k + c, :], ident[0:n, 0:n])
                for c, (c0, n) in enumerate(FCH):
                    mm = pe.transpose(bank[0:n, 2, c * P:(c + 1) * P], wdq[:, c0:c0 + n], ident[:])
                mm.then_inc(wT_ready, 1)
                pe.wait_ge(wT_out, 5)
                with pe.Fori(0, NT // G) as i:
                    pe.wait_ge(xq_ready, i + 1)
                    pe.wait_ge(g_out, G * i)
                    for n in range(G):
                        mm = pe.transpose(bank[:, 0, n * P:(n + 1) * P], xq[:, n, :], ident[:])
                    mm.then_inc(xT_ready, 1)
                    pe.wait_ge(xT_out, i + 1)
                    for n in range(G):
                        pe.wait_ge(hT_out, G * i)
                        pe.wait_ge(out_ready, i)
                        for k in range(2):
                            mm = pe.matmul(bank[:, 4 * k + n, 0:FI], lhsT=xqT[:, n * P:(n + 1) * P], rhs=wguT[:, k, :], start=True, stop=True)
                        mm.then_inc(g_ready, 1)
                    pe.wait_ge(hq_ready, i + 1)
                    for n in range(G):
                        for c, (c0, m) in enumerate(FCH):
                            mm = pe.transpose(bank[0:m, n, c * P:(c + 1) * P], hq[:, n, c0:c0 + m], ident[:])
                        mm.then_inc(hT_ready, 1)
                    for n in range(G):
                        pe.wait_ge(hT_out, G * i + n + 1)
                        for c, (c0, m) in enumerate(FCH):
                            mm = pe.matmul(bank[:, 4, n * P:(n + 1) * P], lhsT=hqT[0:m, n, c, :], rhs=wdT[0:m, c, :], start=c == 0, stop=c == 2)
                    mm.then_inc(y_ready, 1)

            @block.scalar
            def _(act):
                act.wait_ge(wT_ready, 1)
                for k in range(2):
                    act.activation(wguT[:, k, :], bank[:, k, 0:FI], ACT.Copy).then_inc(wT_out, 1)
                for c, (c0, n) in enumerate(FCH):
                    act.activation(wdT[0:n, c, :], bank[0:n, 2, c * P:(c + 1) * P], ACT.Copy).then_inc(wT_out, 1)
                with act.Fori(0, NT // G) as i:
                    act.wait_ge(xT_ready, i + 2)
                    act.activation(xqT[:], bank[:, 0, :], ACT.Copy).then_inc(xT_out, 1)
                    for n in range(G):
                        act.wait_ge(g_ready, G * i + n + 1)
                        act.wait_ge(h_out, G * i + n)
                        act.activation(g[:, n, :], bank[:, n, 0:FI], ACT.Silu).then_inc(g_out, 1)
                    for n in range(G):
                        act.wait_ge(hT_ready, G * i + n + 1)
                        act.activation(hqT[:, n, 0:2, :], bank[:, n, 0:2 * P].rearrange("p (c t) -> p c t", c=2), ACT.Copy)
                        act.activation(hqT[0:96, n, 2, :], bank[0:96, n, 2 * P:3 * P], ACT.Copy).then_inc(hT_out, 1)

            @block.vector
            def _(dve):
                done = [0]

                def link(ins):
                    done[0] += 1
                    ins.then_inc(step_done, 1)
                    dve.wait_ge(step_done, done[0])

                def fp4(dst, src, n):
                    bits = lambda t: t.bitcast(I32)
                    blocks = lambda t: t.rearrange("p (b k) -> p b k", k=QB)
                    sc, rsc = scale[:, 0:n // QB], rscale[:, 0:n // QB]
                    av, lv, hv = a[:, 0:n], lo[:, 0:n], hi[:, 0:n]
                    link(dve.tensor_reduce(sc, blocks(src), AX.X, ALU.max, apply_absolute_value=True))
                    link(dve.tensor_scalar(sc, sc, 1.0 / 6.0, 1e-12, ALU.mult, ALU.max))
                    link(dve.reciprocal(rsc, sc))
                    link(dve.tensor_scalar(sc, sc, 0.5, None, ALU.mult))
                    link(dve.tensor_scalar(bits(av), bits(src), 2 ** 31 - 1, None, ALU.bitwise_and))
                    link(dve.tensor_tensor(blocks(av), blocks(av), bcast(rsc, QB), ALU.mult))
                    link(dve.tensor_scalar(lv, av, 0.25, None, ALU.is_gt))
                    link(dve.tensor_scalar(hv, av, 5.0, 2.0, ALU.is_gt, ALU.mult))
                    for mid in (0.75, 1.25, 1.75):
                        link(dve.scalar_tensor_tensor(lv, av, mid, lv, ALU.is_gt, ALU.add))
                    for mid in (2.5, 3.5):
                        link(dve.scalar_tensor_tensor(hv, av, mid, hv, ALU.is_gt, ALU.add))
                    link(dve.scalar_tensor_tensor(lv, hv, 2.0, lv, ALU.mult, ALU.add))
                    link(dve.scalar_tensor_tensor(bits(lv), bits(src), -2 ** 31, bits(lv), ALU.bitwise_and, ALU.bitwise_or))
                    return dve.tensor_tensor(blocks(dst), blocks(lv), bcast(sc, QB), ALU.mult)

                flat = lambda t: t.rearrange("p n d -> p (n d)")
                dve.wait_ge(consts_loaded, 16 * 8)
                fp4(flat(wguq[:]), flat(wgu_s[:]), 6 * DM).then_inc(wq_ready, 1)
                dve.wait_ge(wq_ready, 1)
                fp4(wdq[:], wd_s[:], FI).then_inc(wq_ready, 1)
                dve.wait_ge(wq_ready, 2)
                dve.sem_clear(step_done)
                with dve.Fori(0, NT // G) as i:
                    done[0] = 0
                    dve.wait_ge(x_loaded, 16 * i + 16)
                    fp4(flat(xq[:]), flat(x[:]), G * DM).then_inc(xq_ready, 1)
                    for n in range(G):
                        dve.wait_ge(g_out, G * i + n + 1)
                        dve.tensor_tensor(h[:, n, :], g[:, n, :], bank[:, 4 + n, 0:FI], ALU.mult).then_inc(h_out, 1)
                    dve.wait_ge(xq_ready, i + 1)
                    dve.wait_ge(h_out, G * i + G)
                    fp4(flat(hq[:]), flat(h[:]), G * FI).then_inc(hq_ready, 1)
                    dve.wait_ge(hq_ready, i + 1)
                    dve.wait_ge(x2_loaded, 16 * i + 16)
                    dve.wait_ge(y_ready, i + 1)
                    dve.tensor_tensor(flat(x2[:]), flat(x2[:]), bank[:, 4, :], ALU.add).then_inc(out_ready, 1)
                    dve.sem_clear(step_done)
def build_program(nc, t):
    scratch = lambda name, shape: nc.dram_tensor(name, shape, F32).ap()
    xn, xnT = scratch("xn_scratch", (NTOK, DM)), scratch("xnT_scratch", (DM, NTOK))
    xa, x1, x2 = scratch("xa_scratch", (NTOK, DM)), scratch("x1_scratch", (NTOK, DM)), scratch("x2_scratch", (NTOK, DM))
    xn2, xn2T = scratch("xn2_scratch", (NTOK, DM)), scratch("xn2T_scratch", (DM, NTOK))
    slots, rows = scratch("slots_scratch", (NSLOT, DM)), scratch("rows_scratch", (NSLOT, DM))
    norm_input(nc, t["x"], xn, xnT, t["ident"])
    mamba_fft(nc, t["x"], xnT, xa, t["winT"], t["dft"], t["convw"], t["xpT"], t["dtT"], t["woutT"], t["small"], t["sel"], t["ident"])
    with ExitStack() as ctx:
        pos = ctx.enter_context(nc.sbuf_tensor("pos", [P, 2, NT], I32))
        gate = ctx.enter_context(nc.sbuf_tensor("gate", [P, 2, NT], F32))
        moe_route(nc, xn, xnT, slots, t["wr"], t["br"], t["iota8"], t["lower"], pos, gate)
        moe_experts(nc, slots, rows, t["w1"], t["b1"], t["w2"], t["b2"], t["ident"])
        moe_combine(nc, xn, rows, xa, x1, xn2, xn2T, t["gamma"], t["beta"], t["ident"], pos, gate)
    delta_attention(nc, xn2, xn2T, x1, x2, t["wqkv"], t["wb"], t["cw"], t["wo"], t["grms"], t["lng"], t["lnb"],
                    t["ident"], t["levels"], t["masks"])
    fp4_ffn(nc, xn2, x2, t["out"], t["wgu"], t["wd"], t["ident"])


def shape_constants():
    k = np.arange(L)
    angle = 2 * np.pi * ((k[:, None] * k[None, :]) % L) / L
    c, s = np.cos(angle), np.sin(angle)
    dft = np.stack([chunks(np.concatenate(t, 1)) for t in ([c, -s], [c, s], [-s, c])], 1)
    i, j = np.arange(P)[:, None], np.arange(P)[None, :]
    levels = []
    for n in range(NLEV):
        b = 1 << n
        levels.append(-((i // (2 * b) == j // (2 * b)) & (i // b % 2 == 1) & (j // b % 2 == 0)).astype(np.float32))
    levels = np.stack(levels, 1)
    tables = {
        "dft": dft,
        "sel": np.tile(np.eye(2 * DS), (3, 1)),
        "ident": np.eye(P),
        "iota8": np.arange(NE),
        "lower": np.triu(np.ones((P, P)), 1),
        "levels": np.stack([levels, levels.transpose(2, 1, 0)], 1),
        "masks": np.stack([i <= j, i // AD == j // AD], 1),
    }
    return {n: np.ascontiguousarray(a, dtype=np.float32) for n, a in tables.items()}


def chunks(a):
    return a.reshape(a.shape[0] // P, P, -1).transpose(1, 0, 2)


def layouts(w):
    both = (("", "A_log", "D"), ("b", "A_b_log", "D_b"))
    per_channel = []
    for r, alog, d in both:
        per_channel += [chunks(w[f"L0_attn_conv1d{r}_w"]).reshape(P, -1), chunks(w[f"L0_attn_conv1d{r}_bias"][:, None]).reshape(P, -1),
                        chunks(w[f"L0_attn_dt_proj{r}_b"][:, None]).reshape(P, -1), chunks(w[f"L0_attn_{alog}"]).reshape(P, -1),
                        chunks(w[f"L0_attn_{d}"][:, None]).reshape(P, -1)]
    per_channel.append(w["L0_attn_fft_conv_b"].reshape(4, P).T)
    xproj = []
    for r, _, _ in both:
        a = w[f"L0_attn_x_proj{r}_w"].T
        xproj.append(chunks(np.concatenate([a[:, :DR], a[:, DR:], a[:, DR:], a[:, DR:]], 1)))
    t = {
        "x": w["L0_attn_hidden_states"].reshape(NTOK, DM),
        "winT": w["L0_attn_in_proj_w"].T,
        "convw": w["L0_attn_fft_conv_w"].transpose(1, 2, 0).reshape(4, P, 5, 2 * DI).transpose(1, 0, 2, 3),
        "xpT": np.stack(xproj, 1),
        "dtT": np.stack([w["L0_attn_dt_proj_w"].T, w["L0_attn_dt_projb_w"].T], 1),
        "woutT": chunks(w["L0_attn_out_proj_w"].T),
        "small": np.concatenate(per_channel, 1),
        "wr": w["L0_ffn_Wr"], "br": w["L0_ffn_br"],
        "w1": w["L0_ffn_W1"], "b1": w["L0_ffn_b1"].reshape(NE, FF // P, P).transpose(0, 2, 1),
        "w2": w["L0_ffn_W2"], "b2": w["L0_ffn_b2"], "gamma": w["L0_ffn_gamma"], "beta": w["L0_ffn_beta"],
        "wqkv": np.stack([w["L1_attn_Wq"], w["L1_attn_Wk"], w["L1_attn_Wv"]], 1),
        "wb": w["L1_attn_Wb"], "wo": w["L1_attn_Wo"],
        "cw": np.stack([w["L1_attn_conv_q"].T, w["L1_attn_conv_k"].T, w["L1_attn_conv_v"].T], 1),
        "grms": w["L1_attn_g_rms"], "lng": w["L1_attn_ln_g"], "lnb": w["L1_attn_ln_b"],
        "wgu": np.stack([w["L1_ffn_w_gate"], w["L1_ffn_w_up"]]), "wd": w["L1_ffn_w_down"],
    }
    return {n: np.ascontiguousarray(a) for n, a in t.items()}


def kernel(**inputs):
    import concourse.bacc as bacc
    from concourse.bass_utils import run_bass_kernel_spmd

    nc = bacc.Bacc("TRN2", target_bir_lowering=False, num_devices=1)
    arrays = {**layouts({n: np.asarray(a) for n, a in inputs.items()}), **shape_constants()}
    arrays = {f"in_{n}": a for n, a in arrays.items()}
    t = {n[3:]: nc.dram_tensor(n, a.shape, mybir.dt.from_np(a.dtype), kind="ExternalInput").ap() for n, a in arrays.items()}
    t["out"] = nc.dram_tensor("out_0", (NTOK, DM), F32, kind="ExternalOutput").ap()
    build_program(nc, t)
    return run_bass_kernel_spmd(nc, [arrays], core_ids=[0]).results[0]["out_0"].reshape(B, L, DM)
```

```python
from contextlib import ExitStack

import numpy as np

import concourse.bass as bass
from concourse import mybir

ALU = mybir.AluOpType
ACT = mybir.ActivationFunctionType
AX = mybir.AxisListType
F32 = mybir.dt.float32
BF16 = mybir.dt.bfloat16
I32 = mybir.dt.int32

P = 128
B, L, DM = 16, 256, 128
NTOK = B * L
NT = NTOK // P
DI, DS, DR = 256, 16, 64
EPS = 1e-5


def makers(nc, ctx, tag):
    def sb(name, shape, dt=F32):
        return ctx.enter_context(nc.sbuf_tensor(f"{tag}_{name}", shape, dt))

    def ps(name, shape, dt=F32):
        return ctx.enter_context(nc.psum_tensor(f"{tag}_{name}", shape, dt))

    def sem(name):
        return ctx.enter_context(nc.semaphore(f"{tag}_{name}"))

    return sb, ps, sem


def bcast(ap, n):
    return ap.unsqueeze(len(ap.shape)).broadcast_to([*ap.shape, n])


NE, CAP, FF = 8, 640, 512
NSLOT = NE * CAP
assert CAP == -(-NTOK * 5 // (4 * NE)) and CAP % P == 0


AH, AD = 4, 32
NLEV = 7


FI, QB = 352, 16
FCH = ((0, 128), (128, 128), (256, 96))


def norm_input(nc, x, xn_dram, xnT_dram, ident_in):
    with ExitStack() as ctx:
        sb, ps, sem = makers(nc, ctx, "n1")
        X = sb("X", [P, NT, DM])
        SQ = sb("SQ", [P, NT, DM])
        XT = sb("XT", [P, NT * P])
        ident = sb("ident", [P, P])
        stat = sb("stat", [P, 4, NT])
        psT = ps("psT", [P, 4, 512])
        x_loaded, ident_loaded = [sem("x_loaded0"), sem("x_loaded1")], sem("ident_loaded")
        var_ready, std_ready = sem("var_ready"), sem("std_ready")
        xn_ready, turned, evicted = sem("xn_ready"), sem("turned"), sem("evicted")
        stored, step_done = sem("stored"), sem("step_done")
        H = NT // 2
        with nc.Block() as block:
            @block.sync
            def _(sp):
                for h in range(2):
                    sp.dma_start(X[:, h * H:(h + 1) * H, :],
                                 x.rearrange("(n p) d -> p n d", p=P)[:, h * H:(h + 1) * H, :]).then_inc(x_loaded[h], 16)
                sp.dma_start(ident[:], ident_in).then_inc(ident_loaded, 16)
                for h in range(2):
                    sp.wait_ge(xn_ready, h + 1)
                    sp.dma_start(xn_dram.rearrange("(n p) d -> p n d", p=P)[:, h * H:(h + 1) * H, :],
                                 X[:, h * H:(h + 1) * H, :]).then_inc(stored, 16)
                sp.wait_ge(evicted, NT // 4)
                sp.dma_start(xnT_dram, XT[:]).then_inc(stored, 16)
                sp.wait_ge(stored, 48)

            @block.vector
            def _(dve):
                done = [0]

                def link(ins):
                    done[0] += 1
                    ins.then_inc(step_done, 1)
                    dve.wait_ge(step_done, done[0])

                for h in range(2):
                    xs, sq = X[:, h * H:(h + 1) * H, :], SQ[:, h * H:(h + 1) * H, :]
                    mean, var = stat[:, 0, h * H:(h + 1) * H], stat[:, 1, h * H:(h + 1) * H]
                    std, rstd = stat[:, 2, h * H:(h + 1) * H], stat[:, 3, h * H:(h + 1) * H]
                    dve.wait_ge(x_loaded[h], 16)
                    link(dve.tensor_reduce(mean, xs, AX.X, ALU.add))
                    link(dve.tensor_scalar(mean, mean, 1.0 / DM, None, ALU.mult))
                    link(dve.tensor_tensor(xs, xs, bcast(mean, DM), ALU.subtract))
                    link(dve.tensor_tensor(sq, xs, xs, ALU.mult))
                    link(dve.tensor_reduce(var, sq, AX.X, ALU.add))
                    dve.tensor_scalar(var, var, 1.0 / DM, EPS, ALU.mult, ALU.add).then_inc(var_ready, 1)
                    dve.wait_ge(std_ready, h + 1)
                    link(dve.reciprocal(rstd, std))
                    dve.tensor_tensor(xs, xs, bcast(rstd, DM), ALU.mult).then_inc(xn_ready, 1)

            @block.scalar
            def _(act):
                for h in range(2):
                    act.wait_ge(var_ready, h + 1)
                    act.activation(stat[:, 2, h * H:(h + 1) * H], stat[:, 1, h * H:(h + 1) * H],
                                   ACT.Sqrt).then_inc(std_ready, 1)
                for g in range(NT // 4):
                    act.wait_ge(turned, g + 1)
                    act.activation(XT[:, g * 512:(g + 1) * 512], psT[:, g % 4, :], ACT.Copy).then_inc(evicted, 1)

            @block.tensor
            def _(pe):
                pe.wait_ge(ident_loaded, 16)
                for g in range(NT // 4):
                    pe.wait_ge(xn_ready, 1 + g // (NT // 8))
                    if g >= 4:
                        pe.wait_ge(evicted, g - 3)
                    for k in range(4):
                        mm = pe.transpose(psT[:, g % 4, k * P:(k + 1) * P], X[:, 4 * g + k, :], ident[:])
                    mm.then_inc(turned, 1)


def mamba_fft(nc, x, xnT_dram, x1_dram, winT, dft, convw, xpT, dtT, woutT, small, sel_in, ident_in):
    NPAIR = B // 2
    ROW = 2 * L
    HN = DS // 2
    FFT_STEP = 5
    with ExitStack() as ctx:
        sb, ps, sem = makers(nc, ctx, "m")
        winT_s = sb("winT", [P, 4 * P])
        dft_s = sb("dft", [P, 3, 2, 512])
        convw_s = sb("convw", [P, 4, 5, 512])
        xp_s = sb("xp", [P, 2, 2, 160])
        dtT_s = sb("dtT", [DR, 2, DI])
        wout_s = sb("wout", [P, 2, DM])
        small_s = sb("small", [P, 96])
        negA = sb("negA", [P, 2, 32])
        self_s = sb("self", [96, 32])
        sel = sb("sel", [96, 32], BF16)
        one = sb("one", [P, 1])
        ident = sb("ident", [P, P])
        diag = sb("diag", [P, 2, 2, 4, P])
        xnT = sb("xnT", [P, ROW])
        xtok = sb("xtok", [P, 4, P])
        xl = sb("xl", [P, 2, 2, 256])
        XF = sb("XF", [P, 2, 2, 2, 256])
        U = XF[:].rearrange("p a b c d -> p (a b c d)").rearrange("p (k s n) -> p k s n", k=2, s=2)
        xc = sb("xc", [P, 4, 2, 260])
        Z = sb("Z", [P, 4, 2, 256])
        V = xl[:].rearrange("p a b c -> p (a b) c")
        stat = sb("stat", [P, 8, 4])
        xpad = sb("xpad", [P, 2, 2, 2, 3 + L])
        u = sb("u", [P, 2, 2, ROW])
        sz = sb("sz", [P, 2, ROW])
        dt = sb("dt", [DR, ROW])
        bc32 = sb("bc32", [96, ROW])
        bcr = sb("bcr", [96, ROW])
        bcq = sb("bcq", [64, ROW], BF16)
        bcs = sb("bcs", [96, 2, ROW], BF16)
        tmp = sb("tmp", [P, ROW])
        delta = sb("delta", [P, 2, 2, ROW])
        dx = sb("dx", [P, 2, 2, ROW])
        dA = sb("dA", [P, 2, 4, 2, L])
        h = sb("h", [P, 2, HN, ROW])
        y = sb("y", [P, 2, 2, ROW])
        ypart = sb("ypart", [P, ROW])
        psR = ps("psR", [P, 2, 1024])
        psG = ps("psG", [P, 4, 512])

        consts_loaded, rows_zeroed, negA_ready, sel_ready = (sem("consts_loaded"), sem("rows_zeroed"),
                                                           sem("negA_ready"), sem("sel_ready"))
        xnT_loaded, xtok_loaded, x1_stored = sem("xnT_loaded"), sem("xtok_loaded"), sem("x1_stored")
        job_ready, job_evicted = sem("job_ready"), sem("job_evicted")
        diag_ready = sem("diag_ready")
        bc_copied, bcs_ready = sem("bc_copied"), sem("bcs_ready")
        softplus_parts, dx_ready = sem("softplus_parts"), sem("dx_ready")
        spread, spread_used = sem("spread"), sem("spread_used")
        exp_ready, scan_done = sem("exp_ready"), sem("scan_done")
        gate_ready, y_ready, out_ready, res_ready = sem("gate_ready"), sem("y_ready"), sem("out_ready"), sem("res_ready")
        zz_ready, mod2_ready, mod_ready = sem("zz_ready"), sem("mod2_ready"), sem("mod_ready")
        var_ready, std_ready = sem("var_ready"), sem("std_ready")
        dve_step, act_step, pool_step = sem("dve_step"), sem("act_step"), sem("pool_step")

        def cw(r, c, k): return small_s[:, 46 * r + 4 * c + k:46 * r + 4 * c + k + 1]
        def cb(r, c): return small_s[:, 46 * r + 8 + c:46 * r + 9 + c]
        def dtb(r, c): return small_s[:, 46 * r + 10 + c:46 * r + 11 + c]
        def alog(r): return small_s[:, 46 * r + 12:46 * r + 44]
        def dskip(r, c): return small_s[:, 46 * r + 44 + c:46 * r + 45 + c]
        def fcb(o): return small_s[:, 92 + o:93 + o]

        XZ, XL, DW, DIR, S1 = 0, 4, 6, 10, 18
        S2, CV, S3, S4 = S1 + 4, S1 + 8, S1 + 12, S1 + 16
        JOBS = S4 + 4
        OUT = JOBS
        assert OUT % 4 == 2

        def wait_bank(pe, i, j):
            if j == OUT:
                pe.wait_ge(job_evicted, i * JOBS + (OUT - 4) + 1 + JOBS)
            elif j >= 4:
                pe.wait_ge(job_evicted, i * JOBS + j - 3 + JOBS)
            else:
                last = {0: JOBS - 2, 1: JOBS - 1, 2: JOBS - 4, 3: JOBS - 3}[j]
                pe.wait_ge(job_evicted, i * JOBS + last + 1)
                if j == 2:
                    pe.wait_ge(res_ready, i)

        ends = {}
        n = 0
        for j0, k in ((S1, 2), (S2, 4), (CV, 20), (S3, 4), (S4, 4)):
            for j in range(j0, j0 + 4):
                n += k
                ends[j] = (n - 1) // FFT_STEP
        slots = 32
        assert max(ends.values()) < slots

        with nc.Block() as block:
            @block.sync
            def _(sp):
                sp.dma_start(winT_s[:], winT).then_inc(consts_loaded, 16)
                sp.dma_start(small_s[:], small).then_inc(consts_loaded, 16)
                sp.dma_start(xp_s[:], xpT).then_inc(consts_loaded, 16)
                sp.dma_start(dtT_s[:], dtT).then_inc(consts_loaded, 16)
                sp.dma_start(wout_s[:], woutT).then_inc(consts_loaded, 16)
                sp.dma_start(self_s[:], sel_in).then_inc(consts_loaded, 16)
                sp.dma_start(ident[:], ident_in).then_inc(consts_loaded, 16)
                sp.dma_start(dft_s[:], dft).then_inc(consts_loaded, 16)
                sp.dma_start(convw_s[:], convw).then_inc(consts_loaded, 16)
                with sp.Fori(0, NPAIR) as i:
                    sp.wait_ge(job_evicted, i * JOBS + 6)
                    sp.dma_start(xnT[:], xnT_dram[:, bass.ds(i * ROW, ROW)]).then_inc(xnT_loaded, 16)
                    sp.wait_ge(x1_stored, i * 16)
                    sp.dma_start(xtok[:], x.rearrange("(i n p) d -> i p n d", p=P, n=4)[bass.ds(i, 1)].rearrange("i p n d -> p (i n) d")).then_inc(xtok_loaded, 16)
                    sp.wait_ge(res_ready, i + 1)
                    sp.dma_start(x1_dram.rearrange("(i n p) d -> i p n d", p=P, n=4)[bass.ds(i, 1)].rearrange("i p n d -> p (i n) d"), xtok[:]).then_inc(x1_stored, 16)
                sp.wait_ge(x1_stored, 16 * NPAIR)

            @block.gpsimd
            def _(pool):
                pool.memset(xpad[:, :, :, :, 0:3], 0.0)
                pool.memset(xc[:, :, :, 0:2], 0.0)
                pool.memset(xc[:, :, :, 258:260], 0.0)
                pool.memset(dA[:, :, :, :, 0:1], 0.0)
                pool.memset(one[:], 1.0).then_inc(rows_zeroed, 1)
                pool.wait_ge(consts_loaded, 16 * 9)
                with pool.Fori(0, NPAIR) as i:
                    steps = 0
                    for r in range(2):
                        for c in range(2):
                            pool.wait_ge(softplus_parts, i * 4 + r * 2 + c + 1)
                            steps += 1
                            pool.tensor_tensor(delta[:, r, c, :], delta[:, r, c, :], dx[:, r, c, :], ALU.add).then_inc(pool_step, 1)
                            pool.wait_ge(pool_step, steps)
                            pool.tensor_tensor(dx[:, r, c, :], delta[:, r, c, :], u[:, r, c, :], ALU.mult).then_inc(dx_ready, 1)
                    pool.sem_clear(pool_step)

            @block.scalar
            def _(act):
                act.sem_inc(job_evicted, JOBS)
                act.wait_ge(consts_loaded, 16 * 9)
                act.wait_ge(rows_zeroed, 1)
                for r in range(2):
                    act.activation(negA[:, r, :], alog(r), ACT.Exp).then_inc(negA_ready, 1)
                act.wait_ge(negA_ready, 4)
                with act.Fori(0, NPAIR) as i:
                    steps = [0]

                    def link(ins):
                        steps[0] += 1
                        ins.then_inc(act_step, 1)
                        act.wait_ge(act_step, steps[0])

                    def done(j):
                        act.wait_ge(job_ready, i * JOBS + j + 1)
                        return psG[:, j % 4, :]

                    for c in range(2):
                        pz = done(XZ + c).rearrange("p (s l) -> p s l", s=2)
                        act.activation(xpad[:, 0, c, :, 3:], pz, ACT.Copy)
                        act.activation(xpad[:, 1, c, :, 3:][:, :, ::-1], pz, ACT.Copy).then_inc(job_evicted, 1)
                    act.wait_ge(y_ready, i)
                    for c in range(2):
                        act.activation(sz[:, c, :], done(XZ + 2 + c), ACT.Silu).then_inc(job_evicted, 1)
                    for s in range(2):
                        act.activation(xl[:, s, :, :], done(XL + s).rearrange("p (k d) -> p k d", k=2), ACT.Copy).then_inc(job_evicted, 1)
                    for r in range(2):
                        for c in range(2):
                            act.activation(u[:, r, c, :], done(DW + 2 * r + c), ACT.Silu, bias=cb(r, c)).then_inc(job_evicted, 1)
                    for r in range(2):
                        j = DIR + 4 * r
                        act.activation(dt[:], done(j)[0:DR, :], ACT.Copy).then_inc(job_evicted, 1)
                        pb = done(j + 1)[0:96, :]
                        act.wait_ge(bcs_ready, i * 2 + r)
                        act.activation(bcs[:, r, :], pb, ACT.Copy).then_inc(bc_copied, 1)
                        act.activation(bc32[:], pb, ACT.Copy).then_inc(job_evicted, 1)
                        for c in range(2):
                            pd = done(j + 2 + c)
                            act.wait_ge(softplus_parts, i * 4 + 2 * r + c)
                            link(act.activation(tmp[:], pd, ACT.Abs, bias=dtb(r, c)))
                            act.activation(dx[:, r, c, :], pd, ACT.Relu, bias=dtb(r, c)).then_inc(job_evicted, 1)
                            link(act.activation(tmp[:], tmp[:], ACT.Exp, scale=-1.0))
                            act.activation(delta[:, r, c, :], tmp[:], ACT.Ln, bias=one[:]).then_inc(softplus_parts, 1)

                    def decays(e):
                        r, c = e // 8, e % 2
                        n0 = (e // 4 % 2) * HN + (e // 2 % 2) * 4
                        act.wait_ge(scan_done, i * 16 + e + 1)
                        act.wait_ge(dx_ready, i * 4 + r * 2 + c + 1)
                        dr = delta[:, r, c, :].rearrange("p (s l) -> p s l", s=2)[:, :, 1:]
                        for n in range(4):
                            k = 16 * c + n0 + n
                            ins = act.activation(dA[:, e % 2, n, :, 1:], dr, ACT.Exp, scale=negA[:, r, k:k + 1])
                        ins.then_inc(exp_ready, 1)

                    def evict(j):
                        pj = done(j)
                        k = (j - S1) % 4
                        if j < S2:
                            out = XF[:, :, k % 2, k // 2, :]
                            ins = act.activation(out, pj.rearrange("p (a k) -> p a k", a=2), ACT.Copy)
                        elif j < CV:
                            ins = act.activation(xc[:, k, :, 2:258], pj.rearrange("p (s k) -> p s k", s=2), ACT.Copy)
                        elif j < S3:
                            ins = act.activation(Z[:, k, :, :], pj.rearrange("p (s k) -> p s k", s=2), ACT.Silu, bias=fcb(k))
                        elif j < S4:
                            ins = act.activation(U[:, k % 2, k // 2, :], pj, ACT.Copy)
                        else:
                            ins = act.activation(Z[:, k, :, :], pj.rearrange("p (a l) -> p a l", a=2), ACT.Square)
                        ins.then_inc(job_evicted, 1)

                    decays(0)
                    decays(1)
                    for s in range(slots):
                        if s % 8 in (2, 4) and s < slots - 4:
                            e = s // 8 * 4 + (2 if s % 8 == 2 else 4)
                            decays(e)
                            decays(e + 1)
                        for j in sorted(ends):
                            if ends[j] == s:
                                evict(j)
                    act.wait_ge(mod2_ready, i + 1)
                    for k in range(4):
                        ins = act.activation(V[:, k, :], V[:, k, :], ACT.Sqrt, scale=stat[:, 1, k:k + 1])
                    ins.then_inc(mod_ready, 1)
                    act.wait_ge(var_ready, i + 1)
                    act.activation(stat[:, 5, :], stat[:, 4, :], ACT.Sqrt).then_inc(std_ready, 1)
                    act.sem_clear(act_step)

            @block.tensor
            def _(pe):
                pe.wait_ge(consts_loaded, 16 * 9)
                pe.wait_ge(rows_zeroed, 1)
                pe.wait_ge(sel_ready, 1)
                pe.wait_ge(diag_ready, 1)
                with pe.Fori(0, NPAIR) as i:
                    def job(j, mms, start=None):
                        for n, (out, lhsT, rhs, st, sp_) in enumerate(mms):
                            yield
                            if n == 0:
                                if start:
                                    start()
                                wait_bank(pe, i, j)
                            mm = pe.matmul(out, lhsT=lhsT, rhs=rhs, start=st, stop=sp_)
                        mm.then_inc(job_ready if j != OUT else out_ready, 1)

                    def run(steps):
                        for _ in steps:
                            pass

                    pe.wait_ge(xnT_loaded, 16 * i + 16)
                    for c in range(4):
                        run(job(XZ + c, [(psG[:, (XZ + c) % 4, :], winT_s[:, c * P:(c + 1) * P], xnT[:], True, True)]))
                    for s in range(2):
                        g = (XL + s) % 4
                        run(job(XL + s, [(psG[:, g, k * 256:(k + 1) * 256],
                                          xnT[:, s * L + k * P:s * L + (k + 1) * P], winT_s[:, 0:256], True, True)
                                         for k in range(2)]))
                    for r in range(2):
                        for c in range(2):
                            j = DW + 2 * r + c
                            if r == 0:
                                pe.wait_ge(job_evicted, i * JOBS + XZ + c + 1 + JOBS)
                            run(job(j, [(psG[:, j % 4, :], diag[:, r, c, k, :], xpad[:, r, c, :, k:k + L], k == 0, k == 3) for k in range(4)]))
                    for r in range(2):
                        j = DIR + 4 * r
                        pe.wait_ge(job_evicted, i * JOBS + DW + 2 * r + 2 + JOBS)
                        run(job(j, [(psG[0:DR, j % 4, :], xp_s[:, r, c, 0:DR], u[:, r, c, :], c == 0, c == 1) for c in range(2)]))
                        run(job(j + 1, [(psG[0:96, (j + 1) % 4, :], xp_s[:, r, c, DR:DR + 96], u[:, r, c, :], c == 0, c == 1) for c in range(2)]))
                        for c in range(2):
                            if c == 0:
                                pe.wait_ge(job_evicted, i * JOBS + j + 1 + JOBS)
                            run(job(j + 2 + c, [(psG[:, (j + 2 + c) % 4, :], dtT_s[:, r, c * P:(c + 1) * P], dt[:], True, True)]))

                    def evicted(upto):
                        return lambda: pe.wait_ge(job_evicted, i * JOBS + upto + JOBS)

                    def fft():
                        C, S, NS = (dft_s[:, 1, :, 0:256], dft_s[:, 1, :, 256:512], dft_s[:, 0, :, 256:512])
                        for k in range(4):
                            s, dc = k // 2, k % 2
                            yield from job(S1 + k, [(psG[:, (S1 + k) % 4, :], xl[:, s, lc, dc * P:(dc + 1) * P],
                                                     dft_s[:, 0, lc, :], lc == 0, lc == 1) for lc in range(2)],
                                           evicted(XL + 2) if k == 0 else None)
                        for k in range(4):
                            im, mc = k // 2, k % 2
                            pairs = ((C, 0), (S, 1)) if not im else ((C, 1), (NS, 0))
                            yield from job(S2 + k, [(psG[:, (S2 + k) % 4, :], t[:, dc, mc * P:(mc + 1) * P],
                                                     XF[:, a, dc, :, :], (n, dc) == (0, 0), (n, dc) == (1, 1))
                                                    for n, (t, a) in enumerate(pairs) for dc in range(2)],
                                           evicted(S2) if k == 0 else None)
                        for o in range(4):
                            yield from job(CV + o, [(psG[:, (CV + o) % 4, :], convw_s[:, c, t, o * P:(o + 1) * P],
                                                     xc[:, c, :, t:t + 256], (c, t) == (0, 0), (c, t) == (3, 4))
                                                    for c in range(4) for t in range(5)],
                                           evicted(CV) if o == 0 else None)
                        for k in range(4):
                            s, kc = k // 2, k % 2
                            yield from job(S3 + k, [(psG[:, (S3 + k) % 4, :], Z[:, m, s, kc * P:(kc + 1) * P],
                                                     dft_s[:, 1 + m // 2, m % 2, :], m == 0, m == 3) for m in range(4)],
                                           evicted(S3) if k == 0 else None)
                        for k in range(4):
                            s, dc = k // 2, k % 2
                            yield from job(S4 + k, [(psG[:, (S4 + k) % 4, :], U[:, kc, s, a * 256 + dc * P:a * 256 + (dc + 1) * P],
                                                     dft_s[:, 1 + a, kc, :], (a, kc) == (0, 0), (a, kc) == (1, 1))
                                                    for a in range(2) for kc in range(2)],
                                           evicted(S4) if k == 0 else None)

                    steps = fft()
                    next(steps)
                    for s in range(slots):
                        r, hf, k = s // 16, s // 8 % 2, s % 8
                        if s % 16 == 0:
                            pe.wait_ge(bcs_ready, i * 2 + r + 1)
                        pe.wait_ge(spread_used, i * slots + s + 1)
                        for m in range(2):
                            row = DS * (k // 4) + HN * hf + 2 * (k % 4) + m
                            mm = pe.matmul(psR[:, s % 2, m * 512:(m + 1) * 512],
                                           lhsT=sel[:, row:row + 1].broadcast_to([96, P]), rhs=bcs[:, r, :], start=True, stop=True)
                        mm.then_inc(spread, 1)
                        for _ in range(FFT_STEP):
                            next(steps, None)
                    run(steps)
                    pe.wait_ge(y_ready, i + 1)
                    run(job(OUT, [(psG[:, OUT % 4, n * P:(n + 1) * P], y[:, 0, c, n * P:(n + 1) * P], wout_s[:, c, :], c == 0, c == 1)
                                  for n in range(4) for c in range(2)]))

            @block.vector
            def _(dve):
                dve.sem_inc(spread_used, 2)
                dve.sem_inc(scan_done, 2)
                dve.wait_ge(consts_loaded, 16 * 9)
                dve.tensor_copy(sel[:], self_s[:]).then_inc(sel_ready, 1)
                for r in range(2):
                    for c in range(2):
                        for k in range(4):
                            ins = dve.tensor_scalar(diag[:, r, c, k, :], ident[:], cw(r, c, k), None, ALU.mult)
                ins.then_inc(diag_ready, 1)
                dve.wait_ge(negA_ready, 2)
                for r in range(2):
                    dve.tensor_scalar(negA[:, r, :], negA[:, r, :], -1.0, None, ALU.mult).then_inc(negA_ready, 1)
                dve.wait_ge(sel_ready, 1)
                with dve.Fori(0, NPAIR) as i:
                    done = [0]

                    def link(ins):
                        done[0] += 1
                        ins.then_inc(dve_step, 1)
                        dve.wait_ge(dve_step, done[0])

                    dve.wait_ge(job_evicted, i * JOBS + XL + JOBS)
                    link(dve.tensor_reduce(stat[:, 0, :].rearrange("p (s c) -> p c s", s=2),
                                           sz[:].rearrange("p c (s l) -> p c s l", s=2), AX.X, ALU.max))
                    link(dve.tensor_tensor(stat[:, 1, :], stat[:, 0, :], stat[:, 0, :], ALU.mult))
                    link(dve.tensor_scalar(stat[:, 1, :], stat[:, 1, :], 1.0 / (DI * L) ** 2, None, ALU.mult))
                    for r in range(2):
                        dve.wait_ge(bc_copied, i * 2 + r + 1)
                        dve.wait_ge(job_evicted, i * JOBS + DIR + 4 * r + 2 + JOBS)
                        link(dve.tensor_tensor(bcr[:], bc32[:], bcs[:, r, :], ALU.subtract))
                        link(dve.tensor_copy(bcs[64:96, r, :], bcr[64:96, :]))
                        link(dve.tensor_copy(bcq[32:64, :], bcr[32:64, :]))
                        dve.tensor_tensor(bcs[32:64, r, :], bcr[32:64, :], bcq[32:64, :], ALU.subtract).then_inc(bcs_ready, 1)
                    for r in range(2):
                        dve.wait_ge(dx_ready, i * 4 + 2 * r + 2)
                        for hf in range(2):
                            s0 = r * 16 + hf * 8
                            for j in range(4):
                                dve.wait_ge(spread, i * slots + s0 + j + 1)
                                for c in range(2):
                                    ins = dve.tensor_tensor(h[:, c, 2 * j:2 * j + 2, :], psR[:, j % 2, :].rearrange("p (n l) -> p n l", n=2),
                                                            dx[:, r, c, :].unsqueeze(1).broadcast_to([P, 2, ROW]), ALU.mult)
                                    if c == 0:
                                        link(ins)
                                ins.then_inc(spread_used, 1)
                                if j % 2 == 1:
                                    dve.wait_ge(spread_used, i * slots + s0 + j + 1 + 2)
                                    for c in range(2):
                                        e = r * 8 + hf * 4 + (j // 2) * 2 + c
                                        dve.wait_ge(exp_ready, i * 16 + e + 1)
                                        hq = h[:, c, 2 * j - 2:2 * j + 2, :].rearrange("p n l -> p (n l)")
                                        dve.tensor_tensor_scan(hq, dA[:, e % 2].rearrange("p n s l -> p (n s l)"), hq, 0.0,
                                                               ALU.mult, ALU.add).then_inc(scan_done, 1)
                            dve.wait_ge(scan_done, i * 16 + r * 8 + hf * 4 + 4 + 2)
                            for j in range(4):
                                dve.wait_ge(spread, i * slots + s0 + 4 + j + 1)
                                for c in range(2):
                                    hj = h[:, c, 2 * j:2 * j + 2, :]
                                    ins = dve.tensor_tensor(hj, psR[:, j % 2, :].rearrange("p (n l) -> p n l", n=2), hj, ALU.mult)
                                    if c == 0:
                                        link(ins)
                                ins.then_inc(spread_used, 1)
                            dve.wait_ge(spread_used, i * slots + s0 + 8 + 2)
                            for c in range(2):
                                hs = h[:, c].rearrange("p n l -> p l n")
                                if hf == 0:
                                    if r == 0 and c == 0:
                                        dve.wait_ge(out_ready, i)
                                    link(dve.tensor_reduce(y[:, r, c, :], hs, AX.X, ALU.add))
                                else:
                                    link(dve.tensor_reduce(ypart[:], hs, AX.X, ALU.add))
                                    link(dve.tensor_tensor(y[:, r, c, :], y[:, r, c, :], ypart[:], ALU.add))
                                    link(dve.scalar_tensor_tensor(y[:, r, c, :], u[:, r, c, :], dskip(r, c), y[:, r, c, :], ALU.mult, ALU.add))
                    dve.wait_ge(job_evicted, i * JOBS + JOBS + JOBS)
                    dve.tensor_tensor(V, Z[:, :, 0, :], Z[:, :, 1, :], ALU.add).then_inc(mod2_ready, 1)
                    dve.wait_ge(mod_ready, i + 1)
                    link(dve.tensor_reduce(stat[:, 2, :], V, AX.X, ALU.add))
                    link(dve.tensor_scalar(stat[:, 2, :], stat[:, 2, :], 1.0 / L, None, ALU.mult))
                    link(dve.tensor_tensor(V, V, bcast(stat[:, 2, :], L), ALU.subtract))
                    sq = h[:, 0, 0:2, :].rearrange("p n (s l) -> p (n s) l", s=2)
                    link(dve.tensor_tensor(sq, V, V, ALU.mult))
                    link(dve.tensor_reduce(stat[:, 3, :], sq, AX.X, ALU.add))
                    dve.tensor_scalar(stat[:, 4, :], stat[:, 3, :], 1.0 / L, EPS, ALU.mult, ALU.add).then_inc(var_ready, 1)
                    for c in range(2):
                        y0 = y[:, 0, c, :].rearrange("p (s l) -> p s l", s=2)
                        y1 = y[:, 1, c, :].rearrange("p (s l) -> p s l", s=2)
                        link(dve.tensor_tensor(y0, y0, y1[:, :, ::-1], ALU.add))
                    link(dve.tensor_tensor(y[:, 0], y[:, 0], sz[:], ALU.mult))
                    dve.wait_ge(std_ready, i + 1)
                    link(dve.reciprocal(stat[:, 6, :], stat[:, 5, :]))
                    link(dve.tensor_tensor(V, V, bcast(stat[:, 6, :], L), ALU.mult))
                    dve.tensor_tensor(y[:, 0].rearrange("p c (s l) -> p s c l", s=2), y[:, 0].rearrange("p c (s l) -> p s c l", s=2),
                                      V.rearrange("p (s c) l -> p s c l", s=2), ALU.add).then_inc(y_ready, 1)
                    dve.wait_ge(out_ready, i + 1)
                    dve.wait_ge(xtok_loaded, 16 * i + 16)
                    dve.tensor_tensor(xtok[:].rearrange("p n d -> p (n d)"), xtok[:].rearrange("p n d -> p (n d)"),
                                      psG[:, OUT % 4, :], ALU.add).then_inc(res_ready, 1)
                    dve.sem_clear(dve_step)
def moe_route(nc, xn_dram, xnT_dram, slots_dram, wr, br, iota8, lower_in, pos, gate):
    G = 4
    with ExitStack() as ctx:
        sb, ps, sem = makers(nc, ctx, "r")
        xT = sb("xT", [P, NTOK])
        wr_s, br_s, iota = sb("wr", [P, NE]), sb("br", [P, NE]), sb("iota", [P, NE])
        lower, ones = sb("lower", [P, P]), sb("ones", [P, P])
        lg, oh, key = sb("lg", [P, NT, NE]), sb("oh", [P, 2, NT, NE]), sb("key", [P, NT, NE])
        t, t2, gt, base = sb("t", [P, NT, NE]), sb("t2", [P, NT, NE]), sb("gt", [P, NT, NE]), sb("base", [P, NT, NE])
        m, w = sb("m", [P, 3, NT]), sb("w", [P, 3, NT])
        kept, dest = sb("kept", [P, 2, NT]), sb("dest", [P, 2, NT])
        bit, thr, cand, acc = sb("bit", [P, NE], I32), sb("thr", [P, NE], I32), sb("cand", [P, NE], I32), sb("acc", [P, NE], I32)
        cnt, need, first = sb("cnt", [P, NE]), sb("need", [P, NE]), sb("first", [P, NE])
        zeros = sb("zeros", [P, NSLOT // P * DM])
        xbuf, ibuf = sb("xbuf", [P, 2, G, DM]), sb("ibuf", [P, 2, 2, G], I32)
        psL, psC, psA = ps("psL", [P, NT, NE]), ps("psC", [P, NE]), ps("psA", [P, 2, 256])
        loaded, const_ready = sem("loaded"), sem("const_ready")
        logits_ready, diff_ready, exp_ready = sem("logits_ready"), sem("diff_ready"), sem("exp_ready")
        count_ready, count_summed = sem("count_ready"), sem("count_summed")
        mask_ready, mask_summed = sem("mask_ready"), sem("mask_summed")
        slots_zeroed, index_ready, row_loaded, scattered = sem("slots_zeroed"), sem("index_ready"), [sem("row_loaded0"), sem("row_loaded1")], [sem("scattered0"), sem("scattered1")]
        step_done, scatter_begun = sem("step_done"), sem("scatter_begun")
        flat = lambda a: a.rearrange("p n e -> p (n e)")
        over_n = lambda a: a.unsqueeze(1).broadcast_to([P, NT, NE])
        by_e = lambda a: a.rearrange("p n e -> p e n")
        with nc.Block() as block:
            @block.sync
            def _(sp):
                for dst, src in ((wr_s[:], wr), (br_s[:], br.rearrange("(o e) -> o e", o=1).broadcast_to([P, NE])),
                                 (iota[:], iota8.rearrange("(o e) -> o e", o=1).broadcast_to([P, NE])), (lower[:], lower_in), (xT[:], xnT_dram)):
                    sp.dma_start(dst, src).then_inc(loaded, 16)
                sp.wait_ge(const_ready, 3)
                sp.dma_start(slots_dram.rearrange("(p n) d -> p (n d)", p=P), zeros[:]).then_inc(slots_zeroed, 16)
                with sp.Fori(0, NT // (2 * G)) as i:
                    for b in range(2):
                        sp.wait_ge(scattered[b], i * (2 * G * 16))
                        sp.dma_start(xbuf[:, b], xn_dram.rearrange("(i b n p) d -> i b p n d", p=P, n=G, b=2)[bass.ds(i, 1)].rearrange("i b p n d -> b p (i n) d")[b]).then_inc(row_loaded[b], 16)

            @block.tensor
            def _(pe):
                pe.wait_ge(loaded, 5 * 16)
                for n in range(NT):
                    mm = pe.matmul(psL[:, n, :], lhsT=xT[:, n * P:(n + 1) * P], rhs=wr_s[:], start=True, stop=True)
                mm.then_inc(logits_ready, 1)
                pe.wait_ge(const_ready, 3)
                with pe.Fori(0, 31) as i:
                    pe.wait_ge(count_ready, i + 1)
                    pe.matmul(psC[:], lhsT=ones[:], rhs=cnt[:], start=True, stop=True).then_inc(count_summed, 1)
                for k, mask in enumerate((t, t)):
                    pe.wait_ge(mask_ready, k + 1)
                    pe.matmul(psA[:, 0, :], lhsT=lower[:], rhs=flat(mask[:]), start=True, stop=True)
                    pe.matmul(psA[:, 1, :], lhsT=ones[:], rhs=flat(mask[:]), start=True, stop=True).then_inc(mask_summed, 1)

            @block.scalar
            def _(act):
                act.wait_ge(diff_ready, 1)
                act.activation(w[:, 1, :], m[:, 2, :], ACT.Exp).then_inc(exp_ready, 1)

            @block.gpsimd
            def _(pool):
                pool.memset(zeros[:], 0.0).then_inc(const_ready, 1)
                pool.memset(ones[:], 1.0).then_inc(const_ready, 1)
                pool.memset(bit[:], 1 << 29).then_inc(const_ready, 1)
                pool.wait_ge(slots_zeroed, 16)
                with pool.Fori(0, NT // (2 * G)) as i:
                    for b in range(2):
                        pool.wait_ge(index_ready, i * 2 + b + 1)
                        pool.wait_ge(row_loaded[b], i * 16 + 16)
                        pool.sem_inc(scatter_begun, 1)
                        for n in range(G):
                            for k in range(2):
                                pool.indirect_dma_start(slots_dram, bass.IndirectOffsetOnAxis(ap=ibuf[:, b, k, n:n + 1], axis=0),
                                                        xbuf[:, b, n, :], None, bounds_check=NSLOT - 1, oob_is_err=False).then_inc(scattered[b], 16)
                for b in range(2):
                    pool.wait_ge(scattered[b], NT * 16)

            @block.vector
            def _(dve):
                done = [0]

                def link(ins):
                    done[0] += 1
                    ins.then_inc(step_done, 1)
                    dve.wait_ge(step_done, done[0])

                dve.wait_ge(loaded, 5 * 16)
                dve.wait_ge(logits_ready, 1)
                link(dve.memset(thr[:], 0))
                link(dve.tensor_tensor(lg[:], psL[:], over_n(br_s[:]), ALU.add))
                for k in range(2):
                    link(dve.tensor_reduce(m[:, k, :], lg[:], AX.X, ALU.max))
                    link(dve.tensor_tensor(t[:], lg[:], bcast(m[:, k, :], NE), ALU.not_equal))
                    link(dve.scalar_tensor_tensor(t[:], t[:], float(NE), over_n(iota[:]), ALU.mult, ALU.add))
                    link(dve.tensor_reduce(m[:, 2, :], t[:], AX.X, ALU.min))
                    link(dve.tensor_tensor(oh[:, k], over_n(iota[:]), bcast(m[:, 2, :], NE), ALU.is_equal))
                    if k == 0:
                        link(dve.scalar_tensor_tensor(lg[:], oh[:, 0], -3e38, lg[:], ALU.mult, ALU.add))
                dve.tensor_tensor(m[:, 2, :], m[:, 1, :], m[:, 0, :], ALU.subtract).then_inc(diff_ready, 1)
                dve.wait_ge(exp_ready, 1)
                link(dve.tensor_scalar(w[:, 2, :], w[:, 1, :], 1.0, None, ALU.add))
                link(dve.reciprocal(w[:, 0, :], w[:, 2, :]))
                link(dve.tensor_tensor(w[:, 1, :], w[:, 1, :], w[:, 0, :], ALU.mult))
                link(dve.tensor_tensor(key[:], oh[:, 0], bcast(w[:, 0, :], NE), ALU.mult))
                link(dve.tensor_tensor(t[:], oh[:, 1], bcast(w[:, 1, :], NE), ALU.mult))
                link(dve.tensor_tensor(key[:], key[:], t[:], ALU.add))
                link(dve.tensor_tensor(t[:], oh[:, 0], oh[:, 1], ALU.add))
                link(dve.scalar_tensor_tensor(key[:], t[:], -1.0, key[:], ALU.add, ALU.add))
                dve.wait_ge(const_ready, 3)
                dve.sem_clear(step_done)
                with dve.Fori(0, 30) as i:
                    done[0] = 0
                    link(dve.tensor_tensor(cand[:], thr[:], bit[:], ALU.bitwise_or))
                    link(dve.tensor_tensor(t[:], key[:], over_n(cand[:].bitcast(F32)), ALU.is_ge))
                    dve.tensor_reduce(cnt[:], by_e(t[:]), AX.X, ALU.add).then_inc(count_ready, 1)
                    dve.wait_ge(count_summed, i + 1)
                    link(dve.tensor_scalar(acc[:], psC[:], float(CAP), -1.0, ALU.is_ge, ALU.mult))
                    link(dve.tensor_tensor(acc[:], acc[:], bit[:], ALU.bitwise_and))
                    link(dve.tensor_tensor(thr[:], thr[:], acc[:], ALU.bitwise_or))
                    link(dve.tensor_scalar(bit[:], bit[:], 1, None, ALU.logical_shift_right))
                    dve.sem_clear(step_done)
                done[0] = 0
                thrf = over_n(thr[:].bitcast(F32))
                link(dve.tensor_tensor(gt[:], key[:], thrf, ALU.is_gt))
                dve.tensor_reduce(cnt[:], by_e(gt[:]), AX.X, ALU.add).then_inc(count_ready, 1)
                dve.wait_ge(count_summed, 31)
                link(dve.tensor_scalar(need[:], psC[:], -1.0, float(CAP), ALU.mult, ALU.add))
                dve.tensor_tensor(t[:], key[:], thrf, ALU.is_equal).then_inc(mask_ready, 1)

                def rank(k):
                    dve.wait_ge(mask_summed, k + 1)
                    link(dve.tensor_copy(flat(t2[:]), psA[:, 1, :]))
                    for e in range(NE):
                        link(dve.tensor_tensor_scan(base[:, :, e], ones[:, 0:NT], t2[:, :, e], 0.0, ALU.mult, ALU.add))
                    link(dve.tensor_tensor(base[:], base[:], t2[:], ALU.subtract))
                    link(dve.tensor_tensor(flat(base[:]), flat(base[:]), psA[:, 0, :], ALU.add))

                rank(0)
                link(dve.tensor_tensor(base[:], base[:], over_n(need[:]), ALU.is_lt))
                link(dve.tensor_tensor(t[:], t[:], base[:], ALU.mult))
                dve.tensor_tensor(t[:], t[:], gt[:], ALU.add).then_inc(mask_ready, 1)
                link(dve.tensor_scalar(first[:], iota[:], float(CAP), None, ALU.mult))
                rank(1)
                link(dve.tensor_tensor(base[:], base[:], over_n(first[:]), ALU.add))
                for k in range(2):
                    link(dve.tensor_tensor(t2[:], oh[:, k], t[:], ALU.mult))
                    link(dve.tensor_reduce(kept[:, k, :], t2[:], AX.X, ALU.add))
                    link(dve.tensor_tensor(t2[:], t2[:], base[:], ALU.mult))
                    link(dve.tensor_reduce(dest[:, k, :], t2[:], AX.X, ALU.add))
                    link(dve.tensor_tensor(gate[:, k, :], w[:, k, :], kept[:, k, :], ALU.mult))
                link(dve.tensor_scalar(kept[:], kept[:], -float(NSLOT), float(NSLOT), ALU.mult, ALU.add))
                link(dve.tensor_tensor(pos[:], dest[:], kept[:], ALU.add))
                dve.sem_clear(step_done)
                with dve.Fori(0, NT // (2 * G)) as i:
                    for b in range(2):
                        dve.wait_ge(scattered[b], i * (2 * G * 16))
                        dve.tensor_copy(ibuf[:, b], pos[:, :, bass.ds(i * (2 * G) + b * G, G)]).then_inc(index_ready, 1)


def moe_experts(nc, slots_dram, y_dram, w1, b1, w2, b2, ident_in):
    NS, HC = CAP // P, CAP // 2
    with ExitStack() as ctx:
        sb, ps, sem = makers(nc, ctx, "e")
        ident = sb("ident", [P, P])
        xs, xT = sb("xs", [P, 2, NS, DM]), sb("xT", [P, CAP])
        w1s, w2s = sb("w1", [P, 2, FF]), sb("w2", [P, 2, FF // P, DM])
        b1s, b2s = sb("b1", [P, 2, FF // P]), sb("b2", [P, 2, DM])
        hT, ys = sb("hT", [P, FF // P, CAP]), sb("ys", [P, 2, NS, DM])
        psT, psH, psY = ps("psT", [P, 2, 512]), ps("psH", [P, 4, 512]), ps("psY", [P, 2, 512])
        ident_loaded, loaded = sem("ident_loaded"), [sem("loaded0"), sem("loaded1")]
        turned, turned_out = sem("turned"), sem("turned_out")
        h_ready, gelu_ready, y_summed, y_ready = sem("h_ready"), sem("gelu_ready"), sem("y_summed"), sem("y_ready")
        stored = [sem("stored0"), sem("stored1")]
        at = lambda n: (n // 4 if n < 4 else 1, (n % 4) * P)
        with nc.Block() as block:
            @block.sync
            def _(sp):
                sp.dma_start(ident[:], ident_in).then_inc(ident_loaded, 16)
                with sp.Fori(0, NE // 2) as i:
                    for b in range(2):
                        sp.wait_ge(y_summed, i * 2 + b)
                        one = lambda a: a.rearrange("(i b) ... -> i b ...", b=2)[bass.ds(i, 1)]
                        sp.dma_start(xs[:, b], slots_dram.rearrange("(i b n p) d -> i b p n d", b=2, n=NS, p=P)[bass.ds(i, 1)].rearrange("i b p n d -> b p (i n) d")[b]).then_inc(loaded[b], 16)
                        sp.dma_start(w1s[:, b], w1.rearrange("(i b) p f -> i b p f", b=2)[bass.ds(i, 1)].rearrange("i b p f -> b p (i f)")[b]).then_inc(loaded[b], 16)
                        sp.dma_start(w2s[:, b], w2.rearrange("(i b) (c p) f -> i b p c f", b=2, p=P)[bass.ds(i, 1)].rearrange("i b p c f -> b p (i c) f")[b]).then_inc(loaded[b], 16)
                        sp.dma_start(b1s[:, b], b1.rearrange("(i b) p c -> i b p c", b=2)[bass.ds(i, 1)].rearrange("i b p c -> b p (i c)")[b]).then_inc(loaded[b], 16)
                        sp.dma_start(b2s[:, b], b2.rearrange("(i b) f -> i b f", b=2)[bass.ds(i, 1)].rearrange("i b f -> b i f")[b].broadcast_to([P, DM])).then_inc(loaded[b], 16)

            @block.tensor
            def _(pe):
                pe.wait_ge(ident_loaded, 16)
                with pe.Fori(0, NE // 2) as i:
                    for b in range(2):
                        pe.wait_ge(loaded[b], i * 80 + 80)
                        pe.wait_ge(turned_out, (i * 2 + b) * 2)
                        for n in range(NS):
                            g, c = n // 4, n % 4 * P
                            mm = pe.transpose(psT[:, g, c:c + P], xs[:, b, n, :], ident[:])
                        mm.then_inc(turned, 1)
                        pe.wait_ge(turned_out, (i * 2 + b) * 2 + 2)
                        for f in range(FF // P):
                            for q in range(2):
                                k = 2 * f + q
                                pe.wait_ge(gelu_ready, (i * 2 + b) * 8 + k + 1)
                                pe.matmul(psH[:, k % 4, 0:HC], lhsT=w1s[:, b, f * P:(f + 1) * P], rhs=xT[:, q * HC:(q + 1) * HC],
                                          start=True, stop=True).then_inc(h_ready, 1)
                        pe.wait_ge(gelu_ready, (i * 2 + b) * 8 + 8 + 4)
                        pe.wait_ge(y_ready, (i * 2 + b) * 2)
                        for n in range(NS):
                            g, c = n // 4, n % 4 * P
                            for f in range(FF // P):
                                mm = pe.matmul(psY[:, g, c:c + P], lhsT=hT[:, f, n * P:(n + 1) * P], rhs=w2s[:, b, f, :],
                                               start=f == 0, stop=f == FF // P - 1)
                        mm.then_inc(y_summed, 1)

            @block.scalar
            def _(act):
                act.sem_inc(gelu_ready, 4)
                with act.Fori(0, NE // 2) as i:
                    for b in range(2):
                        act.wait_ge(turned, i * 2 + b + 1)
                        act.activation(xT[:, 0:512], psT[:, 0, :], ACT.Copy).then_inc(turned_out, 1)
                        act.activation(xT[:, 512:CAP], psT[:, 1, 0:CAP - 512], ACT.Copy).then_inc(turned_out, 1)
                        act.wait_ge(y_summed, i * 2 + b)
                        for f in range(FF // P):
                            for q in range(2):
                                k = 2 * f + q
                                act.wait_ge(h_ready, (i * 2 + b) * 8 + k + 1)
                                act.activation(hT[:, f, q * HC:(q + 1) * HC], psH[:, k % 4, 0:HC], ACT.Gelu,
                                               bias=b1s[:, b, f:f + 1]).then_inc(gelu_ready, 1)

            @block.vector
            def _(dve):
                with dve.Fori(0, NE // 2) as i:
                    for b in range(2):
                        dve.wait_ge(y_summed, i * 2 + b + 1)
                        dve.wait_ge(stored[b], i * 16)
                        dve.tensor_tensor(ys[:, b, 0:4, :], psY[:, 0, :].rearrange("p (n d) -> p n d", n=4),
                                          b2s[:, b, :].unsqueeze(1).broadcast_to([P, 4, DM]), ALU.add).then_inc(y_ready, 1)
                        dve.tensor_tensor(ys[:, b, 4, :], psY[:, 1, 0:P], b2s[:, b, :], ALU.add).then_inc(y_ready, 1)

            @block.gpsimd
            def _(pool):
                with pool.Fori(0, NE // 2) as i:
                    for b in range(2):
                        pool.wait_ge(y_ready, (i * 2 + b) * 2 + 2)
                        pool.dma_start(y_dram.rearrange("(i b n p) d -> i b p n d", b=2, n=NS, p=P)[bass.ds(i, 1)].rearrange("i b p n d -> b p (i n) d")[b], ys[:, b]).then_inc(stored[b], 16)
                for b in range(2):
                    pool.wait_ge(stored[b], 16 * (NE // 2))


def moe_combine(nc, xn_dram, y_dram, x1_dram, x1_out, xn2_dram, xn2T_dram, gamma, beta, ident_in, pos, gate):
    G = 4
    with ExitStack() as ctx:
        sb, ps, sem = makers(nc, ctx, "c")
        F_, X1, SQ = sb("F", [P, NT, DM]), sb("X1", [P, NT, DM]), sb("SQ", [P, NT, DM])
        XT = sb("XT", [P, NTOK])
        gam, bet, ident = sb("gam", [P, DM]), sb("bet", [P, DM]), sb("ident", [P, P])
        yb, ib = sb("yb", [P, 2, 2, G, DM]), sb("ib", [P, 2, 2, G], I32)
        posg = sb("posg", [P, 2, NT], I32)
        gz = sb("gz", [P, 2, NT])
        stat = sb("stat", [P, 4, NT])
        psT = ps("psT", [P, 4, 512])
        loaded, index_ready, gathered, used = sem("loaded"), sem("index_ready"), [sem("gathered0"), sem("gathered1")], sem("used")
        var_ready, std_ready, xn_ready, x1_ready = sem("var_ready"), sem("std_ready"), sem("xn_ready"), sem("x1_ready")
        turned, evicted, stored, step_done = sem("turned"), sem("evicted"), sem("stored"), sem("step_done")
        gather_begun = sem("gather_begun")
        tok = lambda a: a.rearrange("(n p) d -> p n d", p=P)
        row = lambda a: a.rearrange("(o d) -> o d", o=1).broadcast_to([P, DM])
        with nc.Block() as block:
            @block.sync
            def _(sp):
                for dst, src in ((F_[:], tok(xn_dram)), (X1[:], tok(x1_dram)), (gam[:], row(gamma)), (bet[:], row(beta)), (ident[:], ident_in)):
                    sp.dma_start(dst, src).then_inc(loaded, 16)
                sp.wait_ge(x1_ready, 1)
                sp.dma_start(tok(x1_out), X1[:]).then_inc(stored, 16)
                sp.wait_ge(xn_ready, 1)
                sp.dma_start(tok(xn2_dram), F_[:]).then_inc(stored, 16)
                sp.wait_ge(evicted, NT // 4)
                sp.dma_start(xn2T_dram, XT[:]).then_inc(stored, 16)
                sp.wait_ge(stored, 48)

            @block.gpsimd
            def _(pool):
                with pool.Fori(0, NT // (2 * G)) as i:
                    for b in range(2):
                        pool.wait_ge(index_ready, i * 2 + b + 1)
                        pool.sem_inc(gather_begun, 1)
                        for n in range(G):
                            for k in range(2):
                                pool.indirect_dma_start(yb[:, b, k, n, :], None, y_dram, bass.IndirectOffsetOnAxis(ap=ib[:, b, k, n:n + 1], axis=0)).then_inc(gathered[b], 16)

            @block.vector
            def _(dve):
                done = [0]

                def link(ins):
                    done[0] += 1
                    ins.then_inc(step_done, 1)
                    dve.wait_ge(step_done, done[0])

                link(dve.tensor_scalar(gz[:], pos[:], float(NSLOT), None, ALU.is_lt))
                link(dve.tensor_tensor(posg[:], pos[:], gz[:], ALU.mult))
                dve.wait_ge(loaded, 16 * 5)
                dve.sem_clear(step_done)
                for b in range(2):
                    dve.tensor_copy(ib[:, b], posg[:, :, b * G:(b + 1) * G]).then_inc(index_ready, 1)
                with dve.Fori(0, NT // (2 * G)) as i:
                    done[0] = 0
                    for b in range(2):
                        dve.wait_ge(gathered[b], i * (2 * G * 16) + 2 * G * 16)
                        fs = F_[:, bass.ds(i * (2 * G) + b * G, G), :]
                        for k in range(2):
                            g = gate[:, k, bass.ds(i * (2 * G) + b * G, G)].unsqueeze(2).broadcast_to([P, G, DM])
                            link(dve.tensor_tensor(yb[:, b, k], yb[:, b, k], g, ALU.mult))
                            link(dve.tensor_tensor(fs, fs, yb[:, b, k], ALU.add))
                        dve.tensor_copy(ib[:, b], posg[:, :, bass.ds((i * (2 * G) + b * G + 2 * G) % NT, G)]).then_inc(index_ready, 1)
                    dve.sem_clear(step_done)
                done[0] = 0

                def norm(v, k):
                    link(dve.tensor_reduce(stat[:, 0, :], v, AX.X, ALU.add))
                    link(dve.tensor_scalar(stat[:, 0, :], stat[:, 0, :], 1.0 / DM, None, ALU.mult))
                    link(dve.tensor_tensor(v, v, bcast(stat[:, 0, :], DM), ALU.subtract))
                    link(dve.tensor_tensor(SQ[:], v, v, ALU.mult))
                    link(dve.tensor_reduce(stat[:, 1, :], SQ[:], AX.X, ALU.add))
                    dve.tensor_scalar(stat[:, 1, :], stat[:, 1, :], 1.0 / DM, EPS, ALU.mult, ALU.add).then_inc(var_ready, 1)
                    dve.wait_ge(std_ready, k)
                    link(dve.reciprocal(stat[:, 3, :], stat[:, 2, :]))
                    return dve.tensor_tensor(v, v, bcast(stat[:, 3, :], DM), ALU.mult)

                link(norm(F_[:], 1))
                link(dve.tensor_tensor(F_[:], F_[:], gam[:].unsqueeze(1).broadcast_to([P, NT, DM]), ALU.mult))
                link(dve.tensor_tensor(F_[:], F_[:], bet[:].unsqueeze(1).broadcast_to([P, NT, DM]), ALU.add))
                dve.tensor_tensor(X1[:], X1[:], F_[:], ALU.add).then_inc(x1_ready, 1)
                dve.wait_ge(x1_ready, 1)
                link(dve.tensor_copy(F_[:], X1[:]))
                norm(F_[:], 2).then_inc(xn_ready, 1)

            @block.scalar
            def _(act):
                for k in range(2):
                    act.wait_ge(var_ready, k + 1)
                    act.activation(stat[:, 2, :], stat[:, 1, :], ACT.Sqrt).then_inc(std_ready, 1)
                for g in range(NT // 4):
                    act.wait_ge(turned, g + 1)
                    act.activation(XT[:, g * 512:(g + 1) * 512], psT[:, g % 4, :], ACT.Copy).then_inc(evicted, 1)

            @block.tensor
            def _(pe):
                pe.wait_ge(loaded, 16 * 5)
                pe.wait_ge(xn_ready, 1)
                for g in range(NT // 4):
                    if g >= 4:
                        pe.wait_ge(evicted, g - 3)
                    for k in range(4):
                        mm = pe.transpose(psT[:, g % 4, k * P:(k + 1) * P], F_[:, 4 * g + k, :], ident[:])
                    mm.then_inc(turned, 1)
def layer1(nc, xn2_dram, xn2T_dram, x1_dram, out_dram, wqkv, wb, cw_in, wo, grms, lng, lnb, wgu, wd, ident_in, levels_in, masks_in):
    NPAIR, ROW, G = B // 2, 2 * L, 4
    NL = NLEV - 1
    SLOTS = 2 * (NL + 2)
    with ExitStack() as ctx:
        sb, ps, sem = makers(nc, ctx, "a")
        wqkv_s, wb_s, cw, wo_s = sb("wqkv", [P, 3, P]), sb("wb", [P, AH]), sb("cw", [P, 3, 4]), sb("wo", [P, P])
        grms_s, lng_s, lnb_s, ident = sb("grms", [P, AD]), sb("lng", [P, DM]), sb("lnb", [P, DM]), sb("ident", [P, P])
        lev = sb("lev", [P, 2, NLEV, P])
        masks = sb("masks", [P, 2, P])
        xT, xres, acc = sb("xT", [P, ROW]), sb("xres", [P, G, DM]), sb("acc", [P, G, DM])
        pad, qkv = sb("pad", [P, 3, 2, 3 + L]), sb("qkv", [P, 3, ROW])
        beta = sb("beta", [P, 2, G, AH])
        tok = sb("tok", [P, G, 4, P])
        sq, ss = sb("sq", [P, G, 2, P]), sb("ss", [P, G, 2, AH])
        fm = sb("fm", [P, G, 3, P])
        late = sb("late", [P, 2, 3, P])
        bd = sb("bd", [P, 2, 2, 3, AH, P])
        M, X, XT, QT = (sb(n, [P, 2, AH, P]) for n in ("M", "X", "XT", "QT"))
        PT = sb("PT", [P, 2, AH, P])
        R, D, S = sb("R", [P, 2, P]), sb("D", [P, 2, P]), sb("S", [P, 2, P])
        o, oT, osq = sb("o", [P, G, P]), sb("oT", [P, G, P]), sb("osq", [P, G, P])
        rs, st = sb("rs", [P, 2, 16]), sb("st", [P, 4, G])
        wgu_s, wd_s = sb("wgu", [P, 6, DM]), sb("wd", [P, FI])
        wguT, wdT = sb("wguT", [P, 2, FI]), sb("wdT", [P, 3, DM])
        x, xq, xqT = sb("x", [P, G, DM]), sb("xq", [P, G, DM]), sb("xqT", [P, G * P])
        g, h, hqT = sb("g", [P, 2, FI]), sb("h", [P, G, FI]), sb("hqT", [P, G, 3, P])
        NMAX = G * FI
        a, lo, hi = sb("a", [P, NMAX]), sb("lo", [P, NMAX]), sb("hi", [P, NMAX])
        hq = a
        scale, rscale = sb("scale", [P, NMAX // QB]), sb("rscale", [P, NMAX // QB])
        bank = ps("bank", [P, 8, 512])
        names = """consts_loaded pads_zeroed xT_loaded xres_loaded acc_loaded x_loaded stored
            gram_ready m_out pt_out x_ready q_ready q_out xx_ready x_reset level_begun ks_ready r_ready d_ready d_out
            o_ready o_out s_ready s_out
            rms_sq rms_root on_ready oT_ready oT_out y_ready y_out var_ready std_ready res_added
            xq_ready xqT_ready xqT_out gu_ready g_out h_out hq_ready hT_ready hT_out down_ready down_out
            proj_ready proj_out beta_ready beta_out conv_ready silu_ready tok_ready tok_out norm_sq norm_root keys_ready
            fm_ready fm_out bd_out late_out wq_ready wT_ready wT_out dve_step""".split()
        s_ = {n: sem(n) for n in names}
        row = lambda t: t.rearrange("(o d) -> o d", o=1)
        pair = lambda t, i: t.rearrange("(i n p) d -> i p n d", p=P, n=G)[bass.ds(i, 1)].rearrange("i p n d -> p (i n) d")
        flat = lambda t: t.rearrange("p h t -> p (h t)")
        h4 = lambda k: bank[:, k, :].rearrange("p (h t) -> p h t", h=AH)
        over_h = lambda t: t.unsqueeze(1).broadcast_to([P, AH, P])
        over_n = lambda t: t.unsqueeze(1).broadcast_to([P, G, DM])
        A, C = (0, 2), (1, 3)
        at = lambda i, ck, s: (i * 2 + ck) * 2 + s

        with nc.Block() as block:
            @block.sync
            def _(sp):
                sp.wait_ge(s_["pads_zeroed"], 1)
                for dst, src in ((wqkv_s[:], wqkv), (wb_s[:], wb), (cw[:], cw_in), (wo_s[:], wo), (ident[:], ident_in),
                                 (grms_s[:], row(grms).broadcast_to([P, AD])), (lng_s[:], row(lng).broadcast_to([P, DM])),
                                 (lnb_s[:], row(lnb).broadcast_to([P, DM])), (lev[:], levels_in), (masks[:], masks_in), (wd_s[:], wd)):
                    sp.dma_start(dst, src).then_inc(s_["consts_loaded"], 16)
                for k in range(2):
                    for c, (c0, n) in enumerate(FCH):
                        sp.dma_start(wgu_s[0:n, 3 * k + c, :], wgu[k, c0:c0 + n, :]).then_inc(s_["consts_loaded"], 16)

                def turn(i, has_last, has_next):
                    if has_next:
                        sp.wait_ge(s_["beta_ready"], i + 1)
                        sp.dma_start(xT[:], xn2T_dram[:, bass.ds((i + 1) * ROW, ROW)]).then_inc(s_["xT_loaded"], 16)
                    if has_last:
                        sp.dma_start(xres[:], pair(xn2_dram, i - 1)).then_inc(s_["xres_loaded"], 16)
                    sp.wait_ge(s_["xq_ready"], i)
                    sp.dma_start(x[:], pair(xn2_dram, i)).then_inc(s_["x_loaded"], 16)
                    if has_last:
                        sp.wait_ge(s_["res_added"], i)
                        sp.dma_start(pair(out_dram, i - 1), acc[:]).then_inc(s_["stored"], 16)
                        sp.wait_ge(s_["stored"], i * 16)
                    sp.dma_start(acc[:], pair(x1_dram, i)).then_inc(s_["acc_loaded"], 16)

                sp.dma_start(xT[:], xn2T_dram[:, 0:ROW]).then_inc(s_["xT_loaded"], 16)
                turn(0, False, True)
                with sp.Fori(1, NPAIR - 1) as i:
                    turn(i, True, True)
                turn(NPAIR - 1, True, False)
                sp.wait_ge(s_["res_added"], NPAIR - 1)
                sp.dma_start(xres[:], pair(xn2_dram, NPAIR - 1)).then_inc(s_["xres_loaded"], 16)
                sp.wait_ge(s_["res_added"], NPAIR)
                sp.dma_start(pair(out_dram, NPAIR - 1), acc[:]).then_inc(s_["stored"], 16)
                sp.wait_ge(s_["stored"], NPAIR * 16)

            @block.gpsimd
            def _(pool):
                pool.memset(pad[:, :, :, 0:3], 0.0)
                pool.memset(wgu_s[:], 0.0).then_inc(s_["pads_zeroed"], 1)

            @block.tensor
            def _(pe):
                def wait(name, n):
                    pe.wait_ge(s_[name], n)

                def mm(out, lhsT, rhs, start=True, stop=True, **kw):
                    return pe.matmul(out, lhsT=lhsT, rhs=rhs, start=start, stop=stop, **kw)

                def main(i, slot):
                    ck, k = divmod(slot, NL + 2)
                    if k == 0:
                        wait("bd_out", i * 2 + ck + 1)
                        wait("fm_out", i * 4 + 4)
                        wait("o_out", at(i, ck, 0))
                        wait("s_out", i * 2 + 2 * ck)
                        for s in range(2):
                            n = 2 * s + ck
                            mm(bank[:, A[s], :], fm[:, n, 2, :], flat(bd[:, ck, s, 1]))
                            mm(bank[:, C[s], :], fm[:, n, 1, :], flat(bd[:, ck, s, 2])).then_inc(s_["gram_ready"], 1)
                        if ck == 0:
                            wait("down_out", i)
                        else:
                            wait("proj_out", i * 3 + 6) if not last else wait("hT_out", i * 4)
                        for s in range(2):
                            n = 2 * s + ck
                            mm(bank[:, 4 + s, :], fm[:, n, 1, :], flat(bd[:, ck, s, 0])).then_inc(s_["gram_ready"], 1)
                    elif k <= NL:
                        l = k - 1
                        for s in range(2):
                            wait("x_ready", at(i, ck, 0) * (NL + 1) + 2 * l + s + 1)
                            if l == 0:
                                wait("m_out", at(i, ck, s) + 1)
                            for hd in range(AH):
                                ins = mm(bank[:, A[s], hd * P:(hd + 1) * P], M[:, s, hd, :], XT[:, s, hd, :])
                            ins.then_inc(s_["q_ready"], 1)
                        for s in range(2):
                            wait("q_out", at(i, ck, 0) * NL + 2 * l + s + 1)
                            if l < NL - 1:
                                for hd in range(AH):
                                    mm(bank[:, A[s], hd * P:(hd + 1) * P], QT[:, s, hd, :], X[:, s, hd, :])
                            for hd in range(AH):
                                ins = mm(bank[:, C[s], hd * P:(hd + 1) * P], X[:, s, hd, :], QT[:, s, hd, :])
                            ins.then_inc(s_["xx_ready"], 1)
                    else:
                        if ck == 1:
                            wait("late_out", i + 1)
                            wait("s_out", i * 2 + 2)
                            for s in range(2):
                                mm(bank[:, A[s], 0:P], late[:, s, 1, :], S[:, s, :]).then_inc(s_["ks_ready"], 1)
                        for s in range(2):
                            wait("r_ready", at(i, ck, s) + 1)
                            wait("x_ready", at(i, ck, 0) * (NL + 1) + 2 * NL + s + 1)
                            for hd in range(AH):
                                ins = mm(bank[:, C[s], hd * AD:(hd + 1) * AD], XT[:, s, hd, :], R[:, s, hd * AD:(hd + 1) * AD])
                            ins.then_inc(s_["d_ready"], 1)
                        wait("pt_out", at(i, ck, 0) + 2)
                        for s in range(2):
                            n = 2 * s + ck
                            wait("d_out", at(i, ck, s) + 1)
                            if ck == 1:
                                mm(bank[:, A[s], P:2 * P], late[:, s, 0, :], S[:, s, :], stop=False, skip_group_check=True)
                            for hd in range(AH):
                                ins = mm(bank[:, A[s], P + hd * AD:P + (hd + 1) * AD], PT[:, s, hd, :], D[:, s, hd * AD:(hd + 1) * AD],
                                         start=ck == 0, skip_group_check=ck == 1)
                            ins.then_inc(s_["o_ready"], 1)
                            if ck == 0:
                                mm(bank[:, C[s], P:2 * P], tok[:, n, 1, :], D[:, s, :]).then_inc(s_["s_ready"], 1)

                def tail(i, slot):
                    if slot == 2:
                        wait("on_ready", i + 1)
                        for n in range(G):
                            ins = pe.transpose(bank[:, 6, n * P:(n + 1) * P], o[:, n, :], ident[:])
                        ins.then_inc(s_["oT_ready"], 1)
                    if slot == 3:
                        wait("oT_out", i + 1)
                        for n in range(G):
                            ins = mm(bank[:, 7, n * P:(n + 1) * P], oT[:, n, :], wo_s[:])
                        ins.then_inc(s_["y_ready"], 1)

                def feed(i, slot):
                    if slot == 4:
                        wait("xq_ready", i + 1)
                        for n in range(G):
                            ins = pe.transpose(bank[:, 6, n * P:(n + 1) * P], xq[:, n, :], ident[:])
                        ins.then_inc(s_["xqT_ready"], 1)
                    if slot in (5, 6):
                        wait("xqT_out", i + 1)
                        wait("pt_out", at(i, 0, 0) + 2)
                        wait("y_out", i)
                        for n in range(2 * (slot - 5), 2 * (slot - 5) + 2):
                            wait("h_out", i * G + (n - 2 if n > 1 else 0) + (1 if n > 1 else 0))
                            for k in range(2):
                                ins = mm(bank[:, 4 + 2 * (n % 2) + k, 0:FI], xqT[:, n * P:(n + 1) * P], wguT[:, k, :])
                            ins.then_inc(s_["gu_ready"], 1)
                    if slot == 12:
                        wait("hq_ready", i + 1)
                        if not last:
                            wait("tok_out", (i + 1) * 4 + 4)
                        wait("pt_out", at(i, 1, 0) + 2)
                        for n in range(G):
                            for c, (c0, m) in enumerate(FCH):
                                ins = pe.transpose(bank[0:m, 4 + n, c * P:(c + 1) * P], hq[:, n * FI + c0:n * FI + c0 + m], ident[:])
                            ins.then_inc(s_["hT_ready"], 1)
                    if slot == 13:
                        for n in range(G):
                            wait("hT_out", G * i + n + 1)
                            for c, (c0, m) in enumerate(FCH):
                                ins = mm(bank[:, 4, n * P:(n + 1) * P], hqT[0:m, n, c, :], wdT[0:m, c, :], start=c == 0, stop=c == 2)
                        ins.then_inc(s_["down_ready"], 1)

                def head(i, slot, alone=False):
                    if slot == 7:
                        wait("xT_loaded", 16 * i + 16)
                        if not alone:
                            wait("h_out", i * G)
                        for j in range(3):
                            mm(bank[:, 4 + j, :], wqkv_s[:, j, :], xT[:]).then_inc(s_["proj_ready"], 1)
                        for n in range(G):
                            ins = mm(bank[:, 7, n * AH:(n + 1) * AH], xT[:, n * P:(n + 1) * P], wb_s[:])
                        ins.then_inc(s_["beta_ready"], 1)
                    if slot == 11:
                        wait("silu_ready", 3 * i + 3)
                        wait("beta_out", 2 * i + 1)
                        if not alone:
                            wait("pt_out", at(i, 0, 0))
                        for n in range(G):
                            for j in range(3):
                                ins = pe.transpose(bank[:, 4 + n, j * P:(j + 1) * P], qkv[:, j, n * P:(n + 1) * P], ident[:])
                            ins.then_inc(s_["tok_ready"], 1)
                    if slot == 14:
                        wait("keys_ready", i + 1)
                        if not alone:
                            wait("down_out", i)
                        for n in range(G):
                            for j, src in enumerate((0, 1, 3)):
                                ins = pe.transpose(bank[:, 4 + n, j * P:(j + 1) * P], tok[:, n, src, :], ident[:])
                            ins.then_inc(s_["fm_ready"], 1)

                last = False
                wait("consts_loaded", 17 * 16)
                wait("pads_zeroed", 1)
                wait("wq_ready", 2)
                wguq = a[:, 0:6 * DM].rearrange("p (k d) -> p k d", k=6)
                for k in range(2):
                    for c, (c0, n) in enumerate(FCH):
                        pe.transpose(bank[:, k, c0:c0 + n], wguq[0:n, 3 * k + c, :], ident[0:n, 0:n])
                for c, (c0, n) in enumerate(FCH):
                    ins = pe.transpose(bank[0:n, 2, c * P:(c + 1) * P], a[:, 6 * DM + c0:6 * DM + c0 + n], ident[:])
                ins.then_inc(s_["wT_ready"], 1)
                wait("wT_out", 5)
                for slot in range(SLOTS):
                    head(0, slot, alone=True)

                def turn(i, has_last, has_next):
                    for slot in range(SLOTS):
                        main(i, slot)
                        if has_last:
                            tail(i - 1, slot)
                        feed(i, slot)
                        if has_next:
                            head(i + 1, slot)

                turn(0, False, True)
                with pe.Fori(1, NPAIR - 1) as i:
                    turn(i, True, True)
                last = True
                turn(NPAIR - 1, True, False)
                for slot in range(SLOTS):
                    tail(NPAIR - 1, slot)

            @block.scalar
            def _(act):
                def wait(name, n):
                    act.wait_ge(s_[name], n)

                def copy(out, in_):
                    return act.activation(out, in_, ACT.Copy)

                def reset(s):
                    copy(X[:, s], over_h(ident[:]))
                    copy(XT[:, s], over_h(ident[:])).then_inc(s_["x_reset"], 1)

                def main(i, slot):
                    ck, k = divmod(slot, NL + 2)
                    if k == 0:
                        for s in range(2):
                            wait("gram_ready", at(i, ck, 0) * 2 + s + 1)
                            copy(M[:, s], h4(A[s])).then_inc(s_["m_out"], 1)
                    elif k <= NL:
                        for s in range(2):
                            wait("q_ready", at(i, ck, 0) * NL + 2 * (k - 1) + s + 1)
                            copy(QT[:, s], h4(A[s])).then_inc(s_["q_out"], 1)
                    else:
                        for s in range(2):
                            wait("d_ready", at(i, ck, s) + 1)
                            copy(D[:, s, :], bank[:, C[s], 0:P]).then_inc(s_["d_out"], 1)
                        for s in range(2):
                            reset(s)
                        for s in range(2):
                            wait("o_ready", at(i, ck, s) + 1)
                            copy(o[:, 2 * s + ck, :], bank[:, A[s], P:2 * P]).then_inc(s_["o_out"], 1)

                def tail(i, slot):
                    if slot == 0:
                        wait("rms_sq", i + 1)
                        act.activation(rs[:, 1, :], rs[:, 0, :], ACT.Sqrt).then_inc(s_["rms_root"], 1)
                    if slot == 2:
                        wait("oT_ready", i + 1)
                        copy(oT[:], bank[:, 6, :].rearrange("p (n t) -> p n t", n=G)).then_inc(s_["oT_out"], 1)
                    if slot == 4:
                        wait("var_ready", i + 1)
                        act.activation(st[:, 2, :], st[:, 1, :], ACT.Sqrt).then_inc(s_["std_ready"], 1)

                def feed(i, slot):
                    if slot == 4:
                        wait("xqT_ready", i + 1)
                        copy(xqT[:], bank[:, 6, :]).then_inc(s_["xqT_out"], 1)
                    if slot in (5, 6):
                        for n in range(2 * (slot - 5), 2 * (slot - 5) + 2):
                            wait("gu_ready", G * i + n + 1)
                            if n > 1:
                                wait("h_out", G * i + n - 1)
                            act.activation(g[:, n % 2, :], bank[:, 4 + 2 * (n % 2), 0:FI], ACT.Silu).then_inc(s_["g_out"], 1)
                    if slot == 12:
                        for n in range(G):
                            wait("hT_ready", G * i + n + 1)
                            copy(hqT[:, n, 0:2, :], bank[:, 4 + n, 0:2 * P].rearrange("p (c t) -> p c t", c=2))
                            copy(hqT[0:96, n, 2, :], bank[0:96, 4 + n, 2 * P:3 * P]).then_inc(s_["hT_out"], 1)

                def head(i, slot):
                    if slot == 7:
                        wait("conv_ready", 3 * i)
                        for j in range(3):
                            wait("proj_ready", 3 * i + j + 1)
                            copy(pad[:, j, :, 3:], bank[:, 4 + j, :].rearrange("p (s l) -> p s l", s=2)).then_inc(s_["proj_out"], 1)
                        wait("beta_ready", i + 1)
                        wait("keys_ready", i)
                        act.activation(beta[:, 0].rearrange("p n h -> p (n h)"), bank[:, 7, 0:4 * AH], ACT.Sigmoid).then_inc(s_["beta_out"], 1)
                        wait("beta_out", 2 * i + 1)
                        act.activation(beta[:, 1], beta[:, 0], ACT.Copy, scale=-1.0).then_inc(s_["beta_out"], 1)
                    if slot == 10:
                        for j in range(3):
                            wait("conv_ready", 3 * i + j + 1)
                            act.activation(qkv[:, j, :], qkv[:, j, :], ACT.Silu).then_inc(s_["silu_ready"], 1)
                    if slot == 11:
                        for n in range(G):
                            wait("tok_ready", 4 * i + n + 1)
                            if n == 0:
                                wait("late_out", i)
                            copy(tok[:, n, 0:3, :], bank[:, 4 + n, 0:3 * P].rearrange("p (j t) -> p j t", j=3)).then_inc(s_["tok_out"], 1)
                    if slot == 12:
                        wait("norm_sq", i + 1)
                        act.activation(ss[:], ss[:], ACT.Sqrt).then_inc(s_["norm_root"], 1)
                    if slot == 14:
                        for n in range(G):
                            wait("fm_ready", 4 * i + n + 1)
                            copy(fm[:, n, :, :], bank[:, 4 + n, 0:3 * P].rearrange("p (j t) -> p j t", j=3)).then_inc(s_["fm_out"], 1)

                def turn(i, has_last, has_next):
                    for slot in range(SLOTS):
                        main(i, slot)
                        if has_last:
                            tail(i - 1, slot)
                        feed(i, slot)
                        if has_next:
                            head(i + 1, slot)

                wait("pads_zeroed", 1)
                wait("consts_loaded", 17 * 16)
                for s in range(2):
                    reset(s)
                wait("wT_ready", 1)
                for k in range(2):
                    copy(wguT[:, k, :], bank[:, k, 0:FI]).then_inc(s_["wT_out"], 1)
                for c, (c0, n) in enumerate(FCH):
                    copy(wdT[0:n, c, :], bank[0:n, 2, c * P:(c + 1) * P]).then_inc(s_["wT_out"], 1)
                for slot in range(SLOTS):
                    head(0, slot)
                turn(0, False, True)
                with act.Fori(1, NPAIR - 1) as i:
                    turn(i, True, True)
                turn(NPAIR - 1, True, False)
                for slot in range(SLOTS):
                    tail(NPAIR - 1, slot)

            @block.vector
            def _(dve):
                done = [0]

                def wait(name, n):
                    dve.wait_ge(s_[name], n)

                def link(ins):
                    done[0] += 1
                    ins.then_inc(s_["dve_step"], 1)
                    dve.wait_ge(s_["dve_step"], done[0])

                def clear():
                    dve.sem_clear(s_["dve_step"])
                    done[0] = 0

                mask = lambda t, l: over_h(lev[:, t, l, :]).bitcast(I32)

                def main(i, slot):
                    ck, k = divmod(slot, NL + 2)
                    if k == 0:
                        for s in range(2):
                            wait("m_out", at(i, ck, s) + 1)
                            wait("x_reset", at(i, ck, s) + 1)
                            dve.sem_inc(s_["level_begun"], 1)
                            dve.copy_predicated(X[:, s], mask(0, 0), M[:, s])
                            dve.copy_predicated(XT[:, s], mask(1, 0), h4(C[s])).then_inc(s_["x_ready"], 1)
                        wait("o_ready", at(i, ck, 0))
                        for s in range(2):
                            wait("gram_ready", at(i, ck, 0) * 2 + 2 + s + 1)
                            dve.tensor_tensor(PT[:, s], h4(4 + s), over_h(masks[:, 0, :]), ALU.mult).then_inc(s_["pt_out"], 1)
                    elif k <= NL:
                        l = k - 1
                        for s in range(2):
                            wait("xx_ready", at(i, ck, 0) * NL + 2 * l + s + 1)
                            dve.sem_inc(s_["level_begun"], 1)
                            if l < NL - 1:
                                dve.copy_predicated(X[:, s], mask(0, k), h4(A[s]))
                            dve.copy_predicated(XT[:, s], mask(1, k), h4(C[s])).then_inc(s_["x_ready"], 1)
                    else:
                        for s in range(2):
                            wait("d_ready", at(i, ck, 0))
                            if ck == 0:
                                dve.tensor_copy(R[:, s, :], tok[:, 2 * s, 2, :]).then_inc(s_["r_ready"], 1)
                            else:
                                wait("ks_ready", i * 2 + s + 1)
                                dve.tensor_tensor(R[:, s, :], late[:, s, 2, :], bank[:, A[s], 0:P], ALU.add).then_inc(s_["r_ready"], 1)
                        if ck == 0:
                            for s in range(2):
                                wait("s_ready", i * 2 + s + 1)
                                dve.tensor_tensor(S[:, s, :], bank[:, C[s], P:2 * P], masks[:, 1, :], ALU.mult).then_inc(s_["s_out"], 1)

                def tail(i, slot):
                    v = xres[:]
                    oh = o[:].rearrange("p n (h d) -> p (n h) d", d=AD)
                    if slot == 0:
                        wait("o_out", 4 * i + 4)
                        link(dve.tensor_tensor(osq[:], o[:], o[:], ALU.mult))
                        link(dve.tensor_reduce(rs[:, 0, :], osq[:].rearrange("p n (h d) -> p (n h) d", d=AD), AX.X, ALU.add))
                        dve.tensor_scalar(rs[:, 0, :], rs[:, 0, :], 1.0 / AD, EPS, ALU.mult, ALU.add).then_inc(s_["rms_sq"], 1)
                    if slot == 1:
                        wait("rms_root", i + 1)
                        link(dve.reciprocal(rs[:, 0, :], rs[:, 1, :]))
                        link(dve.tensor_tensor(oh, oh, bcast(rs[:, 0, :], AD), ALU.mult))
                        dve.tensor_tensor(oh, oh, grms_s[:].unsqueeze(1).broadcast_to([P, 16, AD]), ALU.mult).then_inc(s_["on_ready"], 1)
                    if slot == 4:
                        wait("y_ready", i + 1)
                        wait("xres_loaded", 16 * i + 16)
                        dve.tensor_tensor(v, v, bank[:, 7, :].rearrange("p (n t) -> p n t", n=G), ALU.add).then_inc(s_["y_out"], 1)
                        wait("y_out", i + 1)
                        link(dve.tensor_reduce(st[:, 0, :], v, AX.X, ALU.add))
                        link(dve.tensor_scalar(st[:, 0, :], st[:, 0, :], 1.0 / DM, None, ALU.mult))
                        link(dve.tensor_tensor(v, v, bcast(st[:, 0, :], DM), ALU.subtract))
                        link(dve.tensor_tensor(osq[:], v, v, ALU.mult))
                        link(dve.tensor_reduce(st[:, 1, :], osq[:], AX.X, ALU.add))
                        dve.tensor_scalar(st[:, 1, :], st[:, 1, :], 1.0 / DM, EPS, ALU.mult, ALU.add).then_inc(s_["var_ready"], 1)
                    if slot == 5:
                        wait("std_ready", i + 1)
                        link(dve.reciprocal(st[:, 3, :], st[:, 2, :]))
                        link(dve.tensor_tensor(v, v, bcast(st[:, 3, :], DM), ALU.mult))
                        link(dve.tensor_tensor(v, v, over_n(lng_s[:]), ALU.mult))
                        link(dve.tensor_tensor(v, v, over_n(lnb_s[:]), ALU.add))
                        dve.tensor_tensor(acc[:], acc[:], v, ALU.add).then_inc(s_["res_added"], 1)

                def fp4(dst, src, n, signal, a=a):
                    bits = lambda t: t.bitcast(I32)
                    blocks = lambda t: t.rearrange("p (b k) -> p b k", k=QB)
                    sc, rsc = scale[:, 0:n // QB], rscale[:, 0:n // QB]
                    av, lv, hv = a[:, 0:n], lo[:, 0:n], hi[:, 0:n]
                    link(dve.tensor_reduce(sc, blocks(src), AX.X, ALU.max, apply_absolute_value=True))
                    link(dve.tensor_scalar(sc, sc, 1.0 / 6.0, 1e-12, ALU.mult, ALU.max))
                    link(dve.reciprocal(rsc, sc))
                    link(dve.tensor_scalar(sc, sc, 0.5, None, ALU.mult))
                    yield
                    link(dve.tensor_scalar(bits(av), bits(src), 2 ** 31 - 1, None, ALU.bitwise_and))
                    yield
                    link(dve.tensor_tensor(blocks(av), blocks(av), bcast(rsc, QB), ALU.mult))
                    yield
                    link(dve.tensor_scalar(lv, av, 0.25, None, ALU.is_gt))
                    yield
                    link(dve.tensor_scalar(hv, av, 5.0, 2.0, ALU.is_gt, ALU.mult))
                    for mid in (0.75, 1.25, 1.75):
                        yield
                        link(dve.scalar_tensor_tensor(lv, av, mid, lv, ALU.is_gt, ALU.add))
                    for mid in (2.5, 3.5):
                        yield
                        link(dve.scalar_tensor_tensor(hv, av, mid, hv, ALU.is_gt, ALU.add))
                    yield
                    link(dve.scalar_tensor_tensor(lv, hv, 2.0, lv, ALU.mult, ALU.add))
                    yield
                    link(dve.scalar_tensor_tensor(bits(lv), bits(src), -2 ** 31, bits(lv), ALU.bitwise_and, ALU.bitwise_or))
                    yield
                    dve.tensor_tensor(blocks(dst), blocks(lv), bcast(sc, QB), ALU.mult).then_inc(s_[signal], 1)

                rounding = [None]

                def feed(i, slot):
                    if slot == 2:
                        wait("x_loaded", 16 * i + 16)
                        wait("hT_ready", G * i)
                        rounding[0] = fp4(flat(xq[:]), flat(x[:]), G * DM, "xq_ready")
                    if slot in (2, 3):
                        for _ in range(7):
                            next(rounding[0], None)
                    if slot in (5, 6):
                        for n in range(2 * (slot - 5), 2 * (slot - 5) + 2):
                            wait("g_out", G * i + n + 1)
                            dve.tensor_tensor(h[:, n, :], g[:, n % 2, :], bank[:, 5 + 2 * (n % 2), 0:FI], ALU.mult).then_inc(s_["h_out"], 1)
                    if slot == 7:
                        wait("xq_ready", i + 1)
                        wait("h_out", G * i + G)
                        rounding[0] = fp4(hq[:], flat(h[:]), G * FI, "hq_ready")
                    if slot in range(7, 12):
                        for _ in range(3):
                            next(rounding[0], None)
                    if slot == 14:
                        wait("down_ready", i + 1)
                        wait("acc_loaded", 16 * i + 16)
                        dve.tensor_tensor(flat(acc[:]), flat(acc[:]), bank[:, 4, :], ALU.add).then_inc(s_["down_out"], 1)

                def heads(i, ck):
                    wait("fm_out", 4 * i + 4)
                    head_of = masks[:, 1, ::AD].unsqueeze(2).broadcast_to([P, AH, P])
                    for s in range(2):
                        for j in range(3):
                            ins = dve.tensor_tensor(bd[:, ck, s, j], over_h(fm[:, 2 * s + ck, j, :]), head_of, ALU.mult)
                    ins.then_inc(s_["bd_out"], 1)

                def head(i, slot):
                    if slot in (8, 9):
                        for j in (0, 1) if slot == 8 else (2,):
                            wait("proj_out", 3 * i + j + 1)
                            if slot == 8 and j == 0:
                                wait("tok_ready", 4 * i)
                            dst = qkv[:, j, :].rearrange("p (s l) -> p s l", s=2)
                            link(dve.tensor_scalar(dst, pad[:, j, :, 0:L], cw[:, j, 0:1], None, ALU.mult))
                            for k in range(1, 4):
                                ins = dve.scalar_tensor_tensor(dst, pad[:, j, :, k:k + L], cw[:, j, k:k + 1], dst, ALU.mult, ALU.add)
                                if k < 3:
                                    link(ins)
                            ins.then_inc(s_["conv_ready"], 1)
                    if slot == 12:
                        wait("tok_out", 4 * i + 4)
                        qk = tok[:, :, 0:2, :]
                        link(dve.tensor_tensor(sq[:], qk, qk, ALU.mult))
                        link(dve.tensor_reduce(ss[:].rearrange("p n j h -> p (n j h)"), sq[:].rearrange("p n j (h d) -> p (n j h) d", d=AD), AX.X, ALU.add))
                        dve.tensor_scalar(ss[:], ss[:], 1e-6, None, ALU.add).then_inc(s_["norm_sq"], 1)
                    if slot == 13:
                        wait("norm_root", i + 1)
                        wait("beta_out", 2 * i + 2)
                        link(dve.reciprocal(ss[:], ss[:]))
                        for n in range(G):
                            qh = tok[:, n, 0:2, :].rearrange("p j (h d) -> p (j h) d", d=AD)
                            link(dve.tensor_tensor(qh, qh, bcast(ss[:, n].rearrange("p j h -> p (j h)"), AD), ALU.mult))
                            hd = lambda k: tok[:, n, k, :].rearrange("p (h d) -> p h d", d=AD)
                            dve.tensor_tensor(hd(3), hd(1), bcast(beta[:, 1, n, :], AD), ALU.mult)
                            ins = dve.tensor_tensor(hd(2), hd(2), bcast(beta[:, 0, n, :], AD), ALU.mult)
                            if n < G - 1:
                                link(ins)
                        ins.then_inc(s_["keys_ready"], 1)
                    if slot == 15:
                        heads(i, 0)

                def turn(i, has_last, has_next):
                    for slot in range(SLOTS):
                        main(i, slot)
                        if has_last:
                            tail(i - 1, slot)
                        if slot == 6:
                            heads(i, 1)
                        if slot == 8:
                            wait("ks_ready", i * 2)
                            wait("o_ready", i * 4 + 2)
                            for s in range(2):
                                dve.tensor_copy(late[:, s, 0:2, :], fm[:, 2 * s + 1, 0::2, :])
                                ins = dve.tensor_copy(late[:, s, 2, :], tok[:, 2 * s + 1, 2, :])
                            ins.then_inc(s_["late_out"], 1)
                        feed(i, slot)
                        if has_next:
                            head(i + 1, slot)
                    clear()

                wait("consts_loaded", 17 * 16)
                for _ in fp4(a[:, 0:6 * DM], flat(wgu_s[:]), 6 * DM, "wq_ready"):
                    pass
                wait("wq_ready", 1)
                for _ in fp4(a[:, 6 * DM:6 * DM + FI], wd_s[:], FI, "wq_ready", a=a[:, 6 * DM:6 * DM + FI]):
                    pass
                wait("wq_ready", 2)
                clear()
                for slot in range(SLOTS):
                    head(0, slot)
                clear()
                turn(0, False, True)
                with dve.Fori(1, NPAIR - 1) as i:
                    turn(i, True, True)
                turn(NPAIR - 1, True, False)
                for slot in range(SLOTS):
                    tail(NPAIR - 1, slot)
def build_program(nc, t):
    scratch = lambda name, shape: nc.dram_tensor(name, shape, F32).ap()
    xn, xnT = scratch("xn_scratch", (NTOK, DM)), scratch("xnT_scratch", (DM, NTOK))
    xa, x1 = scratch("xa_scratch", (NTOK, DM)), scratch("x1_scratch", (NTOK, DM))
    xn2, xn2T = scratch("xn2_scratch", (NTOK, DM)), scratch("xn2T_scratch", (DM, NTOK))
    slots, rows = scratch("slots_scratch", (NSLOT, DM)), scratch("rows_scratch", (NSLOT, DM))
    norm_input(nc, t["x"], xn, xnT, t["ident"])
    mamba_fft(nc, t["x"], xnT, xa, t["winT"], t["dft"], t["convw"], t["xpT"], t["dtT"], t["woutT"], t["small"], t["sel"], t["ident"])
    with ExitStack() as ctx:
        pos = ctx.enter_context(nc.sbuf_tensor("pos", [P, 2, NT], I32))
        gate = ctx.enter_context(nc.sbuf_tensor("gate", [P, 2, NT], F32))
        moe_route(nc, xn, xnT, slots, t["wr"], t["br"], t["iota8"], t["lower"], pos, gate)
        moe_experts(nc, slots, rows, t["w1"], t["b1"], t["w2"], t["b2"], t["ident"])
        moe_combine(nc, xn, rows, xa, x1, xn2, xn2T, t["gamma"], t["beta"], t["ident"], pos, gate)
    layer1(nc, xn2, xn2T, x1, t["out"], t["wqkv"], t["wb"], t["cw"], t["wo"], t["grms"], t["lng"], t["lnb"],
           t["wgu"], t["wd"], t["ident"], t["levels"], t["masks"])


def shape_constants():
    k = np.arange(L)
    angle = 2 * np.pi * ((k[:, None] * k[None, :]) % L) / L
    c, s = np.cos(angle), np.sin(angle)
    dft = np.stack([chunks(np.concatenate(t, 1)) for t in ([c, -s], [c, s], [-s, c])], 1)
    i, j = np.arange(P)[:, None], np.arange(P)[None, :]
    levels = []
    for n in range(NLEV):
        b = 1 << n
        levels.append(((i // (2 * b) == j // (2 * b)) & (i // b % 2 == 1) & (j // b % 2 == 0)).astype(np.float32))
    levels = np.stack(levels, 1)
    tables = {
        "dft": dft,
        "sel": np.tile(np.eye(2 * DS), (3, 1)),
        "ident": np.eye(P),
        "iota8": np.arange(NE),
        "lower": np.triu(np.ones((P, P)), 1),
        "levels": np.stack([levels, levels.transpose(2, 1, 0)], 1),
        "masks": np.stack([i <= j, i // AD == j // AD], 1),
    }
    return {n: np.ascontiguousarray(a, dtype=np.float32) for n, a in tables.items()}


def chunks(a):
    return a.reshape(a.shape[0] // P, P, -1).transpose(1, 0, 2)


def layouts(w):
    both = (("", "A_log", "D"), ("b", "A_b_log", "D_b"))
    per_channel = []
    for r, alog, d in both:
        per_channel += [chunks(w[f"L0_attn_conv1d{r}_w"]).reshape(P, -1), chunks(w[f"L0_attn_conv1d{r}_bias"][:, None]).reshape(P, -1),
                        chunks(w[f"L0_attn_dt_proj{r}_b"][:, None]).reshape(P, -1), chunks(w[f"L0_attn_{alog}"]).reshape(P, -1),
                        chunks(w[f"L0_attn_{d}"][:, None]).reshape(P, -1)]
    per_channel.append(w["L0_attn_fft_conv_b"].reshape(4, P).T)
    xproj = []
    for r, _, _ in both:
        a = w[f"L0_attn_x_proj{r}_w"].T
        xproj.append(chunks(np.concatenate([a[:, :DR], a[:, DR:], a[:, DR:], a[:, DR:]], 1)))
    t = {
        "x": w["L0_attn_hidden_states"].reshape(NTOK, DM),
        "winT": w["L0_attn_in_proj_w"].T,
        "convw": w["L0_attn_fft_conv_w"].transpose(1, 2, 0).reshape(4, P, 5, 2 * DI).transpose(1, 0, 2, 3),
        "xpT": np.stack(xproj, 1),
        "dtT": np.stack([w["L0_attn_dt_proj_w"].T, w["L0_attn_dt_projb_w"].T], 1),
        "woutT": chunks(w["L0_attn_out_proj_w"].T),
        "small": np.concatenate(per_channel, 1),
        "wr": w["L0_ffn_Wr"], "br": w["L0_ffn_br"],
        "w1": w["L0_ffn_W1"], "b1": w["L0_ffn_b1"].reshape(NE, FF // P, P).transpose(0, 2, 1),
        "w2": w["L0_ffn_W2"], "b2": w["L0_ffn_b2"], "gamma": w["L0_ffn_gamma"], "beta": w["L0_ffn_beta"],
        "wqkv": np.stack([w["L1_attn_Wq"], w["L1_attn_Wk"], w["L1_attn_Wv"]], 1),
        "wb": w["L1_attn_Wb"], "wo": w["L1_attn_Wo"],
        "cw": np.stack([w["L1_attn_conv_q"].T, w["L1_attn_conv_k"].T, w["L1_attn_conv_v"].T], 1),
        "grms": w["L1_attn_g_rms"], "lng": w["L1_attn_ln_g"], "lnb": w["L1_attn_ln_b"],
        "wgu": np.stack([w["L1_ffn_w_gate"], w["L1_ffn_w_up"]]), "wd": w["L1_ffn_w_down"],
    }
    return {n: np.ascontiguousarray(a) for n, a in t.items()}


def kernel(**inputs):
    import concourse.bacc as bacc
    from concourse.bass_utils import run_bass_kernel_spmd

    nc = bacc.Bacc("TRN2", target_bir_lowering=False, num_devices=1)
    arrays = {**layouts({n: np.asarray(a) for n, a in inputs.items()}), **shape_constants()}
    arrays = {f"in_{n}": a for n, a in arrays.items()}
    t = {n[3:]: nc.dram_tensor(n, a.shape, mybir.dt.from_np(a.dtype), kind="ExternalInput").ap() for n, a in arrays.items()}
    t["out"] = nc.dram_tensor("out_0", (NTOK, DM), F32, kind="ExternalOutput").ap()
    build_program(nc, t)
    return run_bass_kernel_spmd(nc, [arrays], core_ids=[0]).results[0]["out_0"].reshape(B, L, DM)
```

```python
from contextlib import ExitStack

import numpy as np

import concourse.bass as bass
from concourse import mybir

ALU = mybir.AluOpType
ACT = mybir.ActivationFunctionType
AX = mybir.AxisListType
F32 = mybir.dt.float32
BF16 = mybir.dt.bfloat16
I32 = mybir.dt.int32

P = 128
B, L, DM = 16, 256, 128
NTOK = B * L
NT = NTOK // P
DI, DS, DR = 256, 16, 64
EPS = 1e-5


def makers(nc, ctx, tag):
    def sb(name, shape, dt=F32):
        return ctx.enter_context(nc.sbuf_tensor(f"{tag}_{name}", shape, dt))

    def ps(name, shape, dt=F32):
        return ctx.enter_context(nc.psum_tensor(f"{tag}_{name}", shape, dt))

    def sem(name):
        return ctx.enter_context(nc.semaphore(f"{tag}_{name}"))

    return sb, ps, sem


def bcast(ap, n):
    return ap.unsqueeze(len(ap.shape)).broadcast_to([*ap.shape, n])


NE, CAP, FF = 8, 640, 512
NSLOT = NE * CAP
assert CAP == -(-NTOK * 5 // (4 * NE)) and CAP % P == 0


AH, AD = 4, 32
NLEV = 7


FI, QB = 352, 16
FCH = ((0, 128), (128, 128), (256, 96))


def norm_input(nc, x, xn_dram, xnT_dram, X, XT, ident_in, stored, load_next):
    with ExitStack() as ctx:
        sb, ps, sem = makers(nc, ctx, "n1")
        SQ = sb("SQ", [P, NT, DM])
        ident = sb("ident", [P, P])
        stat = sb("stat", [P, 4, NT])
        psT = ps("psT", [P, 4, 512])
        GR = 4
        N = NT // GR
        x_loaded, ident_loaded = [sem(f"x_loaded{g}") for g in range(GR)], sem("ident_loaded")
        centred, squared, var_ready, std_ready = sem("centred"), sem("squared"), sem("var_ready"), sem("std_ready")
        xn_ready, turned, evicted = sem("xn_ready"), sem("turned"), sem("evicted")
        step_done = sem("step_done")
        used = x_loaded + [ident_loaded, centred, squared, var_ready, std_ready, xn_ready, turned, evicted, step_done]
        tok = lambda a, g: a.rearrange("(n p) d -> p n d", p=P)[:, g * N:(g + 1) * N, :]
        part = lambda t, g: t[:, g * N:(g + 1) * N, :]
        st = lambda r, g: stat[:, r, g * N:(g + 1) * N]
        with nc.Block() as block:
            @block.sync
            def _(sp):
                for g in range(GR):
                    sp.dma_start(part(X, g), tok(x, g)).then_inc(x_loaded[g], 16)
                sp.dma_start(ident[:], ident_in).then_inc(ident_loaded, 16)
                load_next(sp)
                for g in range(GR):
                    sp.wait_ge(xn_ready, g + 1)
                    sp.dma_start(tok(xn_dram, g), part(X, g)).then_inc(stored, 16)
                sp.wait_ge(evicted, NT // 4)
                sp.dma_start(xnT_dram, XT[:]).then_inc(stored, 16)

            @block.vector
            def _(dve):
                done = [0]

                def link(ins):
                    done[0] += 1
                    ins.then_inc(step_done, 1)
                    dve.wait_ge(step_done, done[0])

                def centre(g):
                    dve.wait_ge(x_loaded[g], 16)
                    link(dve.tensor_reduce(st(0, g), part(X, g), AX.X, ALU.add))
                    link(dve.tensor_scalar(st(0, g), st(0, g), 1.0 / DM, None, ALU.mult))
                    dve.tensor_tensor(part(X, g), part(X, g), bcast(st(0, g), DM), ALU.subtract).then_inc(centred, 1)

                def variance(g):
                    dve.wait_ge(squared, g + 1)
                    link(dve.tensor_reduce(st(1, g), part(SQ, g), AX.X, ALU.add))
                    dve.tensor_scalar(st(1, g), st(1, g), 1.0 / DM, EPS, ALU.mult, ALU.add).then_inc(var_ready, 1)

                def scale(g):
                    dve.wait_ge(std_ready, g + 1)
                    link(dve.reciprocal(st(3, g), st(2, g)))
                    dve.wait_ge(centred, g + 1)
                    dve.tensor_tensor(part(X, g), part(X, g), bcast(st(3, g), DM), ALU.mult).then_inc(xn_ready, 1)

                for k in range(GR + 2):
                    if k < GR:
                        centre(k)
                    if 0 <= k - 1 < GR:
                        variance(k - 1)
                    if k - 2 >= 0:
                        scale(k - 2)

            @block.scalar
            def _(act):
                def square(g):
                    act.wait_ge(centred, g + 1)
                    act.activation(part(SQ, g), part(X, g), ACT.Square).then_inc(squared, 1)

                square(0)
                for g in range(GR):
                    if g + 1 < GR:
                        square(g + 1)
                    act.wait_ge(var_ready, g + 1)
                    act.activation(st(2, g), st(1, g), ACT.Sqrt).then_inc(std_ready, 1)
                for t in range(NT // 4):
                    act.wait_ge(turned, t + 1)
                    act.activation(XT[:, t * 512:(t + 1) * 512], psT[:, t % 4, :], ACT.Copy).then_inc(evicted, 1)

            @block.tensor
            def _(pe):
                pe.wait_ge(ident_loaded, 16)
                for t in range(NT // 4):
                    pe.wait_ge(xn_ready, 1 + 4 * t // N)
                    if t >= 4:
                        pe.wait_ge(evicted, t - 3)
                    for k in range(4):
                        mm = pe.transpose(psT[:, t % 4, k * P:(k + 1) * P], X[:, 4 * t + k, :], ident[:])
                    mm.then_inc(turned, 1)
    return used


class MambaConstants:
    LOADS = 9

    def __init__(self, nc, ctx):
        sb, _, sem = makers(nc, ctx, "mc")
        self.winT = sb("winT", [P, 4 * P])
        self.dft = sb("dft", [P, 3, 2, 512])
        self.convw = sb("convw", [P, 4, 5, 512])
        self.xp = sb("xp", [P, 2, 2, 160])
        self.dtT = sb("dtT", [DR, 2, DI])
        self.wout = sb("wout", [P, 2, DM])
        self.small = sb("small", [P, 96])
        self.sel = sb("self", [96, 32])
        self.ident = sb("ident", [P, P])
        self.loaded = sem("loaded")

    def load(self, sp, t):
        for dst, name in ((self.winT, "winT"), (self.small, "small"), (self.xp, "xpT"), (self.dtT, "dtT"), (self.wout, "woutT"),
                          (self.sel, "sel"), (self.ident, "ident"), (self.dft, "dft"), (self.convw, "convw")):
            sp.dma_start(dst[:], t[name]).then_inc(self.loaded, 16)


def mamba_fft(nc, x, xnT_dram, x1_dram, consts,
              rows_dram, moe_dram, row_of, gate):
    NPAIR = B // 2
    ROW = 2 * L
    HN = DS // 2
    SLOTS = 32
    FFT_STEPS = [4, 4, 5, 4, 3, 2, 2, 4, 4, 7, 4, 2, 8, 3, 4, 8,
                 4, 6, 1, 3, 5, 2, 2, 3, 1, 13, 4, 6, 4, 2, 2, 12]
    with ExitStack() as ctx:
        sb, ps, sem = makers(nc, ctx, "m")
        winT_s, dft_s, convw_s, xp_s, dtT_s, wout_s = consts.winT, consts.dft, consts.convw, consts.xp, consts.dtT, consts.wout
        small_s, self_s, ident = consts.small, consts.sel, consts.ident
        negA = sb("negA", [P, 2, 32])
        sel = sb("sel", [96, 32], BF16)
        one = sb("one", [P, 1])
        diag = sb("diag", [P, 2, 2, 4, P])
        xnT = sb("xnT", [P, ROW])
        xtok = sb("xtok", [P, 4, P])
        outs = sb("outs", [P, 4 * P])
        chosen, index = sb("chosen", [P, 2, DM]), sb("index", [P, 2, 1], I32)
        xl = sb("xl", [P, 2, 2, 256])
        XF = sb("XF", [P, 2, 2, 2, 256])
        U = XF[:].rearrange("p a b c d -> p (a b c d)").rearrange("p (k s n) -> p k s n", k=2, s=2)
        xc = sb("xc", [P, 4, 2, 260])
        Z = sb("Z", [P, 4, 2, 256])
        V = Z[:, :, 0, :]
        stat = sb("stat", [P, 8, 4])
        xpad = sb("xpad", [P, 2, 2, 2, 3 + L])
        u = sb("u", [P, 2, 2, ROW])
        sz = sb("sz", [P, 2, ROW])
        dt = sb("dt", [DR, ROW])
        bc32 = sb("bc32", [96, ROW])
        bcq = sb("bcq", [64, ROW], BF16)
        bcs = sb("bcs", [96, 2, ROW], BF16)
        tmp = sb("tmp", [P, ROW])
        delta = sb("delta", [P, 2, 2, ROW])
        dx = sb("dx", [P, 2, 2, ROW])
        dA = sb("dA", [P, 2, 4, 2, L])
        h = sb("h", [P, 2, HN, ROW])
        y = sb("y", [P, 2, 2, ROW])
        ypart = sb("ypart", [P, ROW])
        bcr = ypart[0:96, :]
        psR = ps("psR", [P, 2, 1024])
        psF = ps("psF", [P, 2, 512])
        psG = ps("psG", [P, 2, 512])

        consts_loaded = consts.loaded
        rows_zeroed, negA_ready, sel_ready = sem("rows_zeroed"), sem("negA_ready"), sem("sel_ready")
        xnT_loaded, xtok_loaded, x1_stored = sem("xnT_loaded"), sem("xtok_loaded"), sem("x1_stored")
        job_ready, job_evicted = sem("job_ready"), sem("job_evicted")
        fft_ready, fft_evicted = sem("fft_ready"), sem("fft_evicted")
        y_done = sem("y_done")
        index_ready, gathered, moe_step, moe_stored = sem("index_ready"), sem("gathered"), sem("moe_step"), sem("moe_stored")
        diag_ready = sem("diag_ready")
        bc_copied, bcs_ready = sem("bc_copied"), sem("bcs_ready")
        softplus_parts, delta_ready, dx_ready = sem("softplus_parts"), sem("delta_ready"), sem("dx_ready")
        spread, spread_used = sem("spread"), sem("spread_used")
        exp_ready, scan_done = sem("exp_ready"), sem("scan_done")
        y_ready, res_ready = sem("y_ready"), sem("res_ready")
        mod2_ready, mod_ready = sem("mod2_ready"), sem("mod_ready")
        var_ready, std_ready = sem("var_ready"), sem("std_ready")
        dve_step, act_step = sem("dve_step"), sem("act_step")

        def cw(r, c, k): return small_s[:, 46 * r + 4 * c + k:46 * r + 4 * c + k + 1]
        def cb(r, c): return small_s[:, 46 * r + 8 + c:46 * r + 9 + c]
        def dtb(r, c): return small_s[:, 46 * r + 10 + c:46 * r + 11 + c]
        def alog(r): return small_s[:, 46 * r + 12:46 * r + 44]
        def dskip(r, c): return small_s[:, 46 * r + 44 + c:46 * r + 45 + c]
        def fcb(o): return small_s[:, 92 + o:93 + o]

        DW1, DT1, BC1, DE1, OUT, GZ, XZ, XL, DW0, DT0, BC0, DE0, JOBS = 0, 2, 3, 4, 6, 8, 10, 12, 14, 16, 17, 18, 20
        JOB_SLOTS = [1, 1, 4, 4, 6, 7, 7, 7, 9, 9, 15, 15, 16, 17, 17, 20, 24, 24, 24, 24]

        def base(i, j=JOBS):
            return 10 if isinstance(i, int) and i == 0 and j < OUT else i * JOBS + 8

        START, END = -10, (NPAIR - 1) * JOBS + 12
        DECAYS = [(2.24, 2), (3.25, 3), (4.75, 4), (5.65, 5), (10.24, 6), (11.25, 7), (12.65, 8), (12.75, 9),
                  (18.24, 10), (19.25, 11), (20.65, 12), (20.75, 13), (26.24, 14), (27.5, 15), (28.65, 16), (28.75, 17)]
        END_ACT, END_DVE = (2.15, 3.1), (0, 2, 4)
        ROWS1, ROWS0, MAXZ = 10, 26, 13
        S1, S2, CV, S3, S4, FJOBS = 0, 4, 8, 12, 16, 20
        ends = {}
        n, limits = 0, np.cumsum(FFT_STEPS)
        for j0, k in ((S1, 2), (S2, 4), (CV, 20), (S3, 4), (S4, 4)):
            for j in range(j0, j0 + 4):
                n += k
                e = int(np.searchsorted(limits, n))
                ends[j] = e + 1 - (limits[e] - n) / FFT_STEPS[e]
        assert max(ends.values()) <= SLOTS

        with nc.Block() as block:
            def waiter(eng):
                def wait(semaphore, n):
                    if not (isinstance(n, int) and n <= 0):
                        eng.wait_ge(semaphore, n)
                return wait

            @block.sync
            def _(sp):
                tokens = lambda t, i: t.rearrange("(i n p) d -> i p n d", p=P, n=4)[bass.ds(i, 1)].rearrange("i p n d -> p (i n) d")

                def turn(i, has_last, has_next):
                    if has_last:
                        sp.wait_ge(res_ready, i + 1)
                        sp.dma_start(tokens(x1_dram, i - 1), xtok[:]).then_inc(x1_stored, 16)
                        sp.wait_ge(x1_stored, i * 16)
                        sp.dma_start(xtok[:], tokens(x, i)).then_inc(xtok_loaded, 16)
                    if has_next:
                        sp.wait_ge(job_evicted, base(i) + GZ + 2)
                        sp.dma_start(xnT[:], xnT_dram[:, bass.ds((i + 1) * ROW, ROW)]).then_inc(xnT_loaded, 16)

                sp.dma_start(xnT[:], xnT_dram[:, 0:ROW]).then_inc(xnT_loaded, 16)
                sp.dma_start(xtok[:], tokens(x, 0)).then_inc(xtok_loaded, 16)
                turn(0, False, True)
                with sp.Fori(1, NPAIR - 1) as i:
                    turn(i, True, True)
                turn(NPAIR - 1, True, False)
                sp.wait_ge(res_ready, NPAIR + 1)
                sp.dma_start(tokens(x1_dram, NPAIR - 1), xtok[:]).then_inc(x1_stored, 16)
                sp.wait_ge(x1_stored, 16 * NPAIR)

            @block.gpsimd
            def _(pool):
                pool.memset(xpad[:, :, :, :, 0:3], 0.0)
                pool.memset(xc[:, :, :, 0:2], 0.0)
                pool.memset(xc[:, :, :, 258:260], 0.0)
                pool.memset(dA[:, :, :, :, 0:1], 0.0)
                pool.memset(one[:], 1.0).then_inc(rows_zeroed, 1)
                pool.sem_inc(res_ready, 1)
                pool.wait_ge(consts_loaded, 16 * consts.LOADS)

                def residual(i, base):
                    pool.wait_ge(job_evicted, base + OUT + 2)
                    pool.wait_ge(xtok_loaded, i * 16 + 16)
                    xt = xtok[:].rearrange("p n d -> p (n d)")
                    pool.tensor_tensor(xt, xt, outs[:], ALU.add).then_inc(res_ready, 1)

                def inputs(i, r):
                    for c in range(2):
                        pool.wait_ge(softplus_parts, i * 4 + r * 2 + c + 1)
                        pool.tensor_tensor(delta[:, r, c, :], delta[:, r, c, :], dx[:, r, c, :], ALU.add).then_inc(delta_ready, 1)
                        pool.wait_ge(delta_ready, i * 4 + r * 2 + c + 1)
                        pool.tensor_tensor(dx[:, r, c, :], delta[:, r, c, :], u[:, r, c, :], ALU.mult).then_inc(dx_ready, 1)

                def experts_sum(i, n):
                    t = i * 4 + n
                    if not (isinstance(t, int) and t == 0):
                        pool.wait_ge(moe_stored, t * 16)
                    pool.tensor_copy(index[:], row_of[:, :, bass.ds(t, 1)]).then_inc(index_ready, 1)
                    pool.wait_ge(index_ready, 2 * t + 1)
                    pool.sem_inc(index_ready, 1)
                    for k in range(2):
                        pool.indirect_dma_start(chosen[:, k, :], None, rows_dram,
                                                bass.IndirectOffsetOnAxis(ap=index[:, k, :], axis=0)).then_inc(gathered, 16)
                    pool.wait_ge(gathered, t * 32 + 32)
                    pool.tensor_tensor(chosen[:], chosen[:], gate[:, :, bass.ds(t, 1)].broadcast_to([P, 2, DM]), ALU.mult).then_inc(moe_step, 1)
                    pool.wait_ge(moe_step, 2 * t + 1)
                    pool.tensor_tensor(chosen[:, 0, :], chosen[:, 0, :], chosen[:, 1, :], ALU.add).then_inc(moe_step, 1)
                    pool.wait_ge(moe_step, 2 * t + 2)
                    pool.dma_start(moe_dram.rearrange("(t p) d -> t p d", p=P)[bass.ds(t, 1)].rearrange("t p d -> p (t d)"),
                                   chosen[:, 0, :]).then_inc(moe_stored, 16)

                def turn(i, has_last, has_next):
                    experts_sum(i, 0)
                    if has_last:
                        residual(i - 1, base(i))
                    experts_sum(i, 1)
                    inputs(i, 1)
                    experts_sum(i, 2)
                    if has_next:
                        inputs(i + 1, 0)
                    experts_sum(i, 3)

                inputs(0, 0)
                turn(0, False, True)
                with pool.Fori(1, NPAIR - 1) as i:
                    turn(i, True, True)
                turn(NPAIR - 1, True, False)
                residual(NPAIR - 1, END)
                pool.wait_ge(moe_stored, NPAIR * 4 * 16)

            @block.scalar
            def _(act):
                wait = waiter(act)
                steps = [0]

                def link(ins):
                    steps[0] += 1
                    ins.then_inc(act_step, 1)
                    act.wait_ge(act_step, steps[0])

                def evict(i, base, j):
                    wait(job_ready, base + j + 1)
                    pj = psG[:, j % 2, :]
                    seqs = pj.rearrange("p (s l) -> p s l", s=2)
                    r = int(j < GZ)
                    q = 2 * i + r
                    if j in (OUT, OUT + 1):
                        if j == OUT:
                            wait(res_ready, i + 1)
                        ins = act.activation(outs[:, (j - OUT) * 256:(j - OUT + 1) * 256], pj[:, 0:256], ACT.Copy)
                    elif j in (DW1, DW1 + 1, DW0, DW0 + 1):
                        c = (j - DW1) % 2
                        wait(y_done, q - 1)
                        ins = act.activation(u[:, r, c, :], pj, ACT.Silu, bias=cb(r, c))
                    elif j in (DT1, DT0):
                        ins = act.activation(dt[:], pj[0:DR], ACT.Copy)
                    elif j in (BC1, BC0):
                        wait(bcs_ready, q)
                        wait(spread, 16 * q - 16)
                        act.activation(bcs[:, r, :], pj[0:96], ACT.Copy).then_inc(bc_copied, 1)
                        ins = act.activation(bc32[:], pj[0:96], ACT.Copy)
                    elif j in (DE1, DE1 + 1, DE0, DE0 + 1):
                        c = (j - DE1) % 2
                        wait(softplus_parts, q * 2 + c)
                        wait(exp_ready, 8 * q - 8)
                        link(act.activation(tmp[:], pj, ACT.Abs, bias=dtb(r, c)))
                        act.activation(dx[:, r, c, :], pj, ACT.Relu, bias=dtb(r, c)).then_inc(job_evicted, 1)
                        link(act.activation(tmp[:], tmp[:], ACT.Exp, scale=-1.0))
                        act.activation(delta[:, r, c, :], tmp[:], ACT.Ln, bias=one[:]).then_inc(softplus_parts, 1)
                        return
                    elif j in (GZ, GZ + 1):
                        wait(y_ready, i)
                        ins = act.activation(sz[:, j - GZ, :], pj, ACT.Silu)
                    elif j in (XZ, XZ + 1):
                        act.activation(xpad[:, 0, j - XZ, :, 3:], seqs, ACT.Copy)
                        ins = act.activation(xpad[:, 1, j - XZ, :, 3:][:, :, ::-1], seqs, ACT.Copy)
                    else:
                        ins = act.activation(xl[:, j - XL, :, :], pj.rearrange("p (k d) -> p k d", k=2), ACT.Copy)
                    ins.then_inc(job_evicted, 1)

                def decays(i, e):
                    r, c = e // 8, e % 2
                    n0 = (e // 4 % 2) * HN + (e // 2 % 2) * 4
                    act.wait_ge(scan_done, i * 16 + e + 1)
                    act.wait_ge(dx_ready, i * 4 + r * 2 + c + 1)
                    dr = delta[:, r, c, :].rearrange("p (s l) -> p s l", s=2)[:, :, 1:]
                    for n in range(4):
                        k = 16 * c + n0 + n
                        ins = act.activation(dA[:, e % 2, n, :, 1:], dr, ACT.Exp, scale=negA[:, r, k:k + 1])
                    ins.then_inc(exp_ready, 1)

                def evict_fft(i, j):
                    wait(fft_ready, i * FJOBS + j + 1)
                    pj, k = psF[:, j % 2, :], j % 4
                    if j < S2:
                        out = XF[:, :, k % 2, k // 2, :]
                        ins = act.activation(out, pj.rearrange("p (a k) -> p a k", a=2), ACT.Copy)
                    elif j < CV:
                        ins = act.activation(xc[:, k, :, 2:258], pj.rearrange("p (s k) -> p s k", s=2), ACT.Copy)
                    elif j < S3:
                        if j == CV:
                            wait(y_ready, i)
                        ins = act.activation(Z[:, k, :, :], pj.rearrange("p (s k) -> p s k", s=2), ACT.Silu, bias=fcb(k))
                    elif j < S4:
                        ins = act.activation(U[:, k % 2, k // 2, :], pj, ACT.Copy)
                    else:
                        ins = act.activation(Z[:, k, :, :], pj.rearrange("p (a l) -> p a l", a=2), ACT.Square)
                    ins.then_inc(fft_evicted, 1)

                def finish(i, part):
                    if part == 0:
                        act.wait_ge(mod2_ready, i + 1)
                        for k in range(4):
                            ins = act.activation(V[:, k, :], V[:, k, :], ACT.Sqrt, scale=stat[:, 1, k:k + 1])
                        ins.then_inc(mod_ready, 1)
                    else:
                        act.wait_ge(var_ready, i + 1)
                        act.activation(stat[:, 5, :], stat[:, 4, :], ACT.Sqrt).then_inc(std_ready, 1)

                def turn(i, has_last, has_next):
                    steps_ = [(JOB_SLOTS[j] + j / 1000, "job", j) for j in range(JOBS)]
                    steps_ += [(ends[j], "fft", j) for j in range(FJOBS)] + [(at, "decays", e) for at, e in DECAYS]
                    steps_ += [(at, "finish", k) for k, at in enumerate(END_ACT)]
                    for _, what, j in sorted(steps_):
                        if what == "fft":
                            evict_fft(i, j)
                        elif what == "decays" and j < 16:
                            decays(i, j)
                        elif what == "decays" and has_next:
                            decays(i + 1, j - 16)
                        elif what == "finish" and has_last:
                            finish(i - 1, j)
                        elif what == "job" and j in (OUT, OUT + 1):
                            if has_last:
                                evict(i - 1, base(i), j)
                        elif what == "job" and j < XZ:
                            evict(i, base(i, j), j)
                        elif what == "job" and has_next:
                            evict(i + 1, base(i), j)
                    act.sem_clear(act_step)
                    steps[0] = 0

                act.wait_ge(consts_loaded, 16 * consts.LOADS)
                act.wait_ge(rows_zeroed, 1)
                for r in range(2):
                    act.activation(negA[:, r, :], alog(r), ACT.Exp).then_inc(negA_ready, 1)
                act.wait_ge(negA_ready, 4)
                for j in range(XZ, JOBS):
                    evict(0, START, j)
                for e in range(2):
                    decays(0, e)
                turn(0, False, True)
                with act.Fori(1, NPAIR - 1) as i:
                    turn(i, True, True)
                turn(NPAIR - 1, True, False)
                for k in range(2):
                    finish(NPAIR - 1, k)
                for j in (OUT, OUT + 1):
                    evict(NPAIR - 1, END, j)

            @block.tensor
            def _(pe):
                wait = waiter(pe)

                def job(i, base, j):
                    n = base + j
                    wait(job_evicted, n if j in (DT1, DT0) else n - 1)
                    out = psG[:, j % 2, :]
                    r = int(j < GZ)
                    if j in (OUT, OUT + 1):
                        if j == OUT:
                            wait(y_ready, i + 1)
                        n0 = 2 * (j - OUT)
                        mms = [(out[:, k * P:(k + 1) * P], y[:, 0, c, (n0 + k) * P:(n0 + k + 1) * P], wout_s[:, c, :], c == 0, c == 1)
                               for k in range(2) for c in range(2)]
                    elif j in (DW1, DW1 + 1, DW0, DW0 + 1):
                        c = (j - DW1) % 2
                        mms = [(out, diag[:, r, c, k, :], xpad[:, r, c, :, k:k + L], k == 0, k == 3) for k in range(4)]
                    elif j in (DT1, DT0):
                        mms = [(out[0:DR], xp_s[:, r, c, 0:DR], u[:, r, c, :], c == 0, c == 1) for c in range(2)]
                    elif j in (BC1, BC0):
                        mms = [(out[0:96], xp_s[:, r, c, DR:DR + 96], u[:, r, c, :], c == 0, c == 1) for c in range(2)]
                    elif j in (DE1, DE1 + 1, DE0, DE0 + 1):
                        c = (j - DE1) % 2
                        mms = [(out, dtT_s[:, r, c * P:(c + 1) * P], dt[:], True, True)]
                    elif j in (GZ, GZ + 1):
                        mms = [(out, winT_s[:, (2 + j - GZ) * P:(3 + j - GZ) * P], xnT[:], True, True)]
                    elif j in (XZ, XZ + 1):
                        if j == XZ:
                            wait(xnT_loaded, 16 * i + 16)
                        mms = [(out, winT_s[:, (j - XZ) * P:(j - XZ + 1) * P], xnT[:], True, True)]
                    else:
                        s = j - XL
                        mms = [(out[:, k * 256:(k + 1) * 256], xnT[:, s * L + k * P:s * L + (k + 1) * P], winT_s[:, 0:256], True, True)
                               for k in range(2)]
                    for out, lhsT, rhs, start, stop in mms:
                        mm = pe.matmul(out, lhsT=lhsT, rhs=rhs, start=start, stop=stop)
                    mm.then_inc(job_ready, 1)

                def fft(i):
                    def stage(j, mms):
                        for n, (lhsT, rhs) in enumerate(mms):
                            yield
                            if n == 0:
                                wait(fft_evicted, i * FJOBS + (j if j % 4 == 0 else j - 1))
                                if j == S1:
                                    wait(job_evicted, base(i) - 4)
                            mm = pe.matmul(psF[:, j % 2, :], lhsT=lhsT, rhs=rhs, start=n == 0, stop=n == len(mms) - 1)
                        mm.then_inc(fft_ready, 1)

                    C, S, NS = (dft_s[:, 1, :, 0:256], dft_s[:, 1, :, 256:512], dft_s[:, 0, :, 256:512])
                    for k in range(4):
                        s, dc = k // 2, k % 2
                        yield from stage(S1 + k, [(xl[:, s, lc, dc * P:(dc + 1) * P], dft_s[:, 0, lc, :]) for lc in range(2)])
                    for k in range(4):
                        im, mc = k // 2, k % 2
                        pairs = ((C, 0), (S, 1)) if not im else ((C, 1), (NS, 0))
                        yield from stage(S2 + k, [(t[:, dc, mc * P:(mc + 1) * P], XF[:, a, dc, :, :]) for t, a in pairs for dc in range(2)])
                    for o in range(4):
                        yield from stage(CV + o, [(convw_s[:, c, t, o * P:(o + 1) * P], xc[:, c, :, t:t + 256])
                                                  for c in range(4) for t in range(5)])
                    for k in range(4):
                        s, kc = k // 2, k % 2
                        yield from stage(S3 + k, [(Z[:, m, s, kc * P:(kc + 1) * P], dft_s[:, 1 + m // 2, m % 2, :]) for m in range(4)])
                    for k in range(4):
                        s, dc = k // 2, k % 2
                        yield from stage(S4 + k, [(U[:, kc, s, a * 256 + dc * P:a * 256 + (dc + 1) * P], dft_s[:, 1 + a, kc, :])
                                                  for a in range(2) for kc in range(2)])

                def turn(i, has_last, has_next):
                    steps = fft(i)
                    next(steps)
                    for s in range(SLOTS):
                        r, hf, k = s // 16, s // 8 % 2, s % 8
                        if s % 16 == 0:
                            pe.wait_ge(bcs_ready, i * 2 + r + 1)
                        pe.wait_ge(spread_used, i * SLOTS + s + 1)
                        for m in range(2):
                            row = DS * (k // 4) + HN * hf + 2 * (k % 4) + m
                            mm = pe.matmul(psR[:, s % 2, m * 512:(m + 1) * 512],
                                           lhsT=sel[:, row:row + 1].broadcast_to([96, P]), rhs=bcs[:, r, :], start=True, stop=True)
                        mm.then_inc(spread, 1)
                        for j in [j for j in range(JOBS) if JOB_SLOTS[j] == s]:
                            if j in (OUT, OUT + 1):
                                if has_last:
                                    job(i - 1, base(i), j)
                            elif j < XZ:
                                job(i, base(i, j), j)
                            elif has_next:
                                job(i + 1, base(i), j)
                        for _ in range(FFT_STEPS[s]):
                            next(steps, None)

                pe.wait_ge(consts_loaded, 16 * consts.LOADS)
                pe.wait_ge(rows_zeroed, 1)
                pe.wait_ge(sel_ready, 1)
                pe.wait_ge(diag_ready, 1)
                for j in range(XZ, JOBS):
                    job(0, START, j)
                turn(0, False, True)
                with pe.Fori(1, NPAIR - 1) as i:
                    turn(i, True, True)
                turn(NPAIR - 1, True, False)
                for j in (OUT, OUT + 1):
                    job(NPAIR - 1, END, j)

            @block.vector
            def _(dve):
                done = [0]
                wait = waiter(dve)

                def link(ins):
                    done[0] += 1
                    ins.then_inc(dve_step, 1)
                    dve.wait_ge(dve_step, done[0])

                def split_rows(i, r):
                    q = 2 * i + r
                    wait(bc_copied, q + 1)
                    wait(job_evicted, (base(i, BC1) + BC1 if r else base(i - 1) + BC0 if not isinstance(i, int) or i else START + BC0) + 1)
                    link(dve.tensor_tensor(bcr[:], bc32[:], bcs[:, r, :], ALU.subtract))
                    link(dve.tensor_copy(bcs[64:96, r, :], bcr[64:96, :]))
                    link(dve.tensor_copy(bcq[32:64, :], bcr[32:64, :]))
                    dve.tensor_tensor(bcs[32:64, r, :], bcr[32:64, :], bcq[32:64, :], ALU.subtract).then_inc(bcs_ready, 1)
                    wait(bcs_ready, q + 1)

                def scans(i, s):
                    r, hf, j = s // 16, s // 8 % 2, s % 8
                    if s % 16 == 0:
                        dve.wait_ge(dx_ready, i * 4 + 2 * r + 2)
                    if j == 0:
                        wait(y_done, 2 * i + r)
                    rows = psR[:, j % 2, :].rearrange("p (n l) -> p n l", n=2)
                    dve.wait_ge(spread, i * SLOTS + s + 1)
                    if j < 4:
                        for c in range(2):
                            ins = dve.tensor_tensor(h[:, c, 2 * j:2 * j + 2, :], rows, dx[:, r, c, :].unsqueeze(1).broadcast_to([P, 2, ROW]), ALU.mult)
                            if c == 0:
                                link(ins)
                        ins.then_inc(spread_used, 1)
                        if j % 2 == 1:
                            dve.wait_ge(spread_used, i * SLOTS + s + 1 + 2)
                            for c in range(2):
                                e = r * 8 + hf * 4 + (j // 2) * 2 + c
                                dve.wait_ge(exp_ready, i * 16 + e + 1)
                                hq = h[:, c, 2 * j - 2:2 * j + 2, :].rearrange("p n l -> p (n l)")
                                dve.tensor_tensor_scan(hq, dA[:, e % 2].rearrange("p n s l -> p (n s l)"), hq, 0.0,
                                                       ALU.mult, ALU.add).then_inc(scan_done, 1)
                        if j == 3:
                            dve.wait_ge(scan_done, i * 16 + r * 8 + hf * 4 + 4 + 2)
                        return
                    for c in range(2):
                        hj = h[:, c, 2 * j - 8:2 * j - 6, :]
                        ins = dve.tensor_tensor(hj, rows, hj, ALU.mult)
                        if c == 0:
                            link(ins)
                    ins.then_inc(spread_used, 1)
                    if j < 7:
                        return
                    dve.wait_ge(spread_used, i * SLOTS + s + 1 + 2)
                    for c in range(2):
                        hs = h[:, c].rearrange("p n l -> p l n")
                        if hf == 0:
                            if c == 0 and r == 0:
                                wait(job_ready, base(i) + OUT + 2)
                            if c == 0:
                                wait(y_ready, i)
                            link(dve.tensor_reduce(y[:, r, c, :], hs, AX.X, ALU.add))
                        else:
                            link(dve.tensor_reduce(ypart[:], hs, AX.X, ALU.add))
                            link(dve.tensor_tensor(y[:, r, c, :], y[:, r, c, :], ypart[:], ALU.add))
                            ins = dve.scalar_tensor_tensor(y[:, r, c, :], u[:, r, c, :], dskip(r, c), y[:, r, c, :], ALU.mult, ALU.add)
                            if c == 0:
                                link(ins)
                            else:
                                ins.then_inc(y_done, 1)

                def finish(i, s):
                    if s == END_DVE[0]:
                        wait(y_done, 2 * i + 2)
                        for c in range(2):
                            y0 = y[:, 0, c, :].rearrange("p (s l) -> p s l", s=2)
                            y1 = y[:, 1, c, :].rearrange("p (s l) -> p s l", s=2)
                            link(dve.tensor_tensor(y0, y0, y1[:, :, ::-1], ALU.add))
                        link(dve.tensor_tensor(y[:, 0], y[:, 0], sz[:], ALU.mult))
                        dve.wait_ge(fft_evicted, i * FJOBS + FJOBS)
                        dve.tensor_tensor(V, V, Z[:, :, 1, :], ALU.add).then_inc(mod2_ready, 1)
                    if s == END_DVE[1]:
                        dve.wait_ge(mod_ready, i + 1)
                        link(dve.tensor_reduce(stat[:, 2, :], V, AX.X, ALU.add))
                        link(dve.tensor_scalar(stat[:, 2, :], stat[:, 2, :], 1.0 / L, None, ALU.mult))
                        link(dve.tensor_tensor(V, V, bcast(stat[:, 2, :], L), ALU.subtract))
                        sq = Z[:, :, 1, :]
                        link(dve.tensor_tensor(sq, V, V, ALU.mult))
                        link(dve.tensor_reduce(stat[:, 3, :], sq, AX.X, ALU.add))
                        dve.tensor_scalar(stat[:, 4, :], stat[:, 3, :], 1.0 / L, EPS, ALU.mult, ALU.add).then_inc(var_ready, 1)
                    if s == END_DVE[2]:
                        dve.wait_ge(std_ready, i + 1)
                        link(dve.reciprocal(stat[:, 6, :], stat[:, 5, :]))
                        link(dve.tensor_tensor(V, V, bcast(stat[:, 6, :], L), ALU.mult))
                        y0 = y[:, 0].rearrange("p c (s l) -> p s c l", s=2)
                        dve.tensor_tensor(y0, y0, V.rearrange("p (s c) l -> p s c l", s=2), ALU.add).then_inc(y_ready, 1)

                def turn(i, has_last, has_next):
                    for s in range(SLOTS):
                        scans(i, s)
                        if has_last:
                            finish(i - 1, s)
                        if s == ROWS1:
                            split_rows(i, 1)
                        if s == MAXZ:
                            dve.wait_ge(job_evicted, base(i) + GZ + 2)
                            link(dve.tensor_reduce(stat[:, 0, :].rearrange("p (s c) -> p c s", s=2),
                                                   sz[:].rearrange("p c (s l) -> p c s l", s=2), AX.X, ALU.max))
                            link(dve.tensor_tensor(stat[:, 1, :], stat[:, 0, :], stat[:, 0, :], ALU.mult))
                            link(dve.tensor_scalar(stat[:, 1, :], stat[:, 1, :], 1.0 / (DI * L) ** 2, None, ALU.mult))
                        if s == ROWS0 and has_next:
                            split_rows(i + 1, 0)
                    dve.sem_clear(dve_step)
                    done[0] = 0

                dve.sem_inc(spread_used, 2)
                dve.sem_inc(scan_done, 2)
                dve.wait_ge(consts_loaded, 16 * consts.LOADS)
                dve.tensor_copy(sel[:], self_s[:]).then_inc(sel_ready, 1)
                for r in range(2):
                    for c in range(2):
                        for k in range(4):
                            ins = dve.tensor_scalar(diag[:, r, c, k, :], ident[:], cw(r, c, k), None, ALU.mult)
                ins.then_inc(diag_ready, 1)
                dve.wait_ge(negA_ready, 2)
                for r in range(2):
                    dve.tensor_scalar(negA[:, r, :], negA[:, r, :], -1.0, None, ALU.mult).then_inc(negA_ready, 1)
                dve.wait_ge(sel_ready, 1)
                split_rows(0, 0)
                turn(0, False, True)
                with dve.Fori(1, NPAIR - 1) as i:
                    turn(i, True, True)
                turn(NPAIR - 1, True, False)
                for s in END_DVE:
                    finish(NPAIR - 1, s)
class RouteConstants:
    def __init__(self, nc, ctx):
        sb, _, sem = makers(nc, ctx, "rc")
        self.wr, self.br, self.iota, self.lower = sb("wr", [P, NE]), sb("br", [P, NE]), sb("iota", [P, NE]), sb("lower", [P, P])
        self.loaded = sem("loaded")

    def load(self, sp, t):
        row = lambda a: a.rearrange("(o e) -> o e", o=1).broadcast_to([P, NE])
        for dst, src in ((self.wr, t["wr"]), (self.br, row(t["br"])), (self.iota, row(t["iota8"])), (self.lower, t["lower"])):
            sp.dma_start(dst[:], src).then_inc(self.loaded, 16)


def moe_route(nc, xn_dram, xT, slots_dram, consts, row_of, gate, xn_stored, used, load_next):
    G = 4
    with ExitStack() as ctx:
        sb, ps, sem = makers(nc, ctx, "r")
        wr_s, br_s, iota, lower, loaded = consts.wr, consts.br, consts.iota, consts.lower, consts.loaded
        ones = sb("ones", [P, P])
        lg, oh, key = sb("lg", [P, NT, NE]), sb("oh", [P, 2, NT, NE]), sb("key", [P, NT, NE])
        t, t2, gt, base = sb("t", [P, NT, NE]), sb("t2", [P, NT, NE]), sb("gt", [P, NT, NE]), sb("base", [P, NT, NE])
        pos = sb("pos", [P, 2, NT], I32)
        m, w = sb("m", [P, 3, NT]), sb("w", [P, 3, NT])
        kept, dest = sb("kept", [P, 2, NT]), sb("dest", [P, 2, NT])
        bits = sb("bits", [P, 2, 3, NE], I32)
        thr, cand, acc = sb("thr", [P, NE], I32), sb("cand", [P, 3, NE], I32), sb("acc", [P, 3, NE], I32)
        t3, cnt3 = sb("t3", [P, 3, NT, NE]), sb("cnt3", [P, 3, NE])
        cnt, need, first = sb("cnt", [P, NE]), sb("need", [P, NE]), sb("first", [P, NE])
        zeros = sb("zeros", [P, NSLOT // P * DM])
        xbuf, ibuf = sb("xbuf", [P, 2, G, DM]), sb("ibuf", [P, 2, 2, G], I32)
        psL, psC, psA = ps("psL", [P, NT, NE]), ps("psC", [P, 3, NE]), ps("psA", [P, 2, 256])
        const_ready = sem("const_ready")
        logits_ready, diff_ready, exp_ready = sem("logits_ready"), sem("diff_ready"), sem("exp_ready")
        count_ready, count_summed = sem("count_ready"), sem("count_summed")
        mask_ready, mask_summed = sem("mask_ready"), sem("mask_summed")
        slots_zeroed, index_ready, row_loaded, scattered = sem("slots_zeroed"), sem("index_ready"), [sem("row_loaded0"), sem("row_loaded1")], [sem("scattered0"), sem("scattered1")]
        step_done, scatter_begun = sem("step_done"), sem("scatter_begun")
        flat = lambda a: a.rearrange("p n e -> p (n e)")
        over_n = lambda a: a.unsqueeze(1).broadcast_to([P, NT, NE])
        by_e = lambda a: a.rearrange("p n e -> p e n")
        with nc.Block() as block:
            @block.sync
            def _(sp):
                sp.wait_ge(const_ready, 3)
                sp.dma_start(slots_dram.rearrange("(p n) d -> p (n d)", p=P), zeros[:]).then_inc(slots_zeroed, 16)
                load_next(sp)
                def rows(i):
                    for b in range(2):
                        if not isinstance(i, int):
                            sp.wait_ge(scattered[b], i * (2 * G * 16))
                        sp.dma_start(xbuf[:, b], xn_dram.rearrange("(i b n p) d -> i b p n d", p=P, n=G, b=2)[bass.ds(i, 1)].rearrange("i b p n d -> b p (i n) d")[b]).then_inc(row_loaded[b], 16)

                sp.wait_ge(xn_stored, 16 * 5)
                rows(0)
                with sp.Fori(1, NT // (2 * G)) as i:
                    rows(i)

            @block.tensor
            def _(pe):
                pe.wait_ge(loaded, 4 * 16)
                for n in range(NT):
                    mm = pe.matmul(psL[:, n, :], lhsT=xT[:, n * P:(n + 1) * P], rhs=wr_s[:], start=True, stop=True)
                mm.then_inc(logits_ready, 1)
                pe.wait_ge(const_ready, 3)
                with pe.Fori(0, 15) as i:
                    pe.wait_ge(count_ready, i + 1)
                    pe.matmul(psC[:], lhsT=ones[:], rhs=cnt3[:], start=True, stop=True).then_inc(count_summed, 1)
                pe.wait_ge(count_ready, 16)
                pe.matmul(psC[:, 0, :], lhsT=ones[:], rhs=cnt[:], start=True, stop=True).then_inc(count_summed, 1)
                for k, mask in enumerate((t, t)):
                    pe.wait_ge(mask_ready, k + 1)
                    pe.matmul(psA[:, 0, :], lhsT=lower[:], rhs=flat(mask[:]), start=True, stop=True)
                    pe.matmul(psA[:, 1, :], lhsT=ones[:], rhs=flat(mask[:]), start=True, stop=True).then_inc(mask_summed, 1)

            @block.scalar
            def _(act):
                act.wait_ge(diff_ready, 1)
                act.activation(w[:, 1, :], m[:, 2, :], ACT.Exp).then_inc(exp_ready, 1)

            @block.gpsimd
            def _(pool):
                for semaphore in used:
                    pool.sem_clear(semaphore)
                pool.memset(zeros[:], 0.0).then_inc(const_ready, 1)
                pool.memset(ones[:], 1.0).then_inc(const_ready, 1)
                for k, (added, step) in enumerate(((1, 1), (2, 3), (3, 1))):
                    pool.memset(bits[:, 0, k, :], added << 28)
                    ins = pool.memset(bits[:, 1, k, :], step << 28)
                ins.then_inc(const_ready, 1)
                pool.wait_ge(slots_zeroed, 16)
                with pool.Fori(0, NT // (2 * G)) as i:
                    for b in range(2):
                        pool.wait_ge(index_ready, i * 2 + b + 1)
                        pool.wait_ge(row_loaded[b], i * 16 + 16)
                        pool.sem_inc(scatter_begun, 1)
                        for n in range(G):
                            for k in range(2):
                                pool.indirect_dma_start(slots_dram, bass.IndirectOffsetOnAxis(ap=ibuf[:, b, k, n:n + 1], axis=0),
                                                        xbuf[:, b, n, :], None, bounds_check=NSLOT - 1, oob_is_err=False).then_inc(scattered[b], 16)
                for b in range(2):
                    pool.wait_ge(scattered[b], NT * 16)

            @block.vector
            def _(dve):
                done = [0]

                def link(ins):
                    done[0] += 1
                    ins.then_inc(step_done, 1)
                    dve.wait_ge(step_done, done[0])

                dve.wait_ge(loaded, 4 * 16)
                dve.wait_ge(logits_ready, 1)
                link(dve.memset(thr[:], 0))
                link(dve.tensor_tensor(lg[:], psL[:], over_n(br_s[:]), ALU.add))
                for k in range(2):
                    link(dve.tensor_reduce(m[:, k, :], lg[:], AX.X, ALU.max))
                    link(dve.tensor_tensor(t[:], lg[:], bcast(m[:, k, :], NE), ALU.not_equal))
                    link(dve.scalar_tensor_tensor(t[:], t[:], float(NE), over_n(iota[:]), ALU.mult, ALU.add))
                    link(dve.tensor_reduce(m[:, 2, :], t[:], AX.X, ALU.min))
                    link(dve.tensor_tensor(oh[:, k], over_n(iota[:]), bcast(m[:, 2, :], NE), ALU.is_equal))
                    if k == 0:
                        link(dve.scalar_tensor_tensor(lg[:], oh[:, 0], -3e38, lg[:], ALU.mult, ALU.add))
                dve.tensor_tensor(m[:, 2, :], m[:, 1, :], m[:, 0, :], ALU.subtract).then_inc(diff_ready, 1)
                dve.wait_ge(exp_ready, 1)
                link(dve.tensor_scalar(w[:, 2, :], w[:, 1, :], 1.0, None, ALU.add))
                link(dve.reciprocal(w[:, 0, :], w[:, 2, :]))
                link(dve.tensor_tensor(w[:, 1, :], w[:, 1, :], w[:, 0, :], ALU.mult))
                link(dve.tensor_tensor(key[:], oh[:, 0], bcast(w[:, 0, :], NE), ALU.mult))
                link(dve.tensor_tensor(t[:], oh[:, 1], bcast(w[:, 1, :], NE), ALU.mult))
                link(dve.tensor_tensor(key[:], key[:], t[:], ALU.add))
                link(dve.tensor_tensor(t[:], oh[:, 0], oh[:, 1], ALU.add))
                link(dve.scalar_tensor_tensor(key[:], t[:], -1.0, key[:], ALU.add, ALU.add))
                dve.wait_ge(const_ready, 3)
                dve.sem_clear(step_done)
                with dve.Fori(0, 15) as i:
                    done[0] = 0
                    link(dve.tensor_tensor(cand[:], thr[:].unsqueeze(1).broadcast_to([P, 3, NE]), bits[:, 0], ALU.bitwise_or))
                    link(dve.tensor_tensor(t3[:], key[:].unsqueeze(1).broadcast_to([P, 3, NT, NE]),
                                           cand[:].bitcast(F32).unsqueeze(2).broadcast_to([P, 3, NT, NE]), ALU.is_ge))
                    dve.tensor_reduce(cnt3[:], t3[:].rearrange("p k n e -> p k e n"), AX.X, ALU.add).then_inc(count_ready, 1)
                    dve.wait_ge(count_summed, i + 1)
                    link(dve.tensor_scalar(acc[:], psC[:], float(CAP), -1.0, ALU.is_ge, ALU.mult))
                    link(dve.tensor_tensor(acc[:], acc[:], bits[:, 1], ALU.bitwise_and))
                    for k in range(3):
                        link(dve.tensor_tensor(thr[:], thr[:], acc[:, k, :], ALU.bitwise_xor))
                    link(dve.tensor_scalar(bits[:], bits[:], 2, None, ALU.logical_shift_right))
                    dve.sem_clear(step_done)
                done[0] = 0
                thrf = over_n(thr[:].bitcast(F32))
                link(dve.tensor_tensor(gt[:], key[:], thrf, ALU.is_gt))
                dve.tensor_reduce(cnt[:], by_e(gt[:]), AX.X, ALU.add).then_inc(count_ready, 1)
                dve.wait_ge(count_summed, 16)
                link(dve.tensor_scalar(need[:], psC[:, 0, :], -1.0, float(CAP), ALU.mult, ALU.add))
                dve.tensor_tensor(t[:], key[:], thrf, ALU.is_equal).then_inc(mask_ready, 1)

                def rank(k):
                    dve.wait_ge(mask_summed, k + 1)
                    link(dve.tensor_copy(flat(t2[:]), psA[:, 1, :]))
                    for e in range(NE):
                        link(dve.tensor_tensor_scan(base[:, :, e], ones[:, 0:NT], t2[:, :, e], 0.0, ALU.mult, ALU.add))
                    link(dve.tensor_tensor(base[:], base[:], t2[:], ALU.subtract))
                    link(dve.tensor_tensor(flat(base[:]), flat(base[:]), psA[:, 0, :], ALU.add))

                rank(0)
                link(dve.tensor_tensor(base[:], base[:], over_n(need[:]), ALU.is_lt))
                link(dve.tensor_tensor(t[:], t[:], base[:], ALU.mult))
                dve.tensor_tensor(t[:], t[:], gt[:], ALU.add).then_inc(mask_ready, 1)
                link(dve.tensor_scalar(first[:], iota[:], float(CAP), None, ALU.mult))
                rank(1)
                link(dve.tensor_tensor(base[:], base[:], over_n(first[:]), ALU.add))
                for k in range(2):
                    link(dve.tensor_tensor(t2[:], oh[:, k], t[:], ALU.mult))
                    link(dve.tensor_reduce(kept[:, k, :], t2[:], AX.X, ALU.add))
                    link(dve.tensor_tensor(t2[:], t2[:], base[:], ALU.mult))
                    link(dve.tensor_reduce(dest[:, k, :], t2[:], AX.X, ALU.add))
                    link(dve.tensor_tensor(gate[:, k, :], w[:, k, :], kept[:, k, :], ALU.mult))
                link(dve.tensor_scalar(kept[:], kept[:], -float(NSLOT), float(NSLOT), ALU.mult, ALU.add))
                link(dve.tensor_tensor(pos[:], dest[:], kept[:], ALU.add))
                link(dve.tensor_scalar(kept[:], pos[:], float(NSLOT), None, ALU.is_lt))
                link(dve.tensor_tensor(row_of[:], pos[:], kept[:], ALU.mult))
                dve.sem_clear(step_done)
                def indices(i):
                    for b in range(2):
                        if not isinstance(i, int):
                            dve.wait_ge(scattered[b], i * (2 * G * 16))
                        dve.tensor_copy(ibuf[:, b], pos[:, :, bass.ds(i * (2 * G) + b * G, G)]).then_inc(index_ready, 1)

                indices(0)
                with dve.Fori(1, NT // (2 * G)) as i:
                    indices(i)


def moe_experts(nc, slots_dram, y_dram, w1, b1, w2, b2, ident_in):
    NS, HC, NB = CAP // P, CAP // 2, 2 * (FF // P)
    TURNS = NE // 2
    with ExitStack() as ctx:
        sb, ps, sem = makers(nc, ctx, "e")
        ident = sb("ident", [P, P])
        xs, xT = sb("xs", [P, 2, NS, DM]), sb("xT", [P, 2, CAP])
        w1s, w2s = sb("w1", [P, 2, FF]), sb("w2", [P, 2, FF // P, DM])
        b1s, b2s = sb("b1", [P, 2, FF // P]), sb("b2", [P, 2, DM])
        hT, ys = sb("hT", [P, FF // P, CAP]), sb("ys", [P, 2, NS, DM])
        psT, psH, psY = ps("psT", [P, 2, 512]), ps("psH", [P, 4, 512]), ps("psY", [P, 2, 512])
        ident_loaded, x_loaded, w_loaded = sem("ident_loaded"), [sem("x_loaded0"), sem("x_loaded1")], [sem("w_loaded0"), sem("w_loaded1")]
        turned, turned_out = sem("turned"), sem("turned_out")
        h_ready, gelu_ready, y_summed, y_ready = sem("h_ready"), sem("gelu_ready"), sem("y_summed"), sem("y_ready")
        stored = [sem("stored0"), sem("stored1")]
        with nc.Block() as block:
            def waiter(eng):
                def wait(semaphore, n):
                    if not (isinstance(n, int) and n <= 0):
                        eng.wait_ge(semaphore, n)
                return wait

            def turns(eng, turn):
                turn(0, False)
                with eng.Fori(1, TURNS - 1) as i:
                    turn(i, False)
                turn(TURNS - 1, True)

            @block.sync
            def _(sp):
                wait = waiter(sp)
                sp.dma_start(ident[:], ident_in).then_inc(ident_loaded, 16)

                def turn(i, last):
                    for b in range(2):
                        wait(turned, i * 2 + b - 1)
                        sp.dma_start(xs[:, b], slots_dram.rearrange("(i b n p) d -> i b p n d", b=2, n=NS, p=P)[bass.ds(i, 1)].rearrange("i b p n d -> b p (i n) d")[b]).then_inc(x_loaded[b], 16)
                        wait(y_summed, i * 2 + b - 1)
                        sp.dma_start(w1s[:, b], w1.rearrange("(i b) p f -> i b p f", b=2)[bass.ds(i, 1)].rearrange("i b p f -> b p (i f)")[b]).then_inc(w_loaded[b], 16)
                        sp.dma_start(w2s[:, b], w2.rearrange("(i b) (c p) f -> i b p c f", b=2, p=P)[bass.ds(i, 1)].rearrange("i b p c f -> b p (i c) f")[b]).then_inc(w_loaded[b], 16)
                        sp.dma_start(b1s[:, b], b1.rearrange("(i b) p c -> i b p c", b=2)[bass.ds(i, 1)].rearrange("i b p c -> b p (i c)")[b]).then_inc(w_loaded[b], 16)
                        wait(y_ready, (i * 2 + b - 1) * 2)
                        sp.dma_start(b2s[:, b], b2.rearrange("(i b) f -> i b f", b=2)[bass.ds(i, 1)].rearrange("i b f -> b i f")[b].broadcast_to([P, DM])).then_inc(w_loaded[b], 16)

                turns(sp, turn)

            @block.tensor
            def _(pe):
                wait = waiter(pe)

                def turn_rows(i, b):
                    wait(x_loaded[b], i * 16 + 16)
                    wait(turned_out, (i * 2 + b) * 2)
                    for n in range(NS):
                        mm = pe.transpose(psT[:, n // 4, n % 4 * P:(n % 4 + 1) * P], xs[:, b, n, :], ident[:])
                    mm.then_inc(turned, 1)

                def turn(i, last):
                    for b in range(2):
                        e = i * 2 + b
                        wait(w_loaded[b], i * 64 + 64)
                        wait(turned_out, e * 2 + 2)
                        for f in range(FF // P):
                            for q in range(2):
                                k = 2 * f + q
                                wait(gelu_ready, e * NB + k - 3)
                                pe.matmul(psH[:, k % 4, 0:HC], lhsT=w1s[:, b, f * P:(f + 1) * P], rhs=xT[:, b, q * HC:(q + 1) * HC],
                                          start=True, stop=True).then_inc(h_ready, 1)
                        if b == 0:
                            turn_rows(i, 1)
                        elif not last:
                            turn_rows(i + 1, 0)
                        wait(gelu_ready, e * NB + NB)
                        wait(y_ready, e * 2)
                        for n in range(NS):
                            for f in range(FF // P):
                                mm = pe.matmul(psY[:, n // 4, n % 4 * P:(n % 4 + 1) * P], lhsT=hT[:, f, n * P:(n + 1) * P], rhs=w2s[:, b, f, :],
                                               start=f == 0, stop=f == FF // P - 1)
                        mm.then_inc(y_summed, 1)

                pe.wait_ge(ident_loaded, 16)
                turn_rows(0, 0)
                turns(pe, turn)

            @block.scalar
            def _(act):
                wait = waiter(act)

                def evict(e, b):
                    wait(turned, e + 1)
                    wait(h_ready, e * NB - NB)
                    act.activation(xT[:, b, 0:512], psT[:, 0, :], ACT.Copy).then_inc(turned_out, 1)
                    act.activation(xT[:, b, 512:CAP], psT[:, 1, 0:CAP - 512], ACT.Copy).then_inc(turned_out, 1)

                def turn(i, last):
                    for b in range(2):
                        e = i * 2 + b
                        wait(y_summed, e)
                        for f in range(FF // P):
                            for q in range(2):
                                wait(h_ready, e * NB + 2 * f + q + 1)
                                act.activation(hT[:, f, q * HC:(q + 1) * HC], psH[:, (2 * f + q) % 4, 0:HC], ACT.Gelu,
                                               bias=b1s[:, b, f:f + 1]).then_inc(gelu_ready, 1)
                        if b == 0 or not last:
                            evict(e + 1, 1 - b)

                evict(0, 0)
                turns(act, turn)

            @block.vector
            def _(dve):
                wait = waiter(dve)

                def turn(i, last):
                    for b in range(2):
                        wait(y_summed, i * 2 + b + 1)
                        wait(stored[b], i * 16)
                        dve.tensor_tensor(ys[:, b, 0:4, :], psY[:, 0, :].rearrange("p (n d) -> p n d", n=4),
                                          b2s[:, b, :].unsqueeze(1).broadcast_to([P, 4, DM]), ALU.add).then_inc(y_ready, 1)
                        dve.tensor_tensor(ys[:, b, 4, :], psY[:, 1, 0:P], b2s[:, b, :], ALU.add).then_inc(y_ready, 1)

                turns(dve, turn)

            @block.gpsimd
            def _(pool):
                def turn(i, last):
                    for b in range(2):
                        pool.wait_ge(y_ready, (i * 2 + b) * 2 + 2)
                        pool.dma_start(y_dram.rearrange("(i b n p) d -> i b p n d", b=2, n=NS, p=P)[bass.ds(i, 1)].rearrange("i b p n d -> b p (i n) d")[b], ys[:, b]).then_inc(stored[b], 16)

                turns(pool, turn)
                for b in range(2):
                    pool.wait_ge(stored[b], 16 * TURNS)


def moe_combine(nc, xn_dram, moe_dram, x1_dram, x1_out, xn2_dram, xn2T_dram, gamma, beta, ident_in,
                zero_next, load_next):
    with ExitStack() as ctx:
        sb, ps, sem = makers(nc, ctx, "c")
        F_, X1, SQ = sb("F", [P, NT, DM]), sb("X1", [P, NT, DM]), sb("SQ", [P, NT, DM])
        MO, XT = sb("MO", [P, NT, DM]), sb("XT", [P, NTOK])
        gam, bet, ident = sb("gam", [P, DM]), sb("bet", [P, DM]), sb("ident", [P, P])
        stat = sb("stat", [P, 4, NT])
        psT = ps("psT", [P, 4, 512])
        GR = 4
        N = NT // GR
        consts_loaded, loaded = sem("consts_loaded"), [sem(f"loaded{g}") for g in range(GR)]
        mean_ready, centred, squared = sem("mean_ready"), sem("centred"), sem("squared")
        var_ready, std_ready, xn_ready, x1_ready = sem("var_ready"), sem("std_ready"), sem("xn_ready"), sem("x1_ready")
        turned, evicted, stored, step_done = sem("turned"), sem("evicted"), sem("stored"), sem("step_done")
        tok = lambda a, g: a.rearrange("(n p) d -> p n d", p=P)[:, g * N:(g + 1) * N, :]
        row = lambda a: a.rearrange("(o d) -> o d", o=1).broadcast_to([P, DM])
        part = lambda t, g: t[:, g * N:(g + 1) * N, :]
        ORDER = [(0, 0)] + [s for g in range(1, GR) for s in ((g, 0), (g - 1, 1))] + [(GR - 1, 1)]
        with nc.Block() as block:
            @block.sync
            def _(sp):
                for g in range(GR):
                    for dst, src in ((F_, xn_dram), (MO, moe_dram), (X1, x1_dram)):
                        sp.dma_start(part(dst, g), tok(src, g)).then_inc(loaded[g], 16)
                    if g == 0:
                        for dst, src in ((gam[:], row(gamma)), (bet[:], row(beta)), (ident[:], ident_in)):
                            sp.dma_start(dst, src).then_inc(consts_loaded, 16)
                load_next(sp)
                for g in range(GR):
                    sp.wait_ge(x1_ready, g + 1)
                    sp.dma_start(tok(x1_out, g), part(X1, g)).then_inc(stored, 16)
                    sp.wait_ge(xn_ready, g + 1)
                    sp.dma_start(tok(xn2_dram, g), part(F_, g)).then_inc(stored, 16)
                    sp.wait_ge(evicted, (g + 1) * N // 4)
                    sp.dma_start(xn2T_dram[:, g * N * P:(g + 1) * N * P], XT[:, g * N * P:(g + 1) * N * P]).then_inc(stored, 16)
                sp.wait_ge(stored, 48 * GR)

            @block.gpsimd
            def _(pool):
                zero_next(pool)

            @block.vector
            def _(dve):
                done = [0]

                def link(ins):
                    done[0] += 1
                    ins.then_inc(step_done, 1)
                    dve.wait_ge(step_done, done[0])

                def begin(m, g, k):
                    v, st = part(F_, g), lambda r: stat[:, r, g * N:(g + 1) * N]
                    if k == 0:
                        dve.wait_ge(loaded[g], 48)
                        link(dve.tensor_tensor(v, v, part(MO, g), ALU.add))
                    link(dve.tensor_reduce(st(0), v, AX.X, ALU.add))
                    dve.tensor_scalar(st(0), st(0), -1.0 / DM, None, ALU.mult).then_inc(mean_ready, 1)

                def variance(m, g):
                    dve.wait_ge(squared, m + 1)
                    st = lambda r: stat[:, r, g * N:(g + 1) * N]
                    link(dve.tensor_reduce(st(1), part(SQ, g), AX.X, ALU.add))
                    dve.tensor_scalar(st(1), st(1), 1.0 / DM, EPS, ALU.mult, ALU.add).then_inc(var_ready, 1)

                def end(m, g, k):
                    v, st = part(F_, g), lambda r: stat[:, r, g * N:(g + 1) * N]
                    dve.wait_ge(std_ready, m + 1)
                    link(dve.reciprocal(st(3), st(2)))
                    if k == 1:
                        dve.tensor_tensor(v, v, bcast(st(3), DM), ALU.mult).then_inc(xn_ready, 1)
                        return
                    link(dve.tensor_tensor(v, v, bcast(st(3), DM), ALU.mult))
                    link(dve.tensor_tensor(v, v, gam[:].unsqueeze(1).broadcast_to([P, N, DM]), ALU.mult))
                    link(dve.tensor_tensor(v, v, bet[:].unsqueeze(1).broadcast_to([P, N, DM]), ALU.add))
                    dve.tensor_tensor(part(X1, g), part(X1, g), v, ALU.add).then_inc(x1_ready, 1)
                    dve.wait_ge(x1_ready, g + 1)
                    link(dve.tensor_copy(v, part(X1, g)))

                dve.wait_ge(consts_loaded, 48)
                begin(0, *ORDER[0])
                for m, (g, k) in enumerate(ORDER):
                    if m + 2 < len(ORDER):
                        begin(m + 1, *ORDER[m + 1])
                    variance(m, g)
                    end(m, g, k)
                    if m + 2 == len(ORDER):
                        begin(m + 1, *ORDER[m + 1])

            @block.scalar
            def _(act):
                def evict(g):
                    for t in range(g * N // 4, (g + 1) * N // 4):
                        act.wait_ge(turned, t + 1)
                        act.activation(XT[:, t * 512:(t + 1) * 512], psT[:, t % 4, :], ACT.Copy).then_inc(evicted, 1)

                def std(m):
                    act.wait_ge(var_ready, m + 1)
                    g = ORDER[m][0]
                    act.activation(stat[:, 2, g * N:(g + 1) * N], stat[:, 1, g * N:(g + 1) * N], ACT.Sqrt).then_inc(std_ready, 1)

                def centre(m):
                    g = ORDER[m][0]
                    act.wait_ge(mean_ready, m + 1)
                    for n in range(g * N, (g + 1) * N):
                        ins = act.activation(F_[:, n, :], F_[:, n, :], ACT.Identity, bias=stat[:, 0, n:n + 1])
                    ins.then_inc(centred, 1)
                    act.wait_ge(centred, m + 1)
                    act.activation(part(SQ, g), part(F_, g), ACT.Square).then_inc(squared, 1)

                centre(0)
                for m in range(len(ORDER)):
                    std(m)
                    if m + 1 < len(ORDER):
                        centre(m + 1)
                    if m > 0 and ORDER[m - 1][1] == 1:
                        evict(ORDER[m - 1][0])
                evict(GR - 1)

            @block.tensor
            def _(pe):
                pe.wait_ge(consts_loaded, 48)
                for t in range(NT // 4):
                    pe.wait_ge(xn_ready, 4 * t // N + 1)
                    if t >= 4:
                        pe.wait_ge(evicted, t - 3)
                    for k in range(4):
                        mm = pe.transpose(psT[:, t % 4, k * P:(k + 1) * P], F_[:, 4 * t + k, :], ident[:])
                    mm.then_inc(turned, 1)
class Layer1Constants:
    LOADS = 17

    def __init__(self, nc, ctx):
        sb, _, sem = makers(nc, ctx, "lc")
        self.wqkv, self.wb, self.cw, self.wo = sb("wqkv", [P, 3, P]), sb("wb", [P, AH]), sb("cw", [P, 3, 4]), sb("wo", [P, P])
        self.grms, self.lng, self.lnb, self.ident = sb("grms", [P, AD]), sb("lng", [P, DM]), sb("lnb", [P, DM]), sb("ident", [P, P])
        self.levels = sb("levels", [P, 2, NLEV, P])
        self.masks = sb("masks", [P, 2, P])
        self.wgu, self.wd = sb("wgu", [P, 6, DM]), sb("wd", [P, FI])
        self.loaded, self.zeroed = sem("loaded"), sem("zeroed")

    def zero(self, pool):
        pool.memset(self.wgu[:], 0.0).then_inc(self.zeroed, 1)

    def load(self, sp, t):
        row = lambda a: a.rearrange("(o d) -> o d", o=1)
        for dst, src in ((self.wqkv, t["wqkv"]), (self.wb, t["wb"]), (self.cw, t["cw"]), (self.wo, t["wo"]), (self.ident, t["ident"]),
                         (self.grms, row(t["grms"]).broadcast_to([P, AD])), (self.lng, row(t["lng"]).broadcast_to([P, DM])),
                         (self.lnb, row(t["lnb"]).broadcast_to([P, DM])), (self.levels, t["levels"]), (self.masks, t["masks"]),
                         (self.wd, t["wd"])):
            sp.dma_start(dst[:], src).then_inc(self.loaded, 16)
        sp.wait_ge(self.zeroed, 1)
        for k in range(2):
            for c, (c0, n) in enumerate(FCH):
                sp.dma_start(self.wgu[0:n, 3 * k + c, :], t["wgu"][k, c0:c0 + n, :]).then_inc(self.loaded, 16)


def layer1(nc, xn2_dram, xn2T_dram, x1_dram, out_dram, consts):
    NPAIR, ROW, G = B // 2, 2 * L, 4
    NL = NLEV - 1
    SLOTS = 2 * (NL + 2)
    AT = dict(dve_sq=0, act_rms=1, dve_on=1, pe_oT=2, act_oT=2, pe_y=3, dve_res=3, act_std=4, dve_ln=5, pe_xqT=4,
              act_xqT=4, pe_gu=5, act_gu=5, dve_gu=5, pe_hT=12, act_hT=13, pe_down=13, dve_down=14, pe_proj=7, act_proj=7,
              act_silu=10, pe_tok=11, act_tok=12, dve_nsq=12, act_norm=13, dve_norm=13, pe_fm=14, act_fm=14, act_bd=1)
    CONV = (7, 8, 9)
    XQ, HQ = {0: 3, 1: 3, 2: 6, 3: 2}, {6: 1, 7: 4, 8: 2, 9: 1, 10: 3, 11: 2, 13: 1}
    with ExitStack() as ctx:
        sb, ps, sem = makers(nc, ctx, "a")
        wqkv_s, wb_s, cw, wo_s, ident = consts.wqkv, consts.wb, consts.cw, consts.wo, consts.ident
        grms_s, lng_s, lnb_s, lev, masks = consts.grms, consts.lng, consts.lnb, consts.levels, consts.masks
        wgu_s, wd_s = consts.wgu, consts.wd
        xT, xres, acc = sb("xT", [P, ROW]), sb("xres", [P, G, DM]), sb("acc", [P, G, DM])
        pad, qkv = sb("pad", [P, 3, 2, 3 + L]), sb("qkv", [P, 3, ROW])
        beta = sb("beta", [P, 2, G, AH])
        tok = sb("tok", [P, G, 4, P])
        sq, ss = sb("sq", [P, G, 2, P]), sb("ss", [P, G, 2, AH])
        fm = sb("fm", [P, G, 3, P])
        late = sb("late", [P, 2, 3, P])
        bd = sb("bd", [P, 2, 2, 3, AH, P])
        M, X, XT, QT = (sb(n, [P, 2, AH, P]) for n in ("M", "X", "XT", "QT"))
        PT = sb("PT", [P, 2, AH, P])
        R, D, S = sb("R", [P, 2, P]), sb("D", [P, 2, P]), sb("S", [P, 2, P])
        o, oT, osq = sb("o", [P, G, P]), sb("oT", [P, G, P]), sb("osq", [P, G, P])
        rs, st = sb("rs", [P, 2, 16]), sb("st", [P, 4, G])
        wguT, wdT = sb("wguT", [P, 2, FI]), sb("wdT", [P, 3, DM])
        x, xq, xqT = sb("x", [P, G, DM]), sb("xq", [P, G, DM]), sb("xqT", [P, G * P])
        g, h, hqT = sb("g", [P, 2, FI]), sb("h", [P, G, FI]), sb("hqT", [P, G, 3, P])
        NMAX = G * FI
        a, lo, hi = sb("a", [P, NMAX]), sb("lo", [P, NMAX]), sb("hi", [P, NMAX])
        hq = a
        scale, rscale = sb("scale", [P, NMAX // QB]), sb("rscale", [P, NMAX // QB])
        bank = ps("bank", [P, 8, 512])
        names = """pads_zeroed xT_loaded xres_loaded acc_loaded x_loaded stored
            gram_ready m_out pt_out x_ready q_ready q_out xx_ready x_reset level_begun ks_ready r_ready d_ready d_out
            o_ready o_out s_ready s_out
            rms_sq rms_root on_ready oT_ready oT_out y_ready y_out var_ready std_ready res_added
            xq_ready xqT_ready xqT_out gu_ready g_out h_out hq_ready hT_ready hT_out down_ready down_out
            proj_ready proj_out beta_ready beta_out conv_ready silu_ready tok_ready tok_out norm_sq norm_root keys_ready
            fm_ready fm_out bd_out late_out wq_ready wT_ready wT_out dve_step""".split()
        s_ = {n: sem(n) for n in names}
        s_["consts_loaded"] = consts.loaded
        pair = lambda t, i: t.rearrange("(i n p) d -> i p n d", p=P, n=G)[bass.ds(i, 1)].rearrange("i p n d -> p (i n) d")
        flat = lambda t: t.rearrange("p h t -> p (h t)")
        h4 = lambda k: bank[:, k, :].rearrange("p (h t) -> p h t", h=AH)
        over_h = lambda t: t.unsqueeze(1).broadcast_to([P, AH, P])
        over_n = lambda t: t.unsqueeze(1).broadcast_to([P, G, DM])
        cols = lambda t, n, odd: t.rearrange("p (g two n) -> p g two n", two=2, n=n)[:, :, odd, :]
        cols_h = lambda t, n, odd: t.rearrange("p h (g two n) -> p h g two n", two=2, n=n)[:, :, :, odd, :]
        A, C = (0, 2), (1, 3)
        at = lambda i, ck, s: (i * 2 + ck) * 2 + s

        with nc.Block() as block:
            @block.sync
            def _(sp):
                def turn(i, has_last, has_next):
                    if has_next:
                        sp.wait_ge(s_["beta_ready"], i + 1)
                        sp.dma_start(xT[:], xn2T_dram[:, bass.ds((i + 1) * ROW, ROW)]).then_inc(s_["xT_loaded"], 16)
                    if has_last:
                        sp.dma_start(xres[:], pair(xn2_dram, i - 1)).then_inc(s_["xres_loaded"], 16)
                    sp.wait_ge(s_["xq_ready"], i)
                    sp.dma_start(x[:], pair(xn2_dram, i)).then_inc(s_["x_loaded"], 16)
                    if has_last:
                        sp.wait_ge(s_["res_added"], i)
                        sp.dma_start(pair(out_dram, i - 1), acc[:]).then_inc(s_["stored"], 16)
                        sp.wait_ge(s_["stored"], i * 16)
                    sp.dma_start(acc[:], pair(x1_dram, i)).then_inc(s_["acc_loaded"], 16)

                sp.dma_start(xT[:], xn2T_dram[:, 0:ROW]).then_inc(s_["xT_loaded"], 16)
                turn(0, False, True)
                with sp.Fori(1, NPAIR - 1) as i:
                    turn(i, True, True)
                turn(NPAIR - 1, True, False)
                sp.wait_ge(s_["res_added"], NPAIR - 1)
                sp.dma_start(xres[:], pair(xn2_dram, NPAIR - 1)).then_inc(s_["xres_loaded"], 16)
                sp.wait_ge(s_["res_added"], NPAIR)
                sp.dma_start(pair(out_dram, NPAIR - 1), acc[:]).then_inc(s_["stored"], 16)
                sp.wait_ge(s_["stored"], NPAIR * 16)

            @block.gpsimd
            def _(pool):
                pool.memset(pad[:, :, :, 0:3], 0.0)
                pool.memset(QT[:], 0.0)
                pool.memset(bd[:], 0.0).then_inc(s_["pads_zeroed"], 1)

            @block.tensor
            def _(pe):
                def wait(name, n):
                    pe.wait_ge(s_[name], n)

                def mm(out, lhsT, rhs, start=True, stop=True, **kw):
                    return pe.matmul(out, lhsT=lhsT, rhs=rhs, start=start, stop=stop, **kw)

                def main(i, slot):
                    ck, k = divmod(slot, NL + 2)
                    if k == 0:
                        wait("bd_out", 2 * i + ck + 1)
                        wait("fm_out", i * 4 + 4)
                        wait("o_out", at(i, ck, 0))
                        wait("s_out", i * 2 + 2 * ck)
                        for s in range(2):
                            n = 2 * s + ck
                            mm(bank[:, A[s], :], fm[:, n, 2, :], flat(bd[:, ck, s, 1]))
                            mm(bank[:, C[s], :], fm[:, n, 1, :], flat(bd[:, ck, s, 2])).then_inc(s_["gram_ready"], 1)
                        if ck == 0:
                            wait("down_out", i)
                        else:
                            wait("proj_out", i * 3 + 6) if not last else wait("hT_out", i * 4)
                        for s in range(2):
                            n = 2 * s + ck
                            mm(bank[:, 4 + s, :], fm[:, n, 1, :], flat(bd[:, ck, s, 0])).then_inc(s_["gram_ready"], 1)
                    elif k <= NL:
                        l = k - 1
                        for s in range(2):
                            wait("x_ready", at(i, ck, 0) * (NL + 1) + 2 * l + s + 1)
                            if l == 0:
                                wait("m_out", at(i, ck, s) + 1)
                            for hd in range(AH):
                                ins = mm(bank[:, A[s], hd * P:(hd + 1) * P], M[:, s, hd, :], XT[:, s, hd, :])
                            ins.then_inc(s_["q_ready"], 1)
                        for s in range(2):
                            wait("q_out", at(i, ck, 0) * NL + 2 * l + s + 1)
                            if l < NL - 1:
                                for hd in range(AH):
                                    mm(bank[:, A[s], hd * P:(hd + 1) * P], QT[:, s, hd, :], X[:, s, hd, :])
                            for hd in range(AH):
                                ins = mm(bank[:, C[s], hd * P:(hd + 1) * P], X[:, s, hd, :], QT[:, s, hd, :])
                            ins.then_inc(s_["xx_ready"], 1)
                    else:
                        if ck == 1:
                            wait("late_out", i + 1)
                            wait("s_out", i * 2 + 2)
                            for s in range(2):
                                mm(bank[:, A[s], 0:P], late[:, s, 1, :], S[:, s, :]).then_inc(s_["ks_ready"], 1)
                        for s in range(2):
                            if ck == 1:
                                wait("r_ready", i * 2 + s + 1)
                            r = R[:, s, :] if ck else tok[:, 2 * s, 2, :]
                            wait("x_ready", at(i, ck, 0) * (NL + 1) + 2 * NL + s + 1)
                            for hd in range(AH):
                                ins = mm(bank[:, C[s], hd * AD:(hd + 1) * AD], XT[:, s, hd, :], r[:, hd * AD:(hd + 1) * AD])
                            ins.then_inc(s_["d_ready"], 1)
                        wait("pt_out", at(i, ck, 0) + 2)
                        for s in range(2):
                            n = 2 * s + ck
                            wait("d_out", at(i, ck, s) + 1)
                            if ck == 1:
                                mm(bank[:, A[s], P:2 * P], late[:, s, 0, :], S[:, s, :], stop=False, skip_group_check=True)
                            for hd in range(AH):
                                ins = mm(bank[:, A[s], P + hd * AD:P + (hd + 1) * AD], PT[:, s, hd, :], D[:, s, hd * AD:(hd + 1) * AD],
                                         start=ck == 0, skip_group_check=ck == 1)
                            ins.then_inc(s_["o_ready"], 1)
                            if ck == 0:
                                mm(bank[:, C[s], P:2 * P], tok[:, n, 1, :], D[:, s, :]).then_inc(s_["s_ready"], 1)

                def tail(i, slot):
                    if slot == AT["pe_oT"]:
                        wait("on_ready", i + 1)
                        for n in range(G):
                            ins = pe.transpose(bank[:, 6, n * P:(n + 1) * P], o[:, n, :], ident[:])
                        ins.then_inc(s_["oT_ready"], 1)
                    if slot == AT["pe_y"]:
                        wait("oT_out", i + 1)
                        for n in range(G):
                            ins = mm(bank[:, 7, n * P:(n + 1) * P], oT[:, n, :], wo_s[:])
                        ins.then_inc(s_["y_ready"], 1)

                def feed(i, slot):
                    if slot == AT["pe_xqT"]:
                        wait("xq_ready", i + 1)
                        for n in range(G):
                            ins = pe.transpose(bank[:, 6, n * P:(n + 1) * P], xq[:, n, :], ident[:])
                        ins.then_inc(s_["xqT_ready"], 1)
                    if slot in (AT["pe_gu"], AT["pe_gu"] + 1):
                        wait("xqT_out", i + 1)
                        wait("pt_out", at(i, 0, 0) + 2)
                        wait("y_out", i)
                        for n in range(2 * (slot - AT["pe_gu"]), 2 * (slot - AT["pe_gu"]) + 2):
                            wait("h_out", i * G + (n - 2 if n > 1 else 0) + (1 if n > 1 else 0))
                            for k in range(2):
                                ins = mm(bank[:, 4 + 2 * (n % 2) + k, 0:FI], xqT[:, n * P:(n + 1) * P], wguT[:, k, :])
                            ins.then_inc(s_["gu_ready"], 1)
                    if slot == AT["pe_hT"]:
                        wait("hq_ready", i + 1)
                        if not last:
                            wait("tok_out", (i + 1) * 4 + 4)
                        wait("pt_out", at(i, 1, 0) + 2)
                        for n in range(G):
                            for c, (c0, m) in enumerate(FCH):
                                ins = pe.transpose(bank[0:m, 4 + n, c * P:(c + 1) * P], hq[:, n * FI + c0:n * FI + c0 + m], ident[:])
                            ins.then_inc(s_["hT_ready"], 1)
                    if slot == AT["pe_down"]:
                        for n in range(G):
                            wait("hT_out", G * i + n + 1)
                            for c, (c0, m) in enumerate(FCH):
                                ins = mm(bank[:, 4, n * P:(n + 1) * P], hqT[0:m, n, c, :], wdT[0:m, c, :], start=c == 0, stop=c == 2)
                        ins.then_inc(s_["down_ready"], 1)

                def head(i, slot, alone=False):
                    if slot == AT["pe_proj"]:
                        wait("xT_loaded", 16 * i + 16)
                        if not alone:
                            wait("h_out", i * G)
                        for j in range(3):
                            mm(bank[:, 4 + j, :], wqkv_s[:, j, :], xT[:]).then_inc(s_["proj_ready"], 1)
                        for n in range(G):
                            ins = mm(bank[:, 7, n * AH:(n + 1) * AH], xT[:, n * P:(n + 1) * P], wb_s[:])
                        ins.then_inc(s_["beta_ready"], 1)
                    if slot == AT["pe_tok"]:
                        wait("silu_ready", 3 * i + 3)
                        wait("beta_out", 2 * i + 1)
                        if not alone:
                            wait("pt_out", at(i, 0, 0))
                        for n in range(G):
                            for j in range(3):
                                ins = pe.transpose(bank[:, 4 + n, j * P:(j + 1) * P], qkv[:, j, n * P:(n + 1) * P], ident[:])
                            ins.then_inc(s_["tok_ready"], 1)
                    if slot == AT["pe_fm"]:
                        wait("keys_ready", i + 1)
                        if not alone:
                            wait("down_out", i)
                        for n in range(G):
                            for j, src in enumerate((0, 1, 3)):
                                ins = pe.transpose(bank[:, 4 + n, j * P:(j + 1) * P], tok[:, n, src, :], ident[:])
                            ins.then_inc(s_["fm_ready"], 1)

                last = False
                wait("consts_loaded", 16 * consts.LOADS)
                wait("pads_zeroed", 1)
                for slot in range(SLOTS):
                    head(0, slot, alone=True)
                wait("wq_ready", 2)
                wguq = a[:, 0:6 * DM].rearrange("p (k d) -> p k d", k=6)
                for k in range(2):
                    for c, (c0, n) in enumerate(FCH):
                        pe.transpose(bank[:, k, c0:c0 + n], wguq[0:n, 3 * k + c, :], ident[0:n, 0:n])
                for c, (c0, n) in enumerate(FCH):
                    ins = pe.transpose(bank[0:n, 2, c * P:(c + 1) * P], a[:, 6 * DM + c0:6 * DM + c0 + n], ident[:])
                ins.then_inc(s_["wT_ready"], 1)
                wait("wT_out", 5)

                def turn(i, has_last, has_next):
                    for slot in range(SLOTS):
                        main(i, slot)
                        if has_last:
                            tail(i - 1, slot)
                        feed(i, slot)
                        if has_next:
                            head(i + 1, slot)

                turn(0, False, True)
                with pe.Fori(1, NPAIR - 1) as i:
                    turn(i, True, True)
                last = True
                turn(NPAIR - 1, True, False)
                for slot in range(SLOTS):
                    tail(NPAIR - 1, slot)

            @block.scalar
            def _(act):
                def wait(name, n):
                    act.wait_ge(s_[name], n)

                def copy(out, in_):
                    return act.activation(out, in_, ACT.Copy)

                def reset(s):
                    copy(X[:, s], over_h(ident[:]))
                    copy(XT[:, s], over_h(ident[:])).then_inc(s_["x_reset"], 1)

                def main(i, slot):
                    ck, k = divmod(slot, NL + 2)
                    if k == 0:
                        for s in range(2):
                            wait("gram_ready", at(i, ck, 0) * 2 + s + 1)
                            copy(M[:, s], h4(A[s])).then_inc(s_["m_out"], 1)
                    elif k <= NL:
                        for s in range(2):
                            wait("q_ready", at(i, ck, 0) * NL + 2 * (k - 1) + s + 1)
                            copy(cols_h(QT[:, s], 1 << k, 1), cols_h(h4(A[s]), 1 << k, 1)).then_inc(s_["q_out"], 1)
                    else:
                        for s in range(2):
                            wait("d_ready", at(i, ck, s) + 1)
                            copy(D[:, s, :], bank[:, C[s], 0:P]).then_inc(s_["d_out"], 1)
                        for s in range(2):
                            reset(s)
                        for s in range(2):
                            wait("o_ready", at(i, ck, s) + 1)
                            copy(o[:, 2 * s + ck, :], bank[:, A[s], P:2 * P]).then_inc(s_["o_out"], 1)

                def tail(i, slot):
                    if slot == AT["act_rms"]:
                        wait("rms_sq", i + 1)
                        act.activation(rs[:, 1, :], rs[:, 0, :], ACT.Sqrt).then_inc(s_["rms_root"], 1)
                    if slot == AT["act_oT"]:
                        wait("oT_ready", i + 1)
                        copy(oT[:], bank[:, 6, :].rearrange("p (n t) -> p n t", n=G)).then_inc(s_["oT_out"], 1)
                    if slot == AT["act_std"]:
                        wait("var_ready", i + 1)
                        act.activation(st[:, 2, :], st[:, 1, :], ACT.Sqrt).then_inc(s_["std_ready"], 1)

                def feed(i, slot):
                    if slot == AT["act_xqT"]:
                        wait("xqT_ready", i + 1)
                        copy(xqT[:], bank[:, 6, :]).then_inc(s_["xqT_out"], 1)
                    if slot in (AT["act_gu"], AT["act_gu"] + 1):
                        for n in range(2 * (slot - AT["act_gu"]), 2 * (slot - AT["act_gu"]) + 2):
                            wait("gu_ready", G * i + n + 1)
                            if n > 1:
                                wait("h_out", G * i + n - 1)
                            act.activation(g[:, n % 2, :], bank[:, 4 + 2 * (n % 2), 0:FI], ACT.Silu).then_inc(s_["g_out"], 1)
                    if slot == AT["act_hT"]:
                        for n in range(G):
                            wait("hT_ready", G * i + n + 1)
                            copy(hqT[:, n, 0:2, :], bank[:, 4 + n, 0:2 * P].rearrange("p (c t) -> p c t", c=2))
                            copy(hqT[0:96, n, 2, :], bank[0:96, 4 + n, 2 * P:3 * P]).then_inc(s_["hT_out"], 1)

                def head(i, slot):
                    if slot == AT["act_proj"]:
                        wait("conv_ready", 3 * i)
                        for j in range(3):
                            wait("proj_ready", 3 * i + j + 1)
                            copy(pad[:, j, :, 3:], bank[:, 4 + j, :].rearrange("p (s l) -> p s l", s=2)).then_inc(s_["proj_out"], 1)
                        wait("beta_ready", i + 1)
                        wait("keys_ready", i)
                        act.activation(beta[:, 0].rearrange("p n h -> p (n h)"), bank[:, 7, 0:4 * AH], ACT.Sigmoid).then_inc(s_["beta_out"], 1)
                        wait("beta_out", 2 * i + 1)
                        act.activation(beta[:, 1], beta[:, 0], ACT.Copy, scale=-1.0).then_inc(s_["beta_out"], 1)
                    if slot == AT["act_silu"]:
                        for j in range(3):
                            wait("conv_ready", 3 * i + j + 1)
                            act.activation(qkv[:, j, :], qkv[:, j, :], ACT.Silu).then_inc(s_["silu_ready"], 1)
                    if slot == AT["act_tok"]:
                        for n in range(G):
                            wait("tok_ready", 4 * i + n + 1)
                            if n == 0:
                                wait("late_out", i)
                            copy(tok[:, n, 0:3, :], bank[:, 4 + n, 0:3 * P].rearrange("p (j t) -> p j t", j=3)).then_inc(s_["tok_out"], 1)
                    if slot == AT["act_norm"]:
                        wait("norm_sq", i + 1)
                        act.activation(ss[:], ss[:], ACT.Sqrt).then_inc(s_["norm_root"], 1)
                    if slot == AT["act_fm"]:
                        for n in range(G):
                            wait("fm_ready", 4 * i + n + 1)
                            copy(fm[:, n, :, :], bank[:, 4 + n, 0:3 * P].rearrange("p (j t) -> p j t", j=3)).then_inc(s_["fm_out"], 1)
                        heads(i, 0)

                def heads(i, ck):
                    wait("fm_out", 4 * i + 4)
                    for s in range(2):
                        for hd in range(AH):
                            rows = slice(hd * AD, (hd + 1) * AD)
                            ins = copy(bd[rows, ck, s, :, hd, :], fm[rows, 2 * s + ck, :, :])
                    ins.then_inc(s_["bd_out"], 1)

                def turn(i, has_last, has_next):
                    for slot in range(SLOTS):
                        main(i, slot)
                        if slot == AT["act_bd"]:
                            heads(i, 1)
                        if slot == 8:
                            wait("ks_ready", i * 2)
                            wait("r_ready", i * 2)
                            wait("o_ready", i * 4 + 2)
                            for s in range(2):
                                copy(late[:, s, 0:2, :], fm[:, 2 * s + 1, 0::2, :])
                                ins = copy(late[:, s, 2, :], tok[:, 2 * s + 1, 2, :])
                            ins.then_inc(s_["late_out"], 1)
                        if has_last:
                            tail(i - 1, slot)
                        feed(i, slot)
                        if has_next:
                            head(i + 1, slot)

                wait("pads_zeroed", 1)
                wait("consts_loaded", 16 * consts.LOADS)
                for s in range(2):
                    reset(s)
                for slot in range(SLOTS):
                    head(0, slot)
                wait("wT_ready", 1)
                for k in range(2):
                    copy(wguT[:, k, :], bank[:, k, 0:FI]).then_inc(s_["wT_out"], 1)
                for c, (c0, n) in enumerate(FCH):
                    copy(wdT[0:n, c, :], bank[0:n, 2, c * P:(c + 1) * P]).then_inc(s_["wT_out"], 1)
                turn(0, False, True)
                with act.Fori(1, NPAIR - 1) as i:
                    turn(i, True, True)
                turn(NPAIR - 1, True, False)
                for slot in range(SLOTS):
                    tail(NPAIR - 1, slot)

            @block.vector
            def _(dve):
                done = [0]

                def wait(name, n):
                    dve.wait_ge(s_[name], n)

                def link(ins):
                    done[0] += 1
                    ins.then_inc(s_["dve_step"], 1)
                    dve.wait_ge(s_["dve_step"], done[0])

                def clear():
                    dve.sem_clear(s_["dve_step"])
                    done[0] = 0

                def grow(t, k, T, source):
                    mask = cols(lev[:, t, k, :], 1 << k, t).unsqueeze(1).broadcast_to([P, AH, P >> (k + 1), 1 << k])
                    return dve.copy_predicated(cols_h(T, 1 << k, t), mask.bitcast(I32), source)

                def main(i, slot):
                    ck, k = divmod(slot, NL + 2)
                    if k == 0:
                        for s in range(2):
                            wait("m_out", at(i, ck, s) + 1)
                            wait("x_reset", at(i, ck, s) + 1)
                            dve.sem_inc(s_["level_begun"], 1)
                            grow(0, 0, X[:, s], cols_h(M[:, s], 1, 0))
                            grow(1, 0, XT[:, s], cols_h(h4(C[s]), 1, 1)).then_inc(s_["x_ready"], 1)
                        wait("o_ready", at(i, ck, 0))
                        for s in range(2):
                            wait("gram_ready", at(i, ck, 0) * 2 + 2 + s + 1)
                            dve.tensor_tensor(PT[:, s], h4(4 + s), over_h(masks[:, 0, :]), ALU.mult).then_inc(s_["pt_out"], 1)
                    elif k <= NL:
                        l = k - 1
                        for s in range(2):
                            wait("xx_ready", at(i, ck, 0) * NL + 2 * l + s + 1)
                            dve.sem_inc(s_["level_begun"], 1)
                            if l < NL - 1:
                                grow(0, k, X[:, s], cols_h(h4(A[s]), 1 << k, 0))
                            grow(1, k, XT[:, s], cols_h(h4(C[s]), 1 << k, 1)).then_inc(s_["x_ready"], 1)
                    else:
                        if ck == 1:
                            for s in range(2):
                                wait("ks_ready", i * 2 + s + 1)
                                dve.tensor_tensor(R[:, s, :], late[:, s, 2, :], bank[:, A[s], 0:P], ALU.add).then_inc(s_["r_ready"], 1)
                        if ck == 0:
                            for s in range(2):
                                wait("s_ready", i * 2 + s + 1)
                                dve.tensor_tensor(S[:, s, :], bank[:, C[s], P:2 * P], masks[:, 1, :], ALU.mult).then_inc(s_["s_out"], 1)

                def tail(i, slot):
                    v = xres[:]
                    oh = o[:].rearrange("p n (h d) -> p (n h) d", d=AD)
                    if slot == AT["dve_sq"]:
                        wait("o_out", 4 * i + 4)
                        link(dve.tensor_tensor(osq[:], o[:], o[:], ALU.mult))
                        link(dve.tensor_reduce(rs[:, 0, :], osq[:].rearrange("p n (h d) -> p (n h) d", d=AD), AX.X, ALU.add))
                        dve.tensor_scalar(rs[:, 0, :], rs[:, 0, :], 1.0 / AD, EPS, ALU.mult, ALU.add).then_inc(s_["rms_sq"], 1)
                    if slot == AT["dve_on"]:
                        wait("rms_root", i + 1)
                        link(dve.reciprocal(rs[:, 0, :], rs[:, 1, :]))
                        link(dve.tensor_tensor(oh, oh, bcast(rs[:, 0, :], AD), ALU.mult))
                        dve.tensor_tensor(oh, oh, grms_s[:].unsqueeze(1).broadcast_to([P, 16, AD]), ALU.mult).then_inc(s_["on_ready"], 1)
                    if slot == AT["dve_res"]:
                        wait("y_ready", i + 1)
                        wait("xres_loaded", 16 * i + 16)
                        dve.tensor_tensor(v, v, bank[:, 7, :].rearrange("p (n t) -> p n t", n=G), ALU.add).then_inc(s_["y_out"], 1)
                        wait("y_out", i + 1)
                        link(dve.tensor_reduce(st[:, 0, :], v, AX.X, ALU.add))
                        link(dve.tensor_scalar(st[:, 0, :], st[:, 0, :], 1.0 / DM, None, ALU.mult))
                        link(dve.tensor_tensor(v, v, bcast(st[:, 0, :], DM), ALU.subtract))
                        link(dve.tensor_tensor(osq[:], v, v, ALU.mult))
                        link(dve.tensor_reduce(st[:, 1, :], osq[:], AX.X, ALU.add))
                        dve.tensor_scalar(st[:, 1, :], st[:, 1, :], 1.0 / DM, EPS, ALU.mult, ALU.add).then_inc(s_["var_ready"], 1)
                    if slot == AT["dve_ln"]:
                        wait("std_ready", i + 1)
                        link(dve.reciprocal(st[:, 3, :], st[:, 2, :]))
                        link(dve.tensor_tensor(v, v, bcast(st[:, 3, :], DM), ALU.mult))
                        link(dve.tensor_tensor(v, v, over_n(lng_s[:]), ALU.mult))
                        link(dve.tensor_tensor(v, v, over_n(lnb_s[:]), ALU.add))
                        dve.tensor_tensor(acc[:], acc[:], v, ALU.add).then_inc(s_["res_added"], 1)

                def fp4(dst, src, n, signal, a=a):
                    bits = lambda t: t.bitcast(I32)
                    blocks = lambda t: t.rearrange("p (b k) -> p b k", k=QB)
                    sc, rsc = scale[:, 0:n // QB], rscale[:, 0:n // QB]
                    av, lv, hv = a[:, 0:n], lo[:, 0:n], hi[:, 0:n]
                    link(dve.tensor_reduce(sc, blocks(src), AX.X, ALU.max, apply_absolute_value=True))
                    link(dve.tensor_scalar(sc, sc, 1.0 / 6.0, 1e-12, ALU.mult, ALU.max))
                    link(dve.reciprocal(rsc, sc))
                    link(dve.tensor_scalar(sc, sc, 0.5, None, ALU.mult))
                    yield
                    link(dve.tensor_scalar(bits(av), bits(src), 2 ** 31 - 1, None, ALU.bitwise_and))
                    yield
                    link(dve.tensor_tensor(blocks(av), blocks(av), bcast(rsc, QB), ALU.mult))
                    yield
                    link(dve.tensor_scalar(lv, av, 0.25, None, ALU.is_gt))
                    yield
                    link(dve.tensor_scalar(hv, av, 5.0, 2.0, ALU.is_gt, ALU.mult))
                    for mid in (0.75, 1.25, 1.75):
                        yield
                        link(dve.scalar_tensor_tensor(lv, av, mid, lv, ALU.is_gt, ALU.add))
                    for mid in (2.5, 3.5):
                        yield
                        link(dve.scalar_tensor_tensor(hv, av, mid, hv, ALU.is_gt, ALU.add))
                    yield
                    link(dve.scalar_tensor_tensor(lv, hv, 2.0, lv, ALU.mult, ALU.add))
                    yield
                    link(dve.scalar_tensor_tensor(bits(lv), bits(src), -2 ** 31, bits(lv), ALU.bitwise_and, ALU.bitwise_or))
                    yield
                    dve.tensor_tensor(blocks(dst), blocks(lv), bcast(sc, QB), ALU.mult).then_inc(s_[signal], 1)

                rounding = [None]

                def feed(i, slot):
                    if slot == min(XQ):
                        wait("x_loaded", 16 * i + 16)
                        wait("hT_ready", G * i)
                        rounding[0] = fp4(flat(xq[:]), flat(x[:]), G * DM, "xq_ready")
                    if slot in XQ:
                        for _ in range(XQ[slot]):
                            next(rounding[0], None)
                    if slot in (AT["dve_gu"], AT["dve_gu"] + 1):
                        for n in range(2 * (slot - AT["dve_gu"]), 2 * (slot - AT["dve_gu"]) + 2):
                            wait("g_out", G * i + n + 1)
                            dve.tensor_tensor(h[:, n, :], g[:, n % 2, :], bank[:, 5 + 2 * (n % 2), 0:FI], ALU.mult).then_inc(s_["h_out"], 1)
                    if slot == min(HQ):
                        wait("xq_ready", i + 1)
                        wait("h_out", G * i + G)
                        rounding[0] = fp4(hq[:], flat(h[:]), G * FI, "hq_ready")
                    if slot in HQ:
                        for _ in range(HQ[slot]):
                            next(rounding[0], None)
                    if slot == AT["dve_down"]:
                        wait("down_ready", i + 1)
                        wait("acc_loaded", 16 * i + 16)
                        dve.tensor_tensor(flat(acc[:]), flat(acc[:]), bank[:, 4, :], ALU.add).then_inc(s_["down_out"], 1)

                def head(i, slot):
                    if slot in CONV:
                        for j in [j for j in range(3) if CONV[j] == slot]:
                            wait("proj_out", 3 * i + j + 1)
                            if j == 0:
                                wait("tok_ready", 4 * i)
                            dst = qkv[:, j, :].rearrange("p (s l) -> p s l", s=2)
                            link(dve.tensor_scalar(dst, pad[:, j, :, 0:L], cw[:, j, 0:1], None, ALU.mult))
                            for k in range(1, 4):
                                ins = dve.scalar_tensor_tensor(dst, pad[:, j, :, k:k + L], cw[:, j, k:k + 1], dst, ALU.mult, ALU.add)
                                if k < 3:
                                    link(ins)
                            ins.then_inc(s_["conv_ready"], 1)
                    if slot == AT["dve_nsq"]:
                        wait("tok_out", 4 * i + 4)
                        qk = tok[:, :, 0:2, :]
                        link(dve.tensor_tensor(sq[:], qk, qk, ALU.mult))
                        link(dve.tensor_reduce(ss[:].rearrange("p n j h -> p (n j h)"), sq[:].rearrange("p n j (h d) -> p (n j h) d", d=AD), AX.X, ALU.add))
                        dve.tensor_scalar(ss[:], ss[:], 1e-6, None, ALU.add).then_inc(s_["norm_sq"], 1)
                    if slot == AT["dve_norm"]:
                        wait("norm_root", i + 1)
                        wait("beta_out", 2 * i + 2)
                        link(dve.reciprocal(ss[:], ss[:]))
                        for n in range(G):
                            qh = tok[:, n, 0:2, :].rearrange("p j (h d) -> p (j h) d", d=AD)
                            link(dve.tensor_tensor(qh, qh, bcast(ss[:, n].rearrange("p j h -> p (j h)"), AD), ALU.mult))
                            hd = lambda k: tok[:, n, k, :].rearrange("p (h d) -> p h d", d=AD)
                            dve.tensor_tensor(hd(3), hd(1), bcast(beta[:, 1, n, :], AD), ALU.mult)
                            ins = dve.tensor_tensor(hd(2), hd(2), bcast(beta[:, 0, n, :], AD), ALU.mult)
                            if n < G - 1:
                                link(ins)
                        ins.then_inc(s_["keys_ready"], 1)

                def turn(i, has_last, has_next):
                    for slot in range(SLOTS):
                        main(i, slot)
                        if has_last:
                            tail(i - 1, slot)
                        feed(i, slot)
                        if has_next:
                            head(i + 1, slot)
                    clear()

                wait("consts_loaded", 16 * consts.LOADS)

                def weights():
                    yield from fp4(a[:, 0:6 * DM], flat(wgu_s[:]), 6 * DM, "wq_ready")
                    wait("wq_ready", 1)
                    yield from fp4(a[:, 6 * DM:6 * DM + FI], wd_s[:], FI, "wq_ready", a=a[:, 6 * DM:6 * DM + FI])

                rest = weights()
                for slot in range(SLOTS):
                    head(0, slot)
                    for _ in range(1 if slot < 7 else 2):
                        next(rest, None)
                for _ in rest:
                    pass
                clear()
                turn(0, False, True)
                with dve.Fori(1, NPAIR - 1) as i:
                    turn(i, True, True)
                turn(NPAIR - 1, True, False)
                for slot in range(SLOTS):
                    tail(NPAIR - 1, slot)
def build_program(nc, t):
    scratch = lambda name, shape: nc.dram_tensor(name, shape, F32).ap()
    xn, xnT = scratch("xn_scratch", (NTOK, DM)), scratch("xnT_scratch", (DM, NTOK))
    xa, x1 = scratch("xa_scratch", (NTOK, DM)), scratch("x1_scratch", (NTOK, DM))
    xn2, xn2T = scratch("xn2_scratch", (NTOK, DM)), scratch("xn2T_scratch", (DM, NTOK))
    slots, rows = scratch("slots_scratch", (NSLOT, DM)), scratch("rows_scratch", (NSLOT, DM))
    moe = scratch("moe_scratch", (NTOK, DM))
    with ExitStack() as ctx:
        consts = MambaConstants(nc, ctx)
        row_of = ctx.enter_context(nc.sbuf_tensor("row_of", [P, 2, NT], I32))
        xn_stored = ctx.enter_context(nc.semaphore("xn_stored"))
        gate = ctx.enter_context(nc.sbuf_tensor("gate", [P, 2, NT], F32))
        with ExitStack() as first:
            xrows = first.enter_context(nc.sbuf_tensor("xrows", [P, NT, DM], F32))
            xT = first.enter_context(nc.sbuf_tensor("xT", [P, NTOK], F32))
            route_consts = RouteConstants(nc, first)
            used = norm_input(nc, t["x"], xn, xnT, xrows, xT, t["ident"], xn_stored, lambda sp: route_consts.load(sp, t))
            moe_route(nc, xn, xT, slots, route_consts, row_of, gate, xn_stored, used,
                      lambda sp: consts.load(sp, t))
        moe_experts(nc, slots, rows, t["w1"], t["b1"], t["w2"], t["b2"], t["ident"])
        mamba_fft(nc, t["x"], xnT, xa, consts, rows, moe, row_of, gate)
    with ExitStack() as ctx:
        consts = Layer1Constants(nc, ctx)
        moe_combine(nc, xn, moe, xa, x1, xn2, xn2T, t["gamma"], t["beta"], t["ident"], consts.zero, lambda sp: consts.load(sp, t))
        layer1(nc, xn2, xn2T, x1, t["out"], consts)


def shape_constants():
    k = np.arange(L)
    angle = 2 * np.pi * ((k[:, None] * k[None, :]) % L) / L
    c, s = np.cos(angle), np.sin(angle)
    dft = np.stack([chunks(np.concatenate(t, 1)) for t in ([c, -s], [c, s], [-s, c])], 1)
    i, j = np.arange(P)[:, None], np.arange(P)[None, :]
    levels = []
    for n in range(NLEV):
        b = 1 << n
        levels.append(((i // (2 * b) == j // (2 * b)) & (i // b % 2 == 1) & (j // b % 2 == 0)).astype(np.float32))
    levels = np.stack(levels, 1)
    tables = {
        "dft": dft,
        "sel": np.tile(np.eye(2 * DS), (3, 1)),
        "ident": np.eye(P),
        "iota8": np.arange(NE),
        "lower": np.triu(np.ones((P, P)), 1),
        "levels": np.stack([levels, levels.transpose(2, 1, 0)], 1),
        "masks": np.stack([i <= j, i // AD == j // AD], 1),
    }
    return {n: np.ascontiguousarray(a, dtype=np.float32) for n, a in tables.items()}


def chunks(a):
    return a.reshape(a.shape[0] // P, P, -1).transpose(1, 0, 2)


def layouts(w):
    both = (("", "A_log", "D"), ("b", "A_b_log", "D_b"))
    per_channel = []
    for r, alog, d in both:
        per_channel += [chunks(w[f"L0_attn_conv1d{r}_w"]).reshape(P, -1), chunks(w[f"L0_attn_conv1d{r}_bias"][:, None]).reshape(P, -1),
                        chunks(w[f"L0_attn_dt_proj{r}_b"][:, None]).reshape(P, -1), chunks(w[f"L0_attn_{alog}"]).reshape(P, -1),
                        chunks(w[f"L0_attn_{d}"][:, None]).reshape(P, -1)]
    per_channel.append(w["L0_attn_fft_conv_b"].reshape(4, P).T)
    xproj = []
    for r, _, _ in both:
        a = w[f"L0_attn_x_proj{r}_w"].T
        xproj.append(chunks(np.concatenate([a[:, :DR], a[:, DR:], a[:, DR:], a[:, DR:]], 1)))
    t = {
        "x": w["L0_attn_hidden_states"].reshape(NTOK, DM),
        "winT": w["L0_attn_in_proj_w"].T,
        "convw": w["L0_attn_fft_conv_w"].transpose(1, 2, 0).reshape(4, P, 5, 2 * DI).transpose(1, 0, 2, 3),
        "xpT": np.stack(xproj, 1),
        "dtT": np.stack([w["L0_attn_dt_proj_w"].T, w["L0_attn_dt_projb_w"].T], 1),
        "woutT": chunks(w["L0_attn_out_proj_w"].T),
        "small": np.concatenate(per_channel, 1),
        "wr": w["L0_ffn_Wr"], "br": w["L0_ffn_br"],
        "w1": w["L0_ffn_W1"], "b1": w["L0_ffn_b1"].reshape(NE, FF // P, P).transpose(0, 2, 1),
        "w2": w["L0_ffn_W2"], "b2": w["L0_ffn_b2"], "gamma": w["L0_ffn_gamma"], "beta": w["L0_ffn_beta"],
        "wqkv": np.stack([w["L1_attn_Wq"], w["L1_attn_Wk"], w["L1_attn_Wv"]], 1),
        "wb": w["L1_attn_Wb"], "wo": w["L1_attn_Wo"],
        "cw": np.stack([w["L1_attn_conv_q"].T, w["L1_attn_conv_k"].T, w["L1_attn_conv_v"].T], 1),
        "grms": w["L1_attn_g_rms"], "lng": w["L1_attn_ln_g"], "lnb": w["L1_attn_ln_b"],
        "wgu": np.stack([w["L1_ffn_w_gate"], w["L1_ffn_w_up"]]), "wd": w["L1_ffn_w_down"],
    }
    return {n: np.ascontiguousarray(a) for n, a in t.items()}


def kernel(**inputs):
    import concourse.bacc as bacc
    from concourse.bass_utils import run_bass_kernel_spmd

    nc = bacc.Bacc("TRN2", target_bir_lowering=False, num_devices=1)
    arrays = {**layouts({n: np.asarray(a) for n, a in inputs.items()}), **shape_constants()}
    arrays = {f"in_{n}": a for n, a in arrays.items()}
    t = {n[3:]: nc.dram_tensor(n, a.shape, mybir.dt.from_np(a.dtype), kind="ExternalInput").ap() for n, a in arrays.items()}
    t["out"] = nc.dram_tensor("out_0", (NTOK, DM), F32, kind="ExternalOutput").ap()
    build_program(nc, t)
    return run_bass_kernel_spmd(nc, [arrays], core_ids=[0]).results[0]["out_0"].reshape(B, L, DM)
```
